# Optimizing a Trainium2 kernel written in Bass

```python
import numpy as np
import jax
import jax.numpy as jnp

def _softmax(x, axis=-1):
    return jax.nn.softmax(x, axis=axis)

def _gelu(x):
    return jax.nn.gelu(x, approximate=True)

def _silu(x):
    return jax.nn.silu(x)

def _sigmoid(x):
    return jax.nn.sigmoid(x)

def _layernorm(x, axis=-1, eps=1e-05):
    m = jnp.mean(x, axis=axis, keepdims=True)
    v = jnp.var(x, axis=axis, keepdims=True)
    return (x - m) / jnp.sqrt(v + eps)

def _scatter_add(tgt, idx, src, axis=0):
    return tgt.at[idx].add(src)

def _segment_sum(src, seg, n):
    return jax.ops.segment_sum(src, seg, n)
kernel_name = 'mk_vit_tower_postln_d2_tok_img256_r4_8ef08d'

def setup_inputs(seed: int=0):
    np.random.seed(seed)
    _w = jnp.asarray

    def _rec_inputs():
        import jax
        import jax.numpy as jnp
        _rk = jax.random.key(seed)
        x = -7.10856e-05 + 0.999911 * jax.random.normal(jax.random.fold_in(_rk, 1), (64, 1, 84, 84), jnp.float32)
        return x
    x = _rec_inputs()

    def _L0_tok_setup():
        import jax, jax.numpy as jnp
        import numpy as np
        INV_SQRT2 = 0.7071067811865476

        def haar_dwt2(x):
            lo = (x[..., ::2] + x[..., 1::2]) * INV_SQRT2
            hi = (x[..., ::2] - x[..., 1::2]) * INV_SQRT2
            cA = (lo[..., ::2, :] + lo[..., 1::2, :]) * INV_SQRT2
            cH = (lo[..., ::2, :] - lo[..., 1::2, :]) * INV_SQRT2
            cV = (hi[..., ::2, :] + hi[..., 1::2, :]) * INV_SQRT2
            cD = (hi[..., ::2, :] - hi[..., 1::2, :]) * INV_SQRT2
            return (cA, (cH, cV, cD))

        def wavedec2_maps(x, levels):
            a = x
            details = []
            for _ in range(levels):
                a, d = haar_dwt2(a)
                details.append(d)
            maps = [a]
            for d in reversed(details):
                maps.extend(d)
            return maps
        key = jax.random.key(seed)
        k1, k2 = jax.random.split(key)
        B, H, W_img = (64, 256, 256)
        x = jax.random.normal(k1, (B, 1, H, W_img), dtype=jnp.float32)
        n_maps = 1 + 3 * 2
        W = jax.random.normal(k2, (n_maps, 64), dtype=jnp.float32) * (1.0 / np.sqrt(n_maps))
        b = jnp.zeros((64,), dtype=jnp.float32)
        return {'x': x, 'W': W, 'b': b}
    _L0_tok_all = _L0_tok_setup()
    _L0_tok_in = {k: v for k, v in _L0_tok_all.items() if k in ('W', 'b')}
    del _L0_tok_all

    def _L0_attn_setup():
        import jax, jax.numpy as jnp
        import numpy as np
        key = jax.random.key(seed)
        kx, kq, kk, kv = jax.random.split(key, 4)
        b, n, d, a = (4, 1024, 64, 64)
        return {'x': jax.random.normal(kx, (b, n, d), dtype=jnp.float32), 'Q': jax.random.normal(kq, (a, d), dtype=jnp.float32), 'K': jax.random.normal(kk, (a, d), dtype=jnp.float32), 'V': jax.random.normal(kv, (d, d), dtype=jnp.float32)}
    _L0_attn_all = _L0_attn_setup()
    _L0_attn_in = {k: v for k, v in _L0_attn_all.items() if k in ('Q', 'K', 'V')}
    del _L0_attn_all

    def _L0_ffn_setup():
        import jax, jax.numpy as jnp
        import numpy as np
        BN_EPS = 0.001

        def _bn(h, g, b, m, v):
            return g * (h - m) * jax.lax.rsqrt(v + BN_EPS) + b
        key = jax.random.key(seed)
        ks = jax.random.split(key, 8)
        B, F, Df = (64, 64, 64)
        E, H, D = (8, 64, 64)
        s1 = 1.0 / np.sqrt(Df)
        s2 = 1.0 / np.sqrt(H)
        return {'x': jax.random.normal(ks[0], (B, F, Df), jnp.float32), 'Wr': jax.random.normal(ks[1], (Df, E), jnp.float32) * s1, 'br': jnp.zeros((E,), jnp.float32), 'W1': jax.random.normal(ks[2], (E, Df, H), jnp.float32) * s1, 'b1': jnp.zeros((E, H), jnp.float32), 'g1': jnp.ones((E, H), jnp.float32), 'be1': jnp.zeros((E, H), jnp.float32), 'm1': jnp.zeros((E, H), jnp.float32), 'v1': jnp.ones((E, H), jnp.float32), 'W2': jax.random.normal(ks[3], (E, H, H), jnp.float32) * s2, 'b2': jnp.zeros((E, H), jnp.float32), 'g2': jnp.ones((E, H), jnp.float32), 'be2': jnp.zeros((E, H), jnp.float32), 'm2': jnp.zeros((E, H), jnp.float32), 'v2': jnp.ones((E, H), jnp.float32), 'Wo': jax.random.normal(ks[4], (E, H, D), jnp.float32) * s2, 'bo': jnp.zeros((E, D), jnp.float32)}
    _L0_ffn_all = _L0_ffn_setup()
    _L0_ffn_in = {k: v for k, v in _L0_ffn_all.items() if k in ('Wr', 'br', 'W1', 'b1', 'g1', 'be1', 'm1', 'v1', 'W2', 'b2', 'g2', 'be2', 'm2', 'v2', 'Wo', 'bo')}
    del _L0_ffn_all

    def _L1_attn_setup():
        import jax, jax.numpy as jnp
        import numpy as np
        U_DECAY = 0.97
        X_DECAY = 0.97
        LN_EPS = 1e-05
        L1_EPS = 1e-12

        def _ln(x):
            m = jnp.mean(x, axis=-1, keepdims=True)
            v = jnp.mean((x - m) ** 2, axis=-1, keepdims=True)
            return (x - m) * jax.lax.rsqrt(v + LN_EPS)
        key = jax.random.key(seed)
        k0, k1, k2, k3 = jax.random.split(key, 4)
        B, T, d, n = (8, 64, 64, 256)
        embeddings = jax.random.normal(k0, (B, T, d), dtype=jnp.float32)
        E = jax.random.normal(k1, (d, n), dtype=jnp.float32) / n ** 0.5
        Dx = jax.random.normal(k2, (n, d), dtype=jnp.float32) / d ** 0.5
        Dy = jax.random.normal(k3, (n, d), dtype=jnp.float32) / d ** 0.5
        return {'embeddings': embeddings, 'E': E, 'Dx': Dx, 'Dy': Dy}
    _L1_attn_all = _L1_attn_setup()
    _L1_attn_in = {k: v for k, v in _L1_attn_all.items() if k in ('E', 'Dx', 'Dy')}
    del _L1_attn_all

    def _L1_ffn_setup():
        import jax, jax.numpy as jnp
        import numpy as np
        B, N, D = (16, 1024, 64)
        NUM_EXPERTS, TOP_K, HEADS = (4, 2, 4)
        N_EDGES = 262144
        LN_EPS = 1e-05

        def _layernorm(x, g, b):
            mu = x.mean(-1, keepdims=True)
            var = ((x - mu) ** 2).mean(-1, keepdims=True)
            return (x - mu) * jax.lax.rsqrt(var + LN_EPS) * g + b

        def _forward(x, edge_index, W_gat, att_src, att_dst, b_gat, ln_gamma, ln_beta, W1, b1, W2, b2):
            Bc, Nc, Dc = x.shape
            M = Bc * Nc
            x_flat = x.reshape(M, Dc)
            h = (x_flat @ W_gat).reshape(M, HEADS, NUM_EXPERTS)
            loops = jnp.arange(M, dtype=edge_index.dtype)
            src = jnp.concatenate([edge_index[0], loops])
            dst = jnp.concatenate([edge_index[1], loops])
            a_src = (h * att_src).sum(-1)
            a_dst = (h * att_dst).sum(-1)
            e = jax.nn.leaky_relu(a_src[src] + a_dst[dst], negative_slope=0.2)
            e_max = jax.ops.segment_max(e, dst, num_segments=M)
            ee = jnp.exp(e - e_max[dst])
            denom = jax.ops.segment_sum(ee, dst, num_segments=M)
            alpha = ee / (denom[dst] + 1e-16)
            msg = h[src] * alpha[:, :, None]
            agg = jax.ops.segment_sum(msg, dst, num_segments=M).reshape(M, HEADS * NUM_EXPERTS) + b_gat
            scores = _layernorm(agg, ln_gamma, ln_beta).reshape(M, HEADS, NUM_EXPERTS).mean(1)
            scores = scores.reshape(Bc, Nc, NUM_EXPERTS)
            topk_s, topk_i = jax.lax.top_k(scores, TOP_K)
            w = jax.nn.softmax(topk_s, axis=-1)
            out = jnp.zeros_like(x)
            for ei in range(NUM_EXPERTS):
                g = jnp.where(topk_i == ei, w, 0.0).sum(-1)
                hh = jax.nn.gelu(x @ W1[ei] + b1[ei], approximate=False)
                out = out + g[..., None] * (hh @ W2[ei] + b2[ei])
            return out
        key = jax.random.key(seed)
        ks = jax.random.split(key, 8)
        s = 0.05
        return {'x': jax.random.normal(ks[0], (B, N, D), jnp.float32), 'W_gat': jax.random.normal(ks[1], (D, HEADS * NUM_EXPERTS), jnp.float32) * s, 'att_src': jax.random.normal(ks[2], (HEADS, NUM_EXPERTS), jnp.float32) * s, 'att_dst': jax.random.normal(ks[3], (HEADS, NUM_EXPERTS), jnp.float32) * s, 'b_gat': jnp.zeros((HEADS * NUM_EXPERTS,), jnp.float32), 'ln_gamma': jnp.ones((HEADS * NUM_EXPERTS,), jnp.float32), 'ln_beta': jnp.zeros((HEADS * NUM_EXPERTS,), jnp.float32), 'W1': jax.random.normal(ks[4], (NUM_EXPERTS, D, 2 * D), jnp.float32) * s, 'b1': jnp.zeros((NUM_EXPERTS, 2 * D), jnp.float32), 'W2': jax.random.normal(ks[5], (NUM_EXPERTS, 2 * D, D), jnp.float32) * s, 'b2': jnp.zeros((NUM_EXPERTS, D), jnp.float32), 'edge_index': jax.random.randint(ks[6], (2, N_EDGES), 0, B * N, jnp.int32)}
    _L1_ffn_all = _L1_ffn_setup()
    _L1_ffn_in = {k: v for k, v in _L1_ffn_all.items() if k in ('W_gat', 'att_src', 'att_dst', 'b_gat', 'ln_gamma', 'ln_beta', 'W1', 'b1', 'W2', 'b2', 'edge_index')}
    del _L1_ffn_all
    return {'x': x, 'L0_tok_W': _L0_tok_in['W'], 'L0_tok_b': _L0_tok_in['b'], 'L0_attn_Q': _L0_attn_in['Q'], 'L0_attn_K': _L0_attn_in['K'], 'L0_attn_V': _L0_attn_in['V'], 'L0_ffn_Wr': _L0_ffn_in['Wr'], 'L0_ffn_br': _L0_ffn_in['br'], 'L0_ffn_W1': _L0_ffn_in['W1'], 'L0_ffn_b1': _L0_ffn_in['b1'], 'L0_ffn_g1': _L0_ffn_in['g1'], 'L0_ffn_be1': _L0_ffn_in['be1'], 'L0_ffn_m1': _L0_ffn_in['m1'], 'L0_ffn_v1': _L0_ffn_in['v1'], 'L0_ffn_W2': _L0_ffn_in['W2'], 'L0_ffn_b2': _L0_ffn_in['b2'], 'L0_ffn_g2': _L0_ffn_in['g2'], 'L0_ffn_be2': _L0_ffn_in['be2'], 'L0_ffn_m2': _L0_ffn_in['m2'], 'L0_ffn_v2': _L0_ffn_in['v2'], 'L0_ffn_Wo': _L0_ffn_in['Wo'], 'L0_ffn_bo': _L0_ffn_in['bo'], 'L1_attn_E': _L1_attn_in['E'], 'L1_attn_Dx': _L1_attn_in['Dx'], 'L1_attn_Dy': _L1_attn_in['Dy'], 'L1_ffn_W_gat': _L1_ffn_in['W_gat'], 'L1_ffn_att_src': _L1_ffn_in['att_src'], 'L1_ffn_att_dst': _L1_ffn_in['att_dst'], 'L1_ffn_b_gat': _L1_ffn_in['b_gat'], 'L1_ffn_ln_gamma': _L1_ffn_in['ln_gamma'], 'L1_ffn_ln_beta': _L1_ffn_in['ln_beta'], 'L1_ffn_W1': _L1_ffn_in['W1'], 'L1_ffn_b1': _L1_ffn_in['b1'], 'L1_ffn_W2': _L1_ffn_in['W2'], 'L1_ffn_b2': _L1_ffn_in['b2'], 'L1_ffn_edge_index': _L1_ffn_in['edge_index']}

def reference(x, L0_tok_W, L0_tok_b, L0_attn_Q, L0_attn_K, L0_attn_V, L0_ffn_Wr, L0_ffn_br, L0_ffn_W1, L0_ffn_b1, L0_ffn_g1, L0_ffn_be1, L0_ffn_m1, L0_ffn_v1, L0_ffn_W2, L0_ffn_b2, L0_ffn_g2, L0_ffn_be2, L0_ffn_m2, L0_ffn_v2, L0_ffn_Wo, L0_ffn_bo, L1_attn_E, L1_attn_Dx, L1_attn_Dy, L1_ffn_W_gat, L1_ffn_att_src, L1_ffn_att_dst, L1_ffn_b_gat, L1_ffn_ln_gamma, L1_ffn_ln_beta, L1_ffn_W1, L1_ffn_b1, L1_ffn_W2, L1_ffn_b2, L1_ffn_edge_index):
    import jax
    import jax.numpy as jnp

    def _L0_tok_ref(x, W, b):
        import jax, jax.numpy as jnp
        import numpy as np
        INV_SQRT2 = 0.7071067811865476

        def haar_dwt2(x):
            lo = (x[..., ::2] + x[..., 1::2]) * INV_SQRT2
            hi = (x[..., ::2] - x[..., 1::2]) * INV_SQRT2
            cA = (lo[..., ::2, :] + lo[..., 1::2, :]) * INV_SQRT2
            cH = (lo[..., ::2, :] - lo[..., 1::2, :]) * INV_SQRT2
            cV = (hi[..., ::2, :] + hi[..., 1::2, :]) * INV_SQRT2
            cD = (hi[..., ::2, :] - hi[..., 1::2, :]) * INV_SQRT2
            return (cA, (cH, cV, cD))

        def wavedec2_maps(x, levels):
            a = x
            details = []
            for _ in range(levels):
                a, d = haar_dwt2(a)
                details.append(d)
            maps = [a]
            for d in reversed(details):
                maps.extend(d)
            return maps
        imgs = x[:, 0]
        B = imgs.shape[0]
        maps = wavedec2_maps(imgs, 2)
        proc = [jax.image.resize(m, (B, 8, 8), method='bilinear') for m in maps]
        feat = jnp.stack(proc, axis=1)
        feat = feat.reshape(B, feat.shape[1], 64).transpose(0, 2, 1)
        return feat @ W + b

    def _L0_attn_ref(x, Q, K, V):
        import jax, jax.numpy as jnp
        import numpy as np
        Qx = jnp.einsum('bnd,ad->bna', x, Q)
        Kx = jnp.einsum('bnd,ad->bna', x, K)
        Vx = jnp.einsum('bnd,ed->bne', x, V)
        A = jnp.einsum('bia,bja->bij', Kx, Qx)
        A = jax.nn.softmax(A, axis=1)
        res = jnp.einsum('bij,bie->bje', A, Vx)
        return res

    def _L0_ffn_ref(x, Wr, br, W1, b1, g1, be1, m1, v1, W2, b2, g2, be2, m2, v2, Wo, bo):
        import jax, jax.numpy as jnp
        import numpy as np
        BN_EPS = 0.001

        def _bn(h, g, b, m, v):
            return g * (h - m) * jax.lax.rsqrt(v + BN_EPS) + b
        feat = jnp.mean(x, axis=0)
        w = jax.nn.softmax(feat @ Wr + br, axis=-1)
        h = jnp.einsum('bfd,edh->bfeh', x, W1) + b1
        h = jax.nn.relu(_bn(h, g1, be1, m1, v1))
        h = jnp.einsum('bfeh,ehk->bfek', h, W2) + b2
        h = jax.nn.relu(_bn(h, g2, be2, m2, v2))
        y = jnp.einsum('bfeh,ehd->bfed', h, Wo) + bo
        return jnp.einsum('bfed,fe->bfd', y, w)

    def _L1_attn_ref(embeddings, E, Dx, Dy):
        import jax, jax.numpy as jnp
        import numpy as np
        U_DECAY = 0.97
        X_DECAY = 0.97
        LN_EPS = 1e-05
        L1_EPS = 1e-12

        def _ln(x):
            m = jnp.mean(x, axis=-1, keepdims=True)
            v = jnp.mean((x - m) ** 2, axis=-1, keepdims=True)
            return (x - m) * jax.lax.rsqrt(v + LN_EPS)
        B, T, d = embeddings.shape
        n = E.shape[1]

        def step(carry, v_prev):
            x_state, rho = carry
            x_update = jax.nn.relu(v_prev @ Dx.T)
            x_t = X_DECAY * x_state + x_update
            x_t = x_t / jnp.maximum(jnp.sum(jnp.abs(x_t), axis=-1, keepdims=True), L1_EPS)
            a_star = jnp.einsum('bdn,bn->bd', rho, x_t)
            y_core = _ln(a_star) @ Dy.T
            y_t = jax.nn.relu(y_core) * jax.nn.relu(x_t)
            v_star = _ln(y_t @ E.T)
            rho_t = U_DECAY * rho + _ln(v_prev)[:, :, None] * x_t[:, None, :]
            return ((x_t, rho_t), v_star)
        x0 = jnp.zeros((B, n), dtype=embeddings.dtype)
        rho0 = jnp.zeros((B, d, n), dtype=embeddings.dtype)
        _, vs = jax.lax.scan(step, (x0, rho0), jnp.swapaxes(embeddings, 0, 1))
        return jnp.swapaxes(vs, 0, 1)

    def _L1_ffn_ref(x, W_gat, att_src, att_dst, b_gat, ln_gamma, ln_beta, W1, b1, W2, b2, edge_index):
        import jax, jax.numpy as jnp
        import numpy as np
        B, N, D = (16, 1024, 64)
        NUM_EXPERTS, TOP_K, HEADS = (4, 2, 4)
        N_EDGES = 262144
        LN_EPS = 1e-05

        def _layernorm(x, g, b):
            mu = x.mean(-1, keepdims=True)
            var = ((x - mu) ** 2).mean(-1, keepdims=True)
            return (x - mu) * jax.lax.rsqrt(var + LN_EPS) * g + b

        def _forward(x, edge_index, W_gat, att_src, att_dst, b_gat, ln_gamma, ln_beta, W1, b1, W2, b2):
            Bc, Nc, Dc = x.shape
            M = Bc * Nc
            x_flat = x.reshape(M, Dc)
            h = (x_flat @ W_gat).reshape(M, HEADS, NUM_EXPERTS)
            loops = jnp.arange(M, dtype=edge_index.dtype)
            src = jnp.concatenate([edge_index[0], loops])
            dst = jnp.concatenate([edge_index[1], loops])
            a_src = (h * att_src).sum(-1)
            a_dst = (h * att_dst).sum(-1)
            e = jax.nn.leaky_relu(a_src[src] + a_dst[dst], negative_slope=0.2)
            e_max = jax.ops.segment_max(e, dst, num_segments=M)
            ee = jnp.exp(e - e_max[dst])
            denom = jax.ops.segment_sum(ee, dst, num_segments=M)
            alpha = ee / (denom[dst] + 1e-16)
            msg = h[src] * alpha[:, :, None]
            agg = jax.ops.segment_sum(msg, dst, num_segments=M).reshape(M, HEADS * NUM_EXPERTS) + b_gat
            scores = _layernorm(agg, ln_gamma, ln_beta).reshape(M, HEADS, NUM_EXPERTS).mean(1)
            scores = scores.reshape(Bc, Nc, NUM_EXPERTS)
            topk_s, topk_i = jax.lax.top_k(scores, TOP_K)
            w = jax.nn.softmax(topk_s, axis=-1)
            out = jnp.zeros_like(x)
            for ei in range(NUM_EXPERTS):
                g = jnp.where(topk_i == ei, w, 0.0).sum(-1)
                hh = jax.nn.gelu(x @ W1[ei] + b1[ei], approximate=False)
                out = out + g[..., None] * (hh @ W2[ei] + b2[ei])
            return out
        return _forward(x, edge_index, W_gat, att_src, att_dst, b_gat, ln_gamma, ln_beta, W1, b1, W2, b2)
    h = _L0_tok_ref(x, L0_tok_W, L0_tok_b)
    h = _layernorm(h + _L0_attn_ref(h, L0_attn_Q, L0_attn_K, L0_attn_V), axis=-1)
    h = _layernorm(h + _L0_ffn_ref(h, L0_ffn_Wr, L0_ffn_br, L0_ffn_W1, L0_ffn_b1, L0_ffn_g1, L0_ffn_be1, L0_ffn_m1, L0_ffn_v1, L0_ffn_W2, L0_ffn_b2, L0_ffn_g2, L0_ffn_be2, L0_ffn_m2, L0_ffn_v2, L0_ffn_Wo, L0_ffn_bo), axis=-1)
    h = _layernorm(h + _L1_attn_ref(h, L1_attn_E, L1_attn_Dx, L1_attn_Dy), axis=-1)
    h = _layernorm(h + _L1_ffn_ref(h, L1_ffn_W_gat, L1_ffn_att_src, L1_ffn_att_dst, L1_ffn_b_gat, L1_ffn_ln_gamma, L1_ffn_ln_beta, L1_ffn_W1, L1_ffn_b1, L1_ffn_W2, L1_ffn_b2, L1_ffn_edge_index), axis=-1)
    return h

_drawn_inputs = setup_inputs


def setup_inputs(seed=0):
    import zlib

    import numpy as np

    out = dict(_drawn_inputs(seed))
    spreads = {'L0_tok_b': (0.0, 0.1),
     'L0_ffn_br': (0.0, 0.1),
     'L0_ffn_b1': (0.0, 0.339),
     'L0_ffn_g1': (1.0, 0.2),
     'L0_ffn_be1': (0.0, 0.321),
     'L0_ffn_m1': (0.0, 0.315),
     'L0_ffn_v1': (1.0, 0.542),
     'L0_ffn_b2': (0.0, 0.1),
     'L0_ffn_g2': (1.0, 0.2),
     'L0_ffn_be2': (0.0, 0.1),
     'L0_ffn_m2': (0.0, 0.1),
     'L0_ffn_v2': (1.0, 0.6),
     'L0_ffn_bo': (0.0, 0.1),
     'L1_ffn_b_gat': (0.0, 0.794),
     'L1_ffn_ln_gamma': (1.0, 0.6),
     'L1_ffn_ln_beta': (0.0, 0.8),
     'L1_ffn_b1': (0.0, 0.371),
     'L1_ffn_b2': (0.0, 0.1)}
    factors = {'L1_ffn_W_gat': 2.686, 'L1_ffn_att_src': 25.434, 'L1_ffn_att_dst': 63.177}
    for name, (base, spread) in spreads.items():
        noise = np.random.default_rng([zlib.crc32(name.encode()), seed]).standard_normal(out[name].shape)
        drawn = base * np.exp(spread * noise) if base else spread * noise
        out[name] = jnp.asarray(drawn.astype(out[name].dtype))
    for name, factor in factors.items():
        out[name] = (out[name] * factor).astype(out[name].dtype)
    return out
```

```python
from contextlib import ExitStack

import numpy as np

import concourse.bass as bass
from concourse import mybir

ALU = mybir.AluOpType
ACT = mybir.ActivationFunctionType
F32 = mybir.dt.float32
BF16 = mybir.dt.bfloat16
I32 = mybir.dt.int32
AX_X = mybir.AxisListType.X

B, IMG = 64, 84
T, D = 64, 64
NTOK = B * T
P = 128
NC = NTOK // P
TILE = 512
NT = NTOK // TILE
CPT = TILE // P
EXP0, NPAIR = 8, 4
NSTATE, NH2 = 256, 2
EXP1, HID1 = 4, 128
HEADS = 4
LN_EPS, BN_EPS, L1_EPS, DECAY = 1e-5, 1e-3, 1e-12, 0.97
NMAP, NOP = 7, 4
NEDGE = 262144
EW = NEDGE // P
FAR = NTOK - 1
SPREAD = 512
BIN_BITS = 18
NSLOT = P << BIN_BITS
PART = 256
LIST = PART + NC
ROW = 24
BIG = 1e30
MAP_OPS = [(0, 0), (1, 0), (0, 1), (1, 1), (3, 2), (2, 3), (3, 3)]


def resize_matrix(n):
    inv = n / 8.0
    kernel = max(inv, 1.0)
    sample = (np.arange(8) + 0.5) * inv - 0.5
    w = np.maximum(0.0, 1.0 - np.abs(sample[:, None] - np.arange(n)[None, :]) / kernel)
    return w / w.sum(axis=1, keepdims=True)


def haar(n, sign):
    m = np.zeros((n // 2, n))
    for k in range(n // 2):
        m[k, 2 * k], m[k, 2 * k + 1] = 1.0, sign
    return m * 0.7071067811865476


def haar_operators():
    half = IMG // 2
    low = haar(IMG, 1.0)
    return np.stack([resize_matrix(half // 2) @ haar(half, 1.0) @ low,
                     resize_matrix(half // 2) @ haar(half, -1.0) @ low,
                     resize_matrix(half) @ low,
                     resize_matrix(half) @ haar(IMG, -1.0)])


def shape_constants():
    ops = haar_operators()
    rows = ops.transpose(2, 0, 1).reshape(IMG, NOP * 8)
    cols = np.zeros((NMAP, 8, NOP, IMG))
    for m, (v, w) in enumerate(MAP_OPS):
        for j in range(8):
            cols[m, j, v] = ops[w, j]
    same = np.arange(P)[:, None] // T == np.arange(P)[None, :] // T
    t = np.arange(P) % T
    gap = t[None, :] - 1 - t[:, None]
    decay = np.where(same & (gap >= 0), DECAY ** np.maximum(gap, 0), 0.0)
    pick = np.zeros((EXP0, NPAIR, P))
    for e in range(EXP0):
        pick[e, e // 2, (e % 2) * 64:(e % 2) * 64 + 64] = 1.0
    return {
        "c_rows": rows.astype(np.float32),
        "c_cols": cols.reshape(NMAP, 8 * NOP, IMG).astype(np.float32),
        "c_other": np.where(same, 0.0, -1e30).astype(np.float32),
        "c_decay": decay.astype(np.float32),
        "c_pick": pick.astype(np.float32),
        "c_ident": np.eye(P, dtype=np.float32),
        "c_later": np.triu(np.ones((P, P), np.float32), 1),
        "c_hi_parity": (np.arange(64)[:, None] % 2 == np.arange(2)[None, :]).astype(np.float32),
        "c_hi_half": (np.arange(64)[:, None] // 2 == np.arange(NC)[None, :]).astype(np.float32),
        "c_before": np.tile((np.arange(4)[None, :] < np.arange(4)[:, None]).astype(np.float32).reshape(1, 16), (P, 1)),
    }


class Steps:

    def __init__(self, eng, sem, base=0):
        self.eng, self.sem, self.base, self.n = eng, sem, base, 0

    def then(self, ins):
        self.mark(ins)
        self.wait()

    def wait(self):
        self.eng.wait_ge(self.sem, self.base + self.n)

    def close(self, per):
        assert self.n < per
        self.wait()
        self.eng.sem_inc(self.sem, per - self.n)

    def mark(self, ins):
        ins.then_inc(self.sem, 1)
        self.n += 1
        return self.n


class Shared:

    def __init__(self):
        self.semaphores = []


def stage(nc, G):
    st = ExitStack()
    st.sb = lambda name, shape, dt=F32: st.enter_context(nc.sbuf_tensor(name, shape, dt))
    st.sem = lambda name: new_semaphore(nc, G, name)
    return st


def new_semaphore(nc, G, name):
    G.semaphores.append(nc.alloc_semaphore(name=name))
    return G.semaphores[-1]


def fresh_semaphores(nc, G):
    nc.all_engine_barrier()
    nc.clear_and_free_semaphores(G.semaphores)
    nc.all_engine_barrier()
    G.semaphores = []


LG = 4
LC = NC // LG


class LayerNorm:

    def __init__(self, st, name, x, out, sq, xc=None):
        self.src, self.out, self.sq = x, out, sq
        self.x = x if xc is None else xc
        self.sum = st.sb(name + "_sum", [P, NC])
        self.var = st.sb(name + "_var", [P, NC])
        self.centred = st.sem(name + "_centred")
        self.squared = st.sem(name + "_squared")
        self.var_ready = st.sem(name + "_var_ready")
        self.std_ready = st.sem(name + "_std_ready")
        self.normed = st.sem(name + "_normed")
        self.own = st.sem(name + "_dve_steps")

    def vector(self, dve):
        own = Steps(dve, self.own)
        for g in range(LG):
            c = slice(g * LC, (g + 1) * LC)
            own.then(dve.tensor_reduce(self.sum[:, c], self.src[:, c, :], AX_X, ALU.add))
            dve.scalar_tensor_tensor(out=self.x[:, c, :], in0=self.sum[:, c].unsqueeze(2).to_broadcast([P, LC, D]),
                                     scalar=-1.0 / D, in1=self.src[:, c, :], op0=ALU.mult,
                                     op1=ALU.add).then_inc(self.centred, 1)
        for g in range(LG):
            c = slice(g * LC, (g + 1) * LC)
            dve.wait_ge(self.squared, g + 1)
            dve.tensor_reduce(self.var[:, c], self.sq[:, c, :], AX_X, ALU.add).then_inc(self.var_ready, 1)
        dve.wait_ge(self.std_ready, 1)
        own.then(dve.reciprocal(self.sum[:, :], self.var[:, :]))
        for g in range(LG):
            c = slice(g * LC, (g + 1) * LC)
            dve.tensor_tensor(self.out[:, c, :], self.x[:, c, :],
                              self.sum[:, c].unsqueeze(2).to_broadcast([P, LC, D]),
                              ALU.mult).then_inc(self.normed, 1)

    def scalar(self, act, eps):
        for g in range(LG):
            c = slice(g * LC, (g + 1) * LC)
            act.wait_ge(self.centred, g + 1)
            act.activation(self.sq[:, c, :], self.x[:, c, :], ACT.Square).then_inc(self.squared, 1)
        act.wait_ge(self.var_ready, LG)
        act.activation(self.var[:, :], self.var[:, :], ACT.Sqrt, bias=eps, scale=1.0 / D).then_inc(self.std_ready, 1)


class ToFeatures:

    def __init__(self, st, name, src, dst, ready, ready_per_group):
        self.src, self.dst, self.ready, self.per = src, dst, ready, ready_per_group
        self.turned = st.sem(name + "_turned")
        self.kept_act = st.sem(name + "_kept_by_act")
        self.kept_dve = st.sem(name + "_kept_by_dve")

    def tensor(self, pe, G):
        for k in range(NT):
            if self.per:
                pe.wait_ge(self.ready, k * CPT // LC + 1)
            for i in range(CPT):
                ins = pe.transpose(G.bank[k][0:D, i * P:(i + 1) * P], self.src[:, k * CPT + i, :], G.ident[:, :])
            ins.then_inc(self.turned, 1)

    def scalar(self, act, G):
        for k in range(0, NT, 2):
            act.wait_ge(self.turned, k + 1)
            act.copy(self.dst[:, k * TILE:(k + 1) * TILE], G.bank[k][0:D, :]).then_inc(self.kept_act, 1)

    def vector(self, dve, G):
        for k in range(1, NT, 2):
            dve.wait_ge(self.turned, k + 1)
            dve.tensor_copy(self.dst[:, k * TILE:(k + 1) * TILE], G.bank[k][0:D, :]).then_inc(self.kept_dve, 1)

    def wait(self, eng):
        eng.wait_ge(self.kept_act, NT // 2)
        eng.wait_ge(self.kept_dve, NT // 2)


def tokens(nc, G, A):
    with stage(nc, G) as st:
        X = st.sb("images", [IMG, B, IMG])
        Y = st.sb("rows_done", [IMG, NOP, B, 8])
        rows = st.sb("row_ops", [IMG, NOP * 8])
        cols = st.sb("col_ops", [NMAP, 8 * NOP, IMG])
        Wm = st.sb("embed_w", [NMAP, D])
        bias = st.sb("embed_b", [D, 1])
        Wj = st.sb("col_weights", [IMG, 8 * NOP, D])
        img_in = [st.sem(f"images_in{i}") for i in range(4)]
        par_in = st.sem("embed_params_in")
        rows_mm = st.sem("rows_mm")
        wj_mm = st.sem("col_weights_mm")
        y_kept = st.sem("rows_kept")
        wj_kept = st.sem("col_weights_kept")
        h_mm = st.sem("embed_mm")
        h_act = st.sem("embed_kept_act")
        h_dve = st.sem("embed_kept_dve")
        xv = A["x"].rearrange("b o h w -> h (b o) w")
        with nc.Block() as block:
            @block.sync
            def _(sp):
                sp.dma_start(rows[:, :], A["c_rows"]).then_inc(par_in, 16)
                for i in range(0, 4, 2):
                    sp.dma_start(X[:, 16 * i:16 * i + 16, :], xv[:, 16 * i:16 * i + 16, :]).then_inc(img_in[i], 16)

            @block.scalar
            def _(act):
                act.dma_start(cols[:, :, :], A["c_cols"]).then_inc(par_in, 16)
                act.dma_start(Wm[:, :], A["L0_tok_W"]).then_inc(par_in, 16)
                act.dma_start(bias[:, :], A["L0_tok_b"].rearrange("(d o) -> d o", o=1)).then_inc(par_in, 16)
                for i in range(1, 4, 2):
                    act.dma_start(X[:, 16 * i:16 * i + 16, :], xv[:, 16 * i:16 * i + 16, :]).then_inc(img_in[i], 16)
                for k in range(4):
                    act.wait_ge(wj_mm, k + 1)
                    act.copy(Wj[:, 8 * k:8 * k + 8, :], G.bank[4 + k][0:IMG, :]).then_inc(wj_kept, 1)
                for j in range(0, 8, 2):
                    act.wait_ge(h_mm, j + 1)
                    act.activation(G.hT[:, :].rearrange("d (r j) -> d r j", j=8)[:, :, j], G.bank[j][0:D, :],
                                   ACT.Identity, bias=bias[:, 0:1]).then_inc(h_act, 1)

            @block.tensor
            def _(pe):
                pe.wait_ge(par_in, 64)
                for k in range(4):
                    for q in range(8 * k, 8 * k + 8):
                        ins = pe.matmul(G.bank[4 + k][0:IMG, (q % 8) * D:(q % 8 + 1) * D], cols[:, q, :], Wm[:, :],
                                        start=True, stop=True)
                    ins.then_inc(wj_mm, 1)
                for k in range(4):
                    pe.wait_ge(img_in[k], 16)
                    for b in range(16):
                        ins = pe.matmul(G.bank[k][0:IMG, b * 32:(b + 1) * 32], X[:, 16 * k + b, :], rows[:, :],
                                        start=True, stop=True)
                    ins.then_inc(rows_mm, 1)
                pe.wait_ge(y_kept, 4)
                pe.wait_ge(wj_kept, 4)
                for j in range(8):
                    for v in range(NOP):
                        ins = pe.matmul(G.bank[j][0:D, :], Wj[:, j * NOP + v, :],
                                        Y[:, v, :, :].rearrange("w b i -> w (b i)"),
                                        start=(v == 0), stop=(v == NOP - 1))
                    ins.then_inc(h_mm, 1)

            @block.vector
            def _(dve):
                for k in range(4):
                    dve.wait_ge(rows_mm, k + 1)
                    dve.tensor_copy(Y[:, :, 16 * k:16 * k + 16, :].rearrange("w v b i -> w b v i"),
                                    G.bank[k][0:IMG, :].rearrange("w (b v i) -> w b v i", v=NOP, i=8)
                                    ).then_inc(y_kept, 1)
                for j in range(1, 8, 2):
                    dve.wait_ge(h_mm, j + 1)
                    dve.tensor_scalar(G.hT[:, :].rearrange("d (r j) -> d r j", j=8)[:, :, j], G.bank[j][0:D, :],
                                      bias[:, 0:1], None, ALU.add).then_inc(h_dve, 1)


def attention0(nc, G, A):
    with stage(nc, G) as st:
        Qw = st.sb("q_w", [D, D])
        Kw = st.sb("k_w", [D, D])
        IV = st.sb("ident_v", [D, 2 * D])
        GT = st.sb("g_t", [D, D])
        Z = st.sb("z", [D, NTOK])
        HV = st.sb("h_and_v", [P, NC, 2 * D])
        other = st.sb("other_image", [P, P])
        S = st.sb("scores", [P, NC, P])
        ET = st.sb("probs_t", [P, NC, P])
        nmax = st.sb("neg_max", [P, NC])
        rmax = st.sb("row_max", [P, NC])
        rsum = st.sb("row_sum", [P, NC])
        rinv = st.sb("row_inv", [P, NC])
        R = st.sb("attn_sum", [P, NC, D])
        par_in = st.sem("attn0_params_in")
        g_mm = st.sem("g_mm")
        g_kept = st.sem("g_kept")
        z_mm, z_act, z_dve = st.sem("z_mm"), st.sem("z_kept_act"), st.sem("z_kept_dve")
        hv_mm, hv_act, hv_dve = st.sem("hv_mm"), st.sem("hv_kept_act"), st.sem("hv_kept_dve")
        s_mm, s_max, s_neg, s_exp = st.sem("scores_mm"), st.sem("scores_max"), st.sem("scores_neg"), st.sem("probs")
        t_mm, t_act, t_dve = st.sem("probs_turned"), st.sem("probs_t_act"), st.sem("probs_t_dve")
        o_mm = st.sem("attn_out_mm")
        own = st.sem("attn0_dve_steps")
        rinv_s = st.sem("row_inv_ready")
        ln = LayerNorm(st, "ln0", R, G.tm, S[:, 0:NC // 2, :].rearrange("p c (u d) -> p (c u) d", u=2))
        tf = ToFeatures(st, "ln0_turn", G.tm, G.hT, ln.normed, True)
        with nc.Block() as block:
            @block.sync
            def _(sp):
                sp.dma_start(Qw[:, :], A["L0_attn_Q"]).then_inc(par_in, 16)
                sp.dma_start(Kw[:, :], A["L0_attn_K"]).then_inc(par_in, 16)
                sp.dma_start(IV[:, 0:D], A["c_ident"][0:D, 0:D]).then_inc(par_in, 16)
                sp.dma_start(IV[:, D:2 * D], A["L0_attn_VT"]).then_inc(par_in, 16)
                sp.dma_start(other[:, :], A["c_other"]).then_inc(par_in, 16)
                sp.dma_start(G.ident[:, :], A["c_ident"]).then_inc(par_in, 16)

            @block.tensor
            def _(pe):
                pe.wait_ge(par_in, 96)
                pe.matmul(G.bank[0][0:D, 0:D], Qw[:, :], Kw[:, :], start=True, stop=True).then_inc(g_mm, 1)
                pe.wait_ge(g_kept, 1)
                for k in range(NT):
                    pe.matmul(G.bank[k][0:D, :], GT[:, :], G.hT[:, k * TILE:(k + 1) * TILE],
                              start=True, stop=True).then_inc(z_mm, 1)
                for k in range(NT):
                    pe.wait_ge(z_dve if k % 2 else z_act, k // 2 + 1)
                    for i in range(CPT):
                        c = k * CPT + i
                        ins = pe.matmul(G.bank[k][:, i * P:(i + 1) * P], G.hT[:, c * P:(c + 1) * P], IV[:, :],
                                        start=True, stop=True)
                    ins.then_inc(hv_mm, 1)
                for k in range(NT):
                    pe.wait_ge(hv_dve if k % 2 else hv_act, k // 2 + 1)
                    for i in range(CPT):
                        c = slice((k * CPT + i) * P, (k * CPT + i + 1) * P)
                        ins = pe.matmul(G.bank[k][:, i * P:(i + 1) * P], Z[:, c], G.hT[:, c], start=True, stop=True)
                    ins.then_inc(s_mm, 1)
                for k in range(NT):
                    pe.wait_ge(s_exp, (k + 1) * CPT)
                    for i in range(CPT):
                        ins = pe.transpose(G.bank[k][:, i * P:(i + 1) * P], S[:, k * CPT + i, :], G.ident[:, :])
                    ins.then_inc(t_mm, 1)
                for k in range(4):
                    pe.wait_ge(t_act, k + 1)
                    pe.wait_ge(t_dve, k + 1)
                    for i in range(8):
                        c = 8 * k + i
                        ins = pe.matmul(G.bank[k][:, i * D:(i + 1) * D], ET[:, c, :], HV[:, c, D:2 * D],
                                        start=True, stop=True)
                    ins.then_inc(o_mm, 1)
                tf.tensor(pe, G)

            @block.scalar
            def _(act):
                for k in range(0, NT, 2):
                    act.wait_ge(z_mm, k + 1)
                    act.copy(Z[:, k * TILE:(k + 1) * TILE], G.bank[k][0:D, :]).then_inc(z_act, 1)
                for k in range(0, NT, 2):
                    act.wait_ge(hv_mm, k + 1)
                    act.copy(HV[:, k * CPT:(k + 1) * CPT, :], G.bank[k][:, :]).then_inc(hv_act, 1)
                for k in range(NT):
                    act.wait_ge(s_neg, k + 1)
                    for c in range(k * CPT, (k + 1) * CPT):
                        act.activation(S[:, c, :], S[:, c, :], ACT.Exp, bias=nmax[:, c:c + 1],
                                       accum_out=rsum[:, c:c + 1]).then_inc(s_exp, 1)
                for k in range(0, NT, 2):
                    act.wait_ge(t_mm, k + 1)
                    act.copy(ET[:, k * CPT:(k + 1) * CPT, :], G.bank[k][:, :]).then_inc(t_act, 1)
                ln.scalar(act, G.ln_eps[:, 0:1])
                tf.scalar(act, G)

            @block.vector
            def _(dve):
                o = Steps(dve, own)
                dve.memset(G.ln_eps[:, :], LN_EPS)
                dve.wait_ge(g_mm, 1)
                dve.tensor_copy(GT[:, :], G.bank[0][0:D, 0:D]).then_inc(g_kept, 1)
                for k in range(1, NT, 2):
                    dve.wait_ge(z_mm, k + 1)
                    dve.tensor_copy(Z[:, k * TILE:(k + 1) * TILE], G.bank[k][0:D, :]).then_inc(z_dve, 1)
                for k in range(1, NT, 2):
                    dve.wait_ge(hv_mm, k + 1)
                    dve.tensor_copy(HV[:, k * CPT:(k + 1) * CPT, :], G.bank[k][:, :]).then_inc(hv_dve, 1)
                dve.wait_ge(par_in, 96)
                for k in range(NT):
                    dve.wait_ge(s_mm, k + 1)
                    for i in range(CPT):
                        c = k * CPT + i
                        ins = dve.tensor_tensor_reduce(out=S[:, c, :], in0=G.bank[k][:, i * P:(i + 1) * P],
                                                       in1=other[:, :], scale=1.0, scalar=-3e38, op0=ALU.add,
                                                       op1=ALU.max, accum_out=rmax[:, c:c + 1])
                        ins.then_inc(s_max, 1)
                    dve.wait_ge(s_max, (k + 1) * CPT)
                    dve.tensor_scalar(nmax[:, k * CPT:(k + 1) * CPT], rmax[:, k * CPT:(k + 1) * CPT], -1.0, None,
                                      ALU.mult).then_inc(s_neg, 1)
                for k in range(1, NT, 2):
                    dve.wait_ge(t_mm, k + 1)
                    dve.tensor_copy(ET[:, k * CPT:(k + 1) * CPT, :], G.bank[k][:, :]).then_inc(t_dve, 1)
                dve.wait_ge(s_exp, NC)
                o.then(dve.reciprocal(rinv[:, :], rsum[:, :]))
                for k in range(4):
                    c = slice(8 * k, 8 * k + 8)
                    dve.wait_ge(o_mm, k + 1)
                    o.then(dve.tensor_tensor(R[:, c, :], G.bank[k][:, :].rearrange("p (c d) -> p c d", d=D),
                                             rinv[:, c].unsqueeze(2).to_broadcast([P, 8, D]), ALU.mult))
                    o.then(dve.tensor_tensor(R[:, c, :], R[:, c, :], HV[:, c, 0:D], ALU.add))
                ln.vector(dve)
                tf.vector(dve, G)


def experts0(nc, G, A):
    with stage(nc, G) as st:
        W1 = st.sb("e0_w1", [D, NPAIR, P])
        W2 = st.sb("e0_w2", [P, NPAIR, P])
        Wo = st.sb("e0_wo", [P, NPAIR, D])
        bo = st.sb("e0_bo", [EXP0, D])
        Wr = st.sb("e0_wr", [D, EXP0])
        br = st.sb("e0_br", [1, EXP0])
        ones = st.sb("e0_ones", [1, P])
        pick = st.sb("e0_pick", [EXP0, NPAIR, P])
        par = {n: st.sb("e0_" + n, [P, NPAIR]) for n in
               ("b1", "g1", "be1", "m1", "v1", "b2", "g2", "be2", "m2", "v2", "A1", "B1", "A2", "B2", "t1", "t2")}
        feat = st.sb("e0_feat", [D, 2, T])
        glog = st.sb("e0_gate_logits", [P, EXP0])
        gate = st.sb("e0_gate", [P, EXP0])
        gm = st.sb("e0_gate_max", [P, 1])
        gs = st.sb("e0_gate_sum", [P, 1])
        gi = st.sb("e0_gate_inv", [P, 1])
        gT = st.sb("e0_gate_t", [EXP0, P])
        wrep = st.sb("e0_gate_rows", [P, NPAIR, T])
        bn_eps = st.sb("e0_bn_eps", [P, 1])
        H1 = st.sb("e0_h1", [P, 2, TILE])
        H2 = st.sb("e0_h2", [P, 2, TILE])
        H2w = st.sb("e0_h2w", [P, 2, NPAIR, TILE])
        R = st.sb("e0_sum", [P, NC, D])
        sq = st.sb("e0_sq", [P, NC, D])
        w_in, zero_s, bn_in = st.sem("e0_weights_in"), st.sem("e0_zeroed"), st.sem("e0_bn_in")
        w2_in = st.sem("e0_w2_in")
        own, var_s, std_s, ab_s = st.sem("e0_dve_steps"), st.sem("e0_bn_var"), st.sem("e0_bn_std"), st.sem("e0_bn_fold")
        feat_s, log_mm, neg_s, exp_s = st.sem("e0_feat_s"), st.sem("e0_log_mm"), st.sem("e0_neg"), st.sem("e0_exp")
        gate_s, gT_mm, gT_s, rep_mm, rep_s = (st.sem("e0_gate_s"), st.sem("e0_gt_mm"), st.sem("e0_gt_s"),
                                              st.sem("e0_rep_mm"), st.sem("e0_rep_s"))
        l1_mm, l1_s, l2_mm, l2_s, gw_s, o_mm, o_s = (st.sem("e0_l1_mm"), st.sem("e0_l1_relu"), st.sem("e0_l2_mm"),
                                                     st.sem("e0_l2_relu"), st.sem("e0_gated"), st.sem("e0_out_mm"),
                                                     st.sem("e0_out_kept"))
        ln = LayerNorm(st, "ln1", R, G.tm, sq)
        tf = ToFeatures(st, "ln1_turn", G.tm, G.hT, ln.normed, True)
        pairs = "(q e) h -> (e h) q"
        NW = 6 + 2 * NPAIR
        with nc.Block() as block:
            @block.gpsimd
            def _(pool):
                pool.memset(W2[:, :, :], 0.0).then_inc(zero_s, 1)

            @block.sync
            def _(sp):
                sp.dma_start(W1[:, :, :].rearrange("d q (e h) -> d (q e) h", e=2),
                             A["L0_ffn_W1"].rearrange("e d h -> d e h")).then_inc(w_in, 16)
                sp.dma_start(Wo[:, :, :], A["L0_ffn_Wo"].rearrange("(q e) h d -> (e h) q d", e=2)).then_inc(w_in, 16)
                sp.dma_start(bo[:, :], A["L0_ffn_bo"]).then_inc(w_in, 16)
                sp.dma_start(Wr[:, :], A["L0_ffn_Wr"]).then_inc(w_in, 16)
                sp.dma_start(br[:, :], A["L0_ffn_br"].rearrange("(o e) -> o e", o=1)).then_inc(w_in, 16)
                sp.dma_start(pick[:, :, :], A["c_pick"]).then_inc(w_in, 16)
                sp.wait_ge(zero_s, 1)
                w2v = A["L0_ffn_W2"].rearrange("(q e) h k -> e h q k", e=2)
                for e in range(2):
                    sp.dma_start(W2[e * D:(e + 1) * D, :, e * D:(e + 1) * D], w2v[e]).then_inc(w2_in, 16)
                for n in ("b1", "g1", "be1", "m1", "v1", "b2", "g2", "be2", "m2", "v2"):
                    sp.dma_start(par[n][:, :], A["bn_" + n]).then_inc(bn_in, 16)

            @block.tensor
            def _(pe):
                pe.wait_ge(w_in, 96)
                pe.wait_ge(feat_s, 2)
                pe.matmul(G.bank[7][:, 0:EXP0], feat[:, :, :].rearrange("d r f -> d (r f)"), Wr[:, :], start=True,
                          stop=False)
                pe.matmul(G.bank[7][:, 0:EXP0], ones[:, :], br[:, :], start=False, stop=True).then_inc(log_mm, 1)
                pe.wait_ge(gate_s, 1)
                pe.transpose(G.bank[6][0:EXP0, 0:P], gate[:, :], G.ident[:, :]).then_inc(gT_mm, 1)
                pe.wait_ge(gT_s, 1)
                for q in range(NPAIR):
                    ins = pe.matmul(G.bank[7][:, 64 + q * T:64 + (q + 1) * T], pick[:, q, :], gT[:, 0:T], start=True,
                                    stop=True)
                ins.then_inc(rep_mm, 1)
                pe.wait_ge(w2_in, 32)

                def layer1(n):
                    k, q = n // NPAIR, n % NPAIR
                    if n >= 2:
                        pe.wait_ge(l1_s, n - 1)
                    pe.matmul(G.bank[n % 2][:, :], W1[:, q, :], G.hT[:, k * TILE:(k + 1) * TILE], start=True,
                              stop=True).then_inc(l1_mm, 1)

                def layer2(n):
                    pe.wait_ge(l1_s, n + 1)
                    if n >= 2:
                        pe.wait_ge(l2_s, n - 1)
                    pe.matmul(G.bank[2 + n % 2][:, :], W2[:, n % NPAIR, :], H1[:, n % 2, :], start=True,
                              stop=True).then_inc(l2_mm, 1)

                def out(k):
                    pe.wait_ge(gw_s, NPAIR * (k + 1))
                    if k >= 2:
                        pe.wait_ge(o_s, k - 1)
                    for i in range(CPT):
                        to = G.bank[4 + k % 2][:, i * D:(i + 1) * D]
                        for q in range(NPAIR):
                            pe.matmul(to, H2w[:, k % 2, q, i * P:(i + 1) * P], Wo[:, q, :], start=(q == 0), stop=False)
                        ins = pe.matmul(to, gT[:, :], bo[:, :], start=False, stop=True)
                    ins.then_inc(o_mm, 1)

                N = NT * NPAIR
                for n in range(N + 1):
                    if n < N:
                        layer1(n)
                    if n >= 1:
                        layer2(n - 1)
                    if n >= 3 and (n - 3) % NPAIR == 0 and n > 3:
                        out((n - 3) // NPAIR - 1)
                out(NT - 1)
                tf.tensor(pe, G)

            @block.scalar
            def _(act):
                for i in (1, 2):
                    act.wait_ge(bn_in, 160)
                    act.wait_ge(var_s, 1)
                    act.activation(par[f"t{i}"][:, :], par[f"v{i}"][:, :], ACT.Sqrt,
                                   bias=bn_eps[:, 0:1]).then_inc(std_s, 1)
                act.wait_ge(neg_s, 1)
                act.activation(gate[:, :], glog[:, :], ACT.Exp, bias=gm[:, 0:1], accum_out=gs[:, 0:1]
                               ).then_inc(exp_s, 1)
                act.wait_ge(ab_s, 2)
                N = NT * NPAIR
                for n in range(N + 1):
                    if n < N:
                        act.wait_ge(l1_mm, n + 1)
                        if n >= 2:
                            act.wait_ge(l2_mm, n - 1)
                        act.activation(H1[:, n % 2, :], G.bank[n % 2][:, :], ACT.Relu, bias=par["B1"][:, n % 4:n % 4 + 1],
                                       scale=par["A1"][:, n % 4:n % 4 + 1]).then_inc(l1_s, 1)
                    if n >= 1:
                        m = n - 1
                        act.wait_ge(l2_mm, m + 1)
                        if m >= 2:
                            act.wait_ge(gw_s, m - 1)
                        act.activation(H2[:, m % 2, :], G.bank[2 + m % 2][:, :], ACT.Relu,
                                       bias=par["B2"][:, m % 4:m % 4 + 1],
                                       scale=par["A2"][:, m % 4:m % 4 + 1]).then_inc(l2_s, 1)
                ln.scalar(act, G.ln_eps[:, 0:1])
                tf.scalar(act, G)

            def residual(dve, k):
                dve.wait_ge(o_mm, k + 1)
                c = slice(k * CPT, (k + 1) * CPT)
                dve.tensor_tensor(R[:, c, :], G.bank[4 + k % 2][:, 0:CPT * D].rearrange("p (c d) -> p c d", d=D),
                                  G.tm[:, c, :], ALU.add).then_inc(o_s, 1)

            @block.vector
            def _(dve):
                o = Steps(dve, own)
                dve.memset(bn_eps[:, :], BN_EPS).then_inc(var_s, 1)
                dve.memset(ones[:, :], 1.0).then_inc(feat_s, 1)
                o.then(dve.tensor_reduce(feat[:, 0, :], G.hT[:, :].rearrange("d (b f) -> d f b", f=T), AX_X, ALU.add))
                o.then(dve.tensor_scalar(feat[:, 0, :], feat[:, 0, :], 1.0 / B, None, ALU.mult))
                dve.tensor_copy(feat[:, 1, :], feat[:, 0, :]).then_inc(feat_s, 1)
                dve.wait_ge(std_s, 2)
                for i in "12":
                    A_, B_, t_ = par["A" + i], par["B" + i], par["t" + i]
                    o.then(dve.reciprocal(A_[:, :], t_[:, :]))
                    o.then(dve.tensor_tensor(A_[:, :], A_[:, :], par["g" + i][:, :], ALU.mult))
                    o.then(dve.tensor_tensor(B_[:, :], par["b" + i][:, :], par["m" + i][:, :], ALU.subtract))
                    o.then(dve.tensor_tensor(B_[:, :], B_[:, :], A_[:, :], ALU.mult))
                    dve.tensor_tensor(B_[:, :], B_[:, :], par["be" + i][:, :], ALU.add).then_inc(ab_s, 1)
                dve.wait_ge(log_mm, 1)
                o.then(dve.tensor_copy(glog[:, :], G.bank[7][:, 0:EXP0]))
                dve.tensor_reduce(gm[:, :], glog[:, :], AX_X, ALU.max, negate=True).then_inc(neg_s, 1)
                dve.wait_ge(exp_s, 1)
                o.then(dve.reciprocal(gi[:, :], gs[:, :]))
                dve.tensor_scalar(gate[:, :], gate[:, :], gi[:, 0:1], None, ALU.mult).then_inc(gate_s, 1)
                dve.wait_ge(gT_mm, 1)
                dve.tensor_copy(gT[:, :], G.bank[6][0:EXP0, 0:P]).then_inc(gT_s, 1)
                dve.wait_ge(rep_mm, 1)
                o.then(dve.tensor_copy(wrep[:, :, :], G.bank[7][:, 64:64 + NPAIR * T]))
                for n in range(NT * NPAIR):
                    k, q = n // NPAIR, n % NPAIR
                    dve.wait_ge(l2_s, n + 1)
                    if q == 0 and k >= 2:
                        dve.wait_ge(o_mm, k - 1)
                    dve.tensor_tensor(H2w[:, k % 2, q, :].rearrange("p (b f) -> p b f", f=T),
                                      H2[:, n % 2, :].rearrange("p (b f) -> p b f", f=T),
                                      wrep[:, q:q + 1, :].to_broadcast([P, TILE // T, T]), ALU.mult).then_inc(gw_s, 1)
                    if q == NPAIR - 1 and k >= 1:
                        residual(dve, k - 1)
                residual(dve, NT - 1)
                dve.wait_ge(o_s, NT)
                ln.vector(dve)
                tf.vector(dve, G)


def attention1(nc, G, A):
    with stage(nc, G) as st:
        DxT = st.sb("dx_t", [D, NSTATE])
        DyT = st.sb("dy_t", [D, NSTATE])
        Ew = st.sb("e_w", [P, NH2, D])
        decay = st.sb("decay", [P, P])
        ones = st.sb("ones_sq", [P, P])
        X = st.sb("state_x", [P, NH2, NTOK])
        S = st.sb("state_sum", [P, NTOK])
        sig = st.sb("state_sigma", [P, B])
        rate = st.sb("state_rate", [P, TILE])
        SM = st.sb("masked_scores", [P, NC, P])
        lnv = st.sb("lnv", [P, NC, D])
        xa = st.sb("xa", [P, NC, D])
        xb = st.sb("xb", [P, NC, D])
        par_in = st.sem("attn1_params_in")
        ones_s = st.sem("attn1_ones")
        u_mm, u_s, sum_mm, sum_s = st.sem("u_mm"), st.sem("u_relu"), st.sem("sum_mm"), st.sem("sum_kept")
        own, chain, x_s = st.sem("attn1_dve_steps"), st.sem("state_sum_steps"), st.sem("state_x_ready")
        st_mm, sm_s, a_mm, a_s = st.sem("st_mm"), st.sem("sm_masked"), st.sem("a_mm"), st.sem("a_kept")
        y_mm, y_s, v_mm, v_s = st.sem("y_mm"), st.sem("y_s"), st.sem("v_mm"), st.sem("v_kept")
        lnv_n = LayerNorm(st, "lnv_n", G.tm, lnv, xb, xc=xa)
        lna = LayerNorm(st, "lna_n", xa, xb, lnv)
        lnw = LayerNorm(st, "lnw_n", xa, xb, lnv)
        lnh = LayerNorm(st, "lnh_n", xa, G.tm, lnv)
        ta = ToFeatures(st, "a_turn", xb, G.hT, lna.normed, True)
        th = ToFeatures(st, "ln3_turn", G.tm, G.hT, lnh.normed, True)
        S3 = S[:, :].rearrange("p (b t) -> p b t", t=T)
        with nc.Block() as block:
            @block.sync
            def _(sp):
                sp.dma_start(DxT[:, :], A["L1_attn_DxT"]).then_inc(par_in, 16)
                sp.dma_start(DyT[:, :], A["L1_attn_DyT"]).then_inc(par_in, 16)
                sp.dma_start(Ew[:, :, :], A["L1_attn_ET"].rearrange("(g p) d -> p g d", g=NH2)).then_inc(par_in, 16)
                sp.dma_start(decay[:, :], A["c_decay"]).then_inc(par_in, 16)

            @block.tensor
            def _(pe):
                pe.wait_ge(par_in, 64)
                pe.wait_ge(ones_s, 1)

                def sums(k):
                    if k >= 2:
                        pe.wait_ge(sum_s, k - 1)
                    pe.wait_ge(u_s, 2 * k + 2)
                    for g in range(NH2):
                        ins = pe.matmul(G.bank[4 + k % 2][:, :], ones[:, :], X[:, g, k * TILE:(k + 1) * TILE],
                                        start=(g == 0), stop=(g == NH2 - 1))
                    ins.then_inc(sum_mm, 1)

                for k in range(NT):
                    for g in range(NH2):
                        n = 2 * k + g
                        if n >= 4:
                            pe.wait_ge(u_s, n - 3)
                        pe.matmul(G.bank[n % 4][:, :], DxT[:, g * P:(g + 1) * P], G.hT[:, k * TILE:(k + 1) * TILE],
                                  start=True, stop=True).then_inc(u_mm, 1)
                    if k:
                        sums(k - 1)
                sums(NT - 1)
                pe.wait_ge(sum_s, NT)
                for k in range(NT):
                    pe.wait_ge(x_s, k + 1)
                    for i in range(CPT):
                        c = slice((k * CPT + i) * P, (k * CPT + i + 1) * P)
                        for g in range(NH2):
                            ins = pe.matmul(G.bank[k][:, i * P:(i + 1) * P], X[:, g, c], X[:, g, c], start=(g == 0),
                                            stop=(g == NH2 - 1))
                    ins.then_inc(st_mm, 1)
                for k in range(4):
                    pe.wait_ge(sm_s, 2 * k + 2)
                    pe.wait_ge(lnv_n.normed, k + 1)
                    for i in range(8):
                        c = 8 * k + i
                        ins = pe.matmul(G.bank[k][:, i * D:(i + 1) * D], SM[:, c, :], lnv[:, c, :], start=True, stop=True)
                    ins.then_inc(a_mm, 1)
                ta.tensor(pe, G)
                for k in range(NT):
                    pe.wait_ge(ta.kept_dve if k % 2 else ta.kept_act, k // 2 + 1)
                    for g in range(NH2):
                        n = 2 * k + g
                        if n == 0:
                            ta.wait(pe)
                        if n >= 8:
                            pe.wait_ge(y_s, n - 7)
                        pe.matmul(G.bank[n % 8][:, :], DyT[:, g * P:(g + 1) * P], G.hT[:, k * TILE:(k + 1) * TILE],
                                  start=True, stop=True).then_inc(y_mm, 1)
                for k in range(4):
                    if k == 0:
                        pe.wait_ge(y_s, 16)
                    for i in range(8):
                        c = 8 * k + i
                        for g in range(NH2):
                            ins = pe.matmul(G.bank[k][:, i * D:(i + 1) * D], X[:, g, c * P:(c + 1) * P], Ew[:, g, :],
                                            start=(g == 0), stop=(g == NH2 - 1))
                    ins.then_inc(v_mm, 1)
                th.tensor(pe, G)

            @block.scalar
            def _(act):
                for n in range(2 * NT):
                    act.wait_ge(u_mm, n + 1)
                    act.activation(X[:, n % 2, (n // 2) * TILE:(n // 2 + 1) * TILE], G.bank[n % 4][:, :],
                                   ACT.Relu).then_inc(u_s, 1)
                lnv_n.scalar(act, G.ln_eps[:, 0:1])
                lna.scalar(act, G.ln_eps[:, 0:1])
                ta.scalar(act, G)
                lnw.scalar(act, G.ln_eps[:, 0:1])
                lnh.scalar(act, G.ln_eps[:, 0:1])
                th.scalar(act, G)

            @block.vector
            def _(dve):
                o = Steps(dve, own)
                dve.memset(ones[:, :], 1.0).then_inc(ones_s, 1)
                for k in range(NT):
                    dve.wait_ge(sum_mm, k + 1)
                    dve.tensor_copy(S[:, k * TILE:(k + 1) * TILE], G.bank[4 + k % 2][:, :]).then_inc(sum_s, 1)
                dve.wait_ge(sum_s, NT)
                with dve.Fori(1, T) as t:
                    dve.tensor_scalar(sig[:, :], S3[:, :, bass.ds(t - 1, 1)].rearrange("p b o -> p (b o)"),
                                      1.0 / L1_EPS, 1.0, ALU.mult, ALU.min).then_inc(chain, 1)
                    dve.wait_ge(chain, 2 * t - 1)
                    now = S3[:, :, bass.ds(t, 1)].rearrange("p b o -> p (b o)")
                    dve.scalar_tensor_tensor(out=now, in0=sig[:, :], scalar=DECAY, in1=now, op0=ALU.mult,
                                             op1=ALU.add).then_inc(chain, 1)
                    dve.wait_ge(chain, 2 * t)
                for k in range(NT):
                    c = slice(k * TILE, (k + 1) * TILE)
                    o.then(dve.tensor_scalar(S[:, c], S[:, c], L1_EPS, None, ALU.max))
                    o.then(dve.reciprocal(S[:, c], S[:, c]))
                    o.then(dve.tensor_scalar(rate[:, :], S[:, c], DECAY, None, ALU.mult))
                    o.then(dve.memset(rate[:, ::T], 0.0))
                    for g in range(NH2):
                        o.mark(dve.tensor_tensor(X[:, g, c], X[:, g, c], S[:, c], ALU.mult))
                    dve.wait_ge(own, o.n)
                    for g in range(NH2):
                        ins = o.mark(dve.tensor_tensor_scan(X[:, g, c], rate[:, :], X[:, g, c], 0.0, ALU.mult, ALU.add))
                    dve.wait_ge(own, o.n)
                    dve.sem_inc(x_s, 1)
                for k in range(NT):
                    dve.wait_ge(st_mm, k + 1)
                    dve.tensor_tensor(SM[:, k * CPT:(k + 1) * CPT, :], G.bank[k][:, :].rearrange("p (c t) -> p c t", t=P),
                                      decay[:, :].unsqueeze(1).to_broadcast([P, CPT, P]), ALU.mult).then_inc(sm_s, 1)
                lnv_n.vector(dve)
                for k in range(4):
                    dve.wait_ge(a_mm, k + 1)
                    dve.tensor_copy(xa[:, 8 * k:8 * k + 8, :], G.bank[k][:, :].rearrange("p (c d) -> p c d", d=D)
                                    ).then_inc(a_s, 1)
                dve.wait_ge(a_s, 4)
                lna.vector(dve)
                ta.vector(dve, G)
                for n in range(2 * NT):
                    x = X[:, n % 2, (n // 2) * TILE:(n // 2 + 1) * TILE]
                    dve.wait_ge(y_mm, n + 1)
                    dve.scalar_tensor_tensor(out=x, in0=G.bank[n % 8][:, :], scalar=0.0, in1=x, op0=ALU.max,
                                             op1=ALU.mult).then_inc(y_s, 1)
                for k in range(4):
                    dve.wait_ge(v_mm, k + 1)
                    dve.tensor_copy(xa[:, 8 * k:8 * k + 8, :], G.bank[k][:, :].rearrange("p (c d) -> p c d", d=D)
                                    ).then_inc(v_s, 1)
                dve.wait_ge(v_s, 4)
                lnw.vector(dve)
                dve.wait_ge(lnw.normed, LG)
                o.then(dve.tensor_tensor(xa[:, :, :], xb[:, :, :], G.tm[:, :, :], ALU.add))
                lnh.vector(dve)
                th.vector(dve, G)


def graph_counts(nc, G, A):
    with stage(nc, G) as st:
        e_i = st.sb("edge_ints", [P, 2, EW], I32)
        srcf = st.sb("srcf", [P, EW])
        dstf = st.sb("dstf", [P, EW])
        tmp = st.sb("edge_tmp", [P, EW])
        hi = st.sb("dst_hi", [P, EW], BF16)
        lo = st.sb("dst_lo", [P, EW], BF16)
        hot = st.sb("dst_one_hot", [P, P, SPREAD // 2], BF16)
        zero = st.sb("zero_weights", [P, P], BF16)
        par = st.sb("hi_parity", [64, 2])
        half = st.sb("hi_half", [64, NC])
        split = st.sb("hist_split", [64, 2, 64])
        near_n = st.sb("near_count", [P, 1])
        near_max = st.sb("near_max", [P, 1])
        r_i = st.sb("rounds_tmp", [P, 1], I32)
        e_in, c_in, own = st.sem("edges_in"), st.sem("hist_consts_in"), st.sem("counts_dve_steps")
        near_s, max_s = st.sem("near_counted"), st.sem("near_max_ready")
        hot_s, used_s, split_s, far_mm = (st.sem("one_hots"), st.sem("one_hots_used"), st.sem("hist_split_ready"),
                                          st.sem("far_mm"))
        zero_s = st.sem("zero_weights_ready")
        W = SPREAD // 2
        NS = EW // W
        ev = A["L1_ffn_edge_index"].rearrange("s (p w) -> s p w", p=P)
        with nc.Block() as block:
            @block.sync
            def _(sp):
                sp.dma_start(e_i[:, 0, :], ev[0]).then_inc(e_in, 16)
                sp.dma_start(e_i[:, 1, :], ev[1]).then_inc(e_in, 16)
                sp.dma_start(par[:, :], A["c_hi_parity"]).then_inc(c_in, 16)
                sp.dma_start(half[:, :], A["c_hi_half"]).then_inc(c_in, 16)

            @block.gpsimd
            def _(pool):
                pool.wait_ge(near_s, 1)
                pool.partition_all_reduce(near_max[:, :], near_n[:, :], P, bass.bass_isa.ReduceOp.max
                                          ).then_inc(max_s, 1)

            @block.vector
            def _(dve):
                o = Steps(dve, own)
                dve.memset(zero[:, :], 0.0).then_inc(zero_s, 1)
                dve.wait_ge(e_in, 32)
                o.mark(dve.tensor_copy(srcf[:, :], e_i[:, 0, :]))
                o.then(dve.tensor_copy(dstf[:, :], e_i[:, 1, :]))
                o.then(dve.tensor_scalar(tmp[:, :], srcf[:, :], float(FAR), None, ALU.is_lt))
                o.mark(dve.tensor_scalar(e_i[:, 0, :], e_i[:, 1, :], 6, None, ALU.logical_shift_right))
                o.then(dve.tensor_scalar(e_i[:, 1, :], e_i[:, 1, :], 63, None, ALU.bitwise_and))
                o.mark(dve.scalar_tensor_tensor(out=hi[:, :], in0=tmp[:, :], scalar=256.0, in1=e_i[:, 0, :],
                                                op0=ALU.mult, op1=ALU.add))
                o.then(dve.tensor_copy(lo[:, :], e_i[:, 1, :]))
                o.then(dve.scalar_tensor_tensor(out=tmp[:, :], in0=dstf[:, :], scalar=float(NTOK), in1=tmp[:, :],
                                                op0=ALU.is_lt, op1=ALU.mult))
                dve.tensor_reduce(near_n[:, :], tmp[:, :], AX_X, ALU.add).then_inc(near_s, 1)
                o.then(dve.scalar_tensor_tensor(out=srcf[:, :], in0=dstf[:, :], scalar=float(NTOK), in1=srcf[:, :],
                                                op0=ALU.mult, op1=ALU.add))
                o.then(dve.scalar_tensor_tensor(out=srcf[:, :], in0=srcf[:, :], scalar=1.0, in1=tmp[:, :],
                                                op0=ALU.add, op1=ALU.mult))
                o.then(dve.tensor_scalar(G.keys[:, :], srcf[:, :], -1.0, None, ALU.add))
                dve.wait_ge(max_s, 1)
                o.then(dve.tensor_scalar(near_max[:, :], near_max[:, :], 15.0, 16.0, ALU.add, ALU.max))
                o.then(dve.tensor_copy(r_i[:, :], near_max[:, :]))
                o.then(dve.tensor_scalar(G.rounds[:, :], r_i[:, :], 4, None, ALU.logical_shift_right))
                with dve.Fori(0, NS) as q:
                    dve.wait_ge(used_s, q + 1)
                    for v in range(64):
                        dve.tensor_scalar(hot[:, v, :], hi[:, bass.ds(q * W, W)], float(v), None, ALU.is_equal)
                    for v in range(64):
                        ins = dve.tensor_scalar(hot[:, 64 + v, :], lo[:, bass.ds(q * W, W)], float(v), None,
                                                ALU.is_equal)
                    ins.then_inc(hot_s, 1)
                dve.wait_ge(used_s, NS + 1)
                dve.wait_ge(c_in, 32)
                for r in range(2):
                    ins = dve.tensor_scalar(split[:, r, :], G.bank[0][0:64, 0:64], par[:, r:r + 1], None, ALU.mult)
                    ins.then_inc(split_s, 1)
                dve.wait_ge(far_mm, 1)
                o.then(dve.tensor_copy(G.n_far[:, :], G.bank[1][:, 0:NC]))

            @block.tensor
            def _(pe):
                pe.wait_ge(zero_s, 1)
                pe.matmul(G.bank[0][:, 0:64], zero[:, :], zero[:, 0:64], start=True, stop=True).then_inc(used_s, 1)
                with pe.Fori(0, NS) as q:
                    pe.wait_ge(hot_s, q + 1)
                    for e in range(W):
                        ins = pe.matmul(G.bank[0][:, 0:64], hot[:, :, e], hot[:, 64:P, e], start=False, stop=True,
                                        skip_group_check=True)
                    ins.then_inc(used_s, 1)
                pe.wait_ge(split_s, 2)
                pe.matmul(G.bank[1][:, 0:NC], split[:, :, :].rearrange("h r l -> h (r l)"), half[:, :], start=True,
                          stop=True).then_inc(far_mm, 1)


def graph_sort(nc, G, A):
    with stage(nc, G) as st:
        iota = st.sb("bins_iota", [P, P], BF16)
        later_f = st.sb("later_f32", [P, P])
        later = st.sb("later", [P, P], BF16)
        upto = st.sb("upto", [P, P], BF16)
        ones = st.sb("ones_bf", [P, P], BF16)
        none = st.sb("empty_slots", [P, PART])
        top = st.sb("top_keys", [P, 8])
        k_i = st.sb("key_i", [P, 8], I32)
        dst_i = st.sb("dst_i", [P, 8], I32)
        bin_i = st.sb("bin_i", [P, 8], I32)
        loc_i = st.sb("loc_i", [P, 8], I32)
        pad = st.sb("pad_f", [P, 8])
        pad_i = st.sb("pad_i", [P, 8], I32)
        bin_f = st.sb("bin_f", [P, 8])
        rank = st.sb("rank_f", [P, 8])
        rank_i = st.sb("rank_i", [P, 8], I32)
        hot = st.sb("bin_one_hot", [P, 8, P], BF16)
        prod = st.sb("rank_prod", [P, 8, P])
        key = [st.sb(f"slot_key{u}", [P, 8]) for u in range(2)]
        idx = [st.sb(f"slot_index{u}", [P, 8], I32) for u in range(2)]
        tmax = st.sb("bin_max", [P, 1])
        tmx = st.sb("bin_max_all", [P, 1])
        p_i = st.sb("parts_i", [P, 1], I32)
        iota_s, c_in, none_s, none_in = st.sem("iota_s"), st.sem("later_in"), st.sem("empty_ready"), st.sem("emptied")
        tri_s, own, hot_s = st.sem("triangles"), st.sem("sort_dve_steps"), st.sem("bin_one_hots")
        rank_mm, read_s, sum_mm = st.sem("rank_mm"), st.sem("ranks_read"), st.sem("totals_mm")
        idx_s, scat, free = st.sem("slot_index_ready"), st.sem("slots_written"), st.sem("slot_buffers_free")
        cnt_s, cmax_s, seen = st.sem("bin_counted"), st.sem("bin_max_ready"), st.sem("slot_index_seen")
        PER = 64
        with nc.Block() as block:
            @block.gpsimd
            def _(pool):
                pool.iota(iota[:, :], [[1, P]], base=0, channel_multiplier=0,
                          allow_small_or_imprecise_dtypes=True).then_inc(iota_s, 1)
                pool.wait_ge(none_in, 16)
                n = pool.value_load(G.rounds[0:1, 0:1], min_val=1, max_val=EW // 16)
                with pool.Fori(0, n) as i:
                    for u in range(2):
                        pool.wait_ge(idx_s, i * 2 + (u + 1))
                        pool.sem_inc(seen, 1)
                        for t in range(8):
                            pool.indirect_dma_start(A["slots"], bass.IndirectOffsetOnAxis(ap=idx[u][:, t:t + 1], axis=0),
                                                    key[u][:, t:t + 1], None, bounds_check=NSLOT - 1,
                                                    oob_is_err=False).then_inc(scat, 16)
                        pool.wait_ge(scat, i * 256 + (u + 1) * 128)
                        pool.sem_inc(free, 1)
                pool.wait_ge(cnt_s, 1)
                pool.partition_all_reduce(tmx[:, :], tmax[:, :], P, bass.bass_isa.ReduceOp.max).then_inc(cmax_s, 1)

            @block.sync
            def _(sp):
                sp.dma_start(later_f[:, :], A["c_later"]).then_inc(c_in, 16)
                sp.wait_ge(none_s, 1)
                sp.dma_start(A["slots"].rearrange("(p s) o -> p (s o)", p=P)[:, 0:PART], none[:, :]).then_inc(none_in, 16)

            @block.tensor
            def _(pe):
                pe.wait_ge(tri_s, 2)
                for h in range(2):
                    ins = pe.matmul(G.bank[h][:, :], ones[:, :], hot[:, 0:4, :], start=True, stop=True)
                ins.then_inc(sum_mm, 1)
                n = pe.value_load(G.rounds[0:1, 0:1], min_val=1, max_val=EW // 16)
                with pe.Fori(0, n) as i:
                    for u in range(2):
                        pe.wait_ge(hot_s, i * 2 + (u + 1))
                        for t in range(8):
                            for m in range(t, 8):
                                ins = pe.matmul(G.bank[m // 4][:, (m % 4) * P:(m % 4 + 1) * P],
                                                later[:, :] if m == t else ones[:, :], hot[:, t, :], start=False,
                                                stop=True, skip_group_check=True)
                        ins.then_inc(rank_mm, 1)
                        pe.wait_ge(read_s, i * 2 + (u + 1))
                        for t in range(8):
                            for m in range(0, t + 1):
                                ins = pe.matmul(G.bank[m // 4][:, (m % 4) * P:(m % 4 + 1) * P],
                                                upto[:, :] if m == t else ones[:, :], hot[:, t, :], start=False,
                                                stop=True, skip_group_check=True)
                        ins.then_inc(sum_mm, 1)

            @block.vector
            def _(dve):
                dve.memset(none[:, :], -1.0).then_inc(none_s, 1)
                dve.memset(ones[:, :], 1.0)
                dve.memset(hot[:, :, :], 0.0).then_inc(tri_s, 1)
                dve.wait_ge(c_in, 16)
                dve.tensor_copy(later[:, :], later_f[:, :])
                dve.tensor_scalar(upto[:, :], later_f[:, :], -1.0, 1.0, ALU.mult, ALU.add).then_inc(tri_s, 1)
                dve.wait_ge(iota_s, 1)
                dve.wait_ge(tri_s, 2)
                dve.sem_inc(free, 2)
                n = dve.value_load(G.rounds[0:1, 0:1], min_val=1, max_val=EW // 16)
                with dve.Fori(0, n) as i:
                    o = Steps(dve, own, i * PER)
                    for u in range(2):
                        o.then(dve.max(top[:, :], G.keys[:, :]))
                        o.mark(dve.tensor_scalar(pad[:, :], top[:, :], 0.0, None, ALU.is_lt))
                        o.mark(dve.match_replace(G.keys[:, :], top[:, :], G.keys[:, :], -1.0))
                        o.then(dve.tensor_copy(k_i[:, :], top[:, :]))
                        o.mark(dve.tensor_copy(pad_i[:, :], pad[:, :]))
                        o.then(dve.tensor_scalar(dst_i[:, :], k_i[:, :], 12, None, ALU.arith_shift_right))
                        o.mark(dve.tensor_scalar(bin_i[:, :], dst_i[:, :], P - 1, None, ALU.bitwise_and))
                        o.mark(dve.tensor_scalar(loc_i[:, :], dst_i[:, :], 7, 13, ALU.arith_shift_right,
                                                 ALU.logical_shift_left))
                        o.then(dve.tensor_scalar(k_i[:, :], k_i[:, :], NTOK - 1, None, ALU.bitwise_and))
                        o.mark(dve.tensor_tensor(k_i[:, :], k_i[:, :], loc_i[:, :], ALU.bitwise_or))
                        o.then(dve.scalar_tensor_tensor(out=bin_f[:, :], in0=pad[:, :], scalar=1024.0,
                                                        in1=bin_i[:, :], op0=ALU.mult, op1=ALU.add))
                        dve.wait_ge(free, i * 2 + (u + 1))
                        dve.wait_ge(sum_mm, i * 2 + (u + 1))
                        o.mark(dve.tensor_copy(key[u][:, :], k_i[:, :]))
                        for t in range(8):
                            ins = dve.tensor_scalar(hot[:, t, :], iota[:, :], bin_f[:, t:t + 1], None, ALU.is_equal)
                        o.then(ins)
                        dve.sem_inc(hot_s, 1)
                        dve.wait_ge(rank_mm, i * 2 + (u + 1))
                        for h in range(2):
                            ins = o.mark(dve.tensor_tensor(prod[:, 4 * h:4 * h + 4, :],
                                                           G.bank[h][:, :].rearrange("p (t b) -> p t b", b=P),
                                                           hot[:, 4 * h:4 * h + 4, :], ALU.mult))
                        o.wait()
                        dve.sem_inc(read_s, 1)
                        o.then(dve.tensor_reduce(rank[:, :], prod[:, :, :], AX_X, ALU.add))
                        o.mark(dve.tensor_scalar(bin_i[:, :], bin_i[:, :], BIN_BITS, None, ALU.logical_shift_left))
                        o.mark(dve.tensor_scalar(pad_i[:, :], pad_i[:, :], BIN_BITS + 8, None, ALU.logical_shift_left))
                        o.then(dve.tensor_copy(rank_i[:, :], rank[:, :]))
                        o.then(dve.tensor_tensor(rank_i[:, :], rank_i[:, :], bin_i[:, :], ALU.bitwise_or))
                        o.then(dve.tensor_tensor(idx[u][:, :], rank_i[:, :], pad_i[:, :], ALU.bitwise_or))
                        dve.sem_inc(idx_s, 1)
                    o.close(PER)
                f = Steps(dve, cnt_s, 0)
                dve.wait_ge(sum_mm, n * 2 + 1)
                dve.tensor_tensor_reduce(out=prod[:, 0, :], in0=G.bank[0][:, 0:P], in1=G.ident[:, :], scale=1.0,
                                         scalar=0.0, op0=ALU.mult, op1=ALU.add, accum_out=G.n_bin[:, 0:1]
                                         ).then_inc(tri_s, 1)
                dve.wait_ge(tri_s, 3)
                f.then(dve.tensor_copy(tmax[:, :], G.n_bin[:, :]))
                dve.wait_ge(cmax_s, 1)
                f.then(dve.tensor_scalar(tmax[:, :], tmx[:, :], float(PART), float(NC + 15), ALU.min, ALU.add))
                f.then(dve.tensor_copy(p_i[:, :], tmax[:, :]))
                f.then(dve.tensor_scalar(G.groups[:, :], p_i[:, :], 4, None, ALU.logical_shift_right))
                f.then(dve.tensor_scalar(tmx[:, :], tmx[:, :], 1.0, None, ALU.max))
                f.then(dve.tensor_scalar(tmx[:, :], tmx[:, :], 1.0 / PART, 0.5 - 0.5 / PART, ALU.mult, ALU.add))
                f.then(dve.tensor_copy(p_i[:, :], tmx[:, :]))
                f.then(dve.tensor_copy(G.passes[:, :], p_i[:, :]))


def experts1(nc, G, A):
    with stage(nc, G) as st:
        W1 = st.sb("e1_w1", [D, EXP1, HID1])
        b1 = st.sb("e1_b1", [HID1, EXP1])
        W2 = st.sb("e1_w2", [HID1, EXP1, D])
        b2 = st.sb("e1_b2", [P, EXP1 * D])
        Wg = st.sb("gat_w", [D, ROW])
        att = st.sb("gat_att", [D, 2, HEADS * EXP1])
        wa = st.sb("gat_w_att", [D, 2, HEADS * EXP1])
        HH = st.sb("e1_hidden", [P, 2, EXP1, TILE])
        w_in, own, wg_s = st.sem("e1_weights_in"), st.sem("e1_dve_steps"), st.sem("gat_w_ready")
        tab_mm, tab_s, tab_out = st.sem("table_mm"), st.sem("table_kept"), st.sem("table_out")
        l1_mm, gelu_s, l2_mm, x_s = st.sem("e1_l1_mm"), st.sem("e1_gelu"), st.sem("e1_l2_mm"), st.sem("e1_out_kept")
        with nc.Block() as block:
            @block.sync
            def _(sp):
                sp.dma_start(Wg[:, 0:16], A["L1_ffn_W_gat"]).then_inc(w_in, 16)
                for i, n in enumerate((A["L1_ffn_att_src"], A["L1_ffn_att_dst"])):
                    sp.dma_start(att[:, i, :], n.rearrange("(o h) e -> o (h e)", o=1).to_broadcast([D, 16])
                                 ).then_inc(w_in, 16)
                sp.dma_start(W1[:, :, :], A["L1_ffn_W1"].rearrange("e d h -> d e h")).then_inc(w_in, 16)
                sp.dma_start(b1[:, :], A["L1_ffn_b1T"]).then_inc(w_in, 16)
                sp.dma_start(W2[:, :, :], A["L1_ffn_W2"].rearrange("e h d -> h e d")).then_inc(w_in, 16)
                sp.dma_start(b2[:, :], A["L1_ffn_b2"].rearrange("(o e) d -> o (e d)", o=1).to_broadcast([P, EXP1 * D])
                             ).then_inc(w_in, 16)
                sp.wait_ge(tab_s, 2)
                sp.dma_start(A["table"].rearrange("(c p) f -> p c f", p=P), G.tab[:, :, :]).then_inc(tab_out, 16)
                sp.wait_ge(tab_out, 16)
                sp.dma_start(G.far[:, :], A["table"][FAR:FAR + 1, :].to_broadcast([P, ROW])).then_inc(tab_out, 16)
                sp.wait_ge(tab_out, 32)

            @block.tensor
            def _(pe):
                pe.wait_ge(w_in, 112)
                pe.wait_ge(wg_s, 1)
                for h in range(2):
                    for i in range(16):
                        c = 16 * h + i
                        ins = pe.matmul(G.bank[h][:, i * ROW:(i + 1) * ROW], G.hT[:, c * P:(c + 1) * P], Wg[:, :],
                                        start=True, stop=True)
                    ins.then_inc(tab_mm, 1)

                def layer2(k):
                    pe.wait_ge(gelu_s, EXP1 * (k + 1))
                    for h in range(2):
                        n = 2 * k + h
                        if n >= 2:
                            pe.wait_ge(x_s, n - 1)
                        for i in range(2):
                            for e in range(EXP1):
                                ins = pe.matmul(G.bank[6 + h][:, (i * EXP1 + e) * D:(i * EXP1 + e + 1) * D],
                                                HH[:, k % 2, e, (2 * h + i) * P:(2 * h + i + 1) * P], W2[:, e, :],
                                                start=True, stop=True)
                        ins.then_inc(l2_mm, 1)

                for k in range(NT):
                    for e in range(EXP1):
                        n = k * EXP1 + e
                        if n >= EXP1:
                            pe.wait_ge(gelu_s, n - EXP1 + 1)
                        pe.matmul(G.bank[2 + n % 4][:, :], W1[:, e, :], G.hT[:, k * TILE:(k + 1) * TILE], start=True,
                                  stop=True).then_inc(l1_mm, 1)
                    if k:
                        layer2(k - 1)
                layer2(NT - 1)

            @block.scalar
            def _(act):
                for n in range(NT * EXP1):
                    k, e = n // EXP1, n % EXP1
                    act.wait_ge(l1_mm, n + 1)
                    if k >= 2 and e == 0:
                        act.wait_ge(l2_mm, 2 * (k - 1))
                    act.activation(HH[:, k % 2, e, :], G.bank[2 + n % 4][:, :], ACT.Gelu, bias=b1[:, e:e + 1]
                                   ).then_inc(gelu_s, 1)

            @block.vector
            def _(dve):
                o = Steps(dve, own)
                dve.wait_ge(w_in, 112)
                o.then(dve.tensor_tensor(wa[:, :, :], att[:, :, :], Wg[:, 0:16].unsqueeze(1).to_broadcast([D, 2, 16]),
                                         ALU.mult))
                dve.tensor_reduce(Wg[:, 16:24], wa[:, :, :].rearrange("d s (h e) -> d (s h) e", e=EXP1), AX_X,
                                  ALU.add).then_inc(wg_s, 1)
                for h in range(2):
                    dve.wait_ge(tab_mm, h + 1)
                    dve.tensor_copy(G.tab[:, 16 * h:16 * h + 16, :], G.bank[h][:, 0:16 * ROW].rearrange(
                        "p (c f) -> p c f", f=ROW)).then_inc(tab_s, 1)
                for n in range(2 * NT):
                    dve.wait_ge(l2_mm, n + 1)
                    dve.tensor_tensor(G.xo[:, 2 * n:2 * n + 2, :], G.bank[6 + n % 2][:, :].rearrange(
                        "p (c f) -> p c f", f=EXP1 * D), b2[:, :].unsqueeze(1).to_broadcast([P, 2, EXP1 * D]),
                        ALU.add).then_inc(x_s, 1)


def graph_fill(nc, G, A):
    with stage(nc, G) as st:
        base = st.sb("fill_base", [P, 8])
        slot = st.sb("fill_slot", [P, 8])
        full = st.sb("fill_full", [P, 8])
        f_i = st.sb("fill_full_i", [P, 8], I32)
        s_i = st.sb("fill_slot_i", [P, 8], I32)
        bin_i = st.sb("fill_bin", [P, 8], I32)
        idx = st.sb("fill_index", [P, 8], I32)
        minus = st.sb("fill_value", [P, 8])
        own, idx_s, out_s, iota_s = (st.sem("fill_dve_steps"), st.sem("fill_index_ready"), st.sem("fill_written"),
                                     st.sem("fill_iota"))
        done, seen = st.sem("fill_done"), st.sem("fill_index_seen")
        per = PART // 8
        with nc.Block() as block:
            @block.gpsimd
            def _(pool):
                pool.iota(s_i[:, :], [[1, 8]], base=0, channel_multiplier=0).then_inc(iota_s, 1)
                pool.iota(bin_i[:, :], [[0, 8]], base=0, channel_multiplier=1).then_inc(iota_s, 1)
                n = pool.value_load(G.passes[0:1, 0:1], min_val=1, max_val=NEDGE // PART)
                with pool.If(n > 1):
                    with pool.Fori(0, (n - 1) * per) as i:
                        pool.wait_ge(idx_s, i + 1)
                        pool.sem_inc(seen, 1)
                        for t in range(8):
                            pool.indirect_dma_start(A["slots"], bass.IndirectOffsetOnAxis(ap=idx[:, t:t + 1], axis=0),
                                                    minus[:, t:t + 1], None, bounds_check=NSLOT - 1,
                                                    oob_is_err=False).then_inc(out_s, 16)
                        pool.wait_ge(out_s, i * 128 + 128)
                        pool.sem_inc(done, 1)

            @block.vector
            def _(dve):
                dve.wait_ge(iota_s, 2)
                o = Steps(dve, own)
                o.mark(dve.memset(minus[:, :], -1.0))
                o.mark(dve.tensor_scalar(bin_i[:, :], bin_i[:, :], BIN_BITS, None, ALU.logical_shift_left))
                o.then(dve.tensor_copy(slot[:, :], s_i[:, :]))
                o.then(dve.tensor_scalar(slot[:, :], slot[:, :], float(PART), None, ALU.add))
                start, PER = o.n, 16
                n = dve.value_load(G.passes[0:1, 0:1], min_val=1, max_val=NEDGE // PART)
                with dve.If(n > 1):
                    with dve.Fori(0, (n - 1) * per) as i:
                        r = Steps(dve, own, i * PER + start)
                        r.then(dve.tensor_scalar(full[:, :], slot[:, :], G.n_bin[:, 0:1], None, ALU.is_lt))
                        r.mark(dve.tensor_copy(f_i[:, :], full[:, :]))
                        r.then(dve.tensor_copy(s_i[:, :], slot[:, :]))
                        r.mark(dve.tensor_scalar(f_i[:, :], f_i[:, :], BIN_BITS + 8, None, ALU.logical_shift_left))
                        r.then(dve.tensor_tensor(s_i[:, :], s_i[:, :], bin_i[:, :], ALU.bitwise_or))
                        r.then(dve.tensor_tensor(idx[:, :], s_i[:, :], f_i[:, :], ALU.bitwise_or))
                        dve.sem_inc(idx_s, 1)
                        r.then(dve.tensor_scalar(slot[:, :], slot[:, :], 8.0, None, ALU.add))
                        dve.wait_ge(done, i + 1)
                        r.close(PER)


def graph_attention(nc, G, A):
    with stage(nc, G) as st:
        sb, sem = st.sb, st.sem
        marks = sb("self_marks", [P, NC])
        marks_i = sb("self_marks_i", [P, NC], I32)
        thr_i = sb("node_thresholds_i", [P, NC], I32)
        thr = sb("node_thresholds", [P, NC])
        row_i = sb("list_row_i", [P, NC], I32)
        rowf = sb("list_row", [P, NC])
        L = sb("list_raw", [P, LIST])
        top = sb("list_top", [P, 8])
        K = sb("list_sorted", [P, LIST])
        Ki = sb("list_i", [P, LIST], I32)
        loc_i = sb("list_node_i", [P, LIST], I32)
        src_i = sb("list_src_i", [P, LIST], I32)
        self_i = sb("list_self_i", [P, LIST], I32)
        loc = sb("list_node", [P, LIST])
        valid = sb("list_valid", [P, LIST])
        selfm = sb("list_self", [P, LIST])
        first = sb("pass_is_first", [P, 1])
        cont = sb("same_as_before", [P, LIST])
        contb = sb("same_as_after", [P, LIST])
        mc = sb("before_penalty", [P, LIST])
        mb = sb("after_penalty", [P, LIST])
        ge = sb("at_or_above", [P, NC, LIST], BF16)
        endf = sb("segment_end", [P, NC])
        end_i = sb("segment_end_i", [P, NC], I32)
        Gt = sb("gathered", [P, LIST, ROW])
        AS = sb("edge_src", [P, HEADS, LIST])
        AD = sb("edge_dst", [P, HEADS, LIST])
        MF = sb("edge_max", [P, HEADS, LIST])
        MB = sb("edge_max_back", [P, HEADS, LIST])
        Wt = sb("edge_weight", [P, HEADS, LIST])
        MSG = sb("edge_msg", [P, 16, LIST])
        R = sb("segment_rows", [P, LIST, ROW])
        N = sb("node_rows", [P, NC, ROW])
        m_run = sb("node_max", [P, NC, HEADS])
        m_new = sb("node_max_new", [P, NC, HEADS])
        den = sb("node_den", [P, NC, HEADS])
        agg = sb("node_agg", [P, NC, 16])
        lr = [sb(f"node_lrelu{i}", [P, NC, HEADS]) for i in range(3)]
        zz = sb("node_z", [P, 3, NC, HEADS])
        t16 = sb("node_t16", [P, NC, 16])
        gp = {n: sb("gat_" + n, [P, 16]) for n in ("bias", "gamma", "beta")}
        before = sb("expert_before", [P, 16])
        s1, s2, s3 = sb("gate_s1", [P, NC]), sb("gate_s2", [P, NC]), sb("gate_s3", [P, NC])
        sc, ex, rk = sb("gate_scores", [P, NC, EXP1]), sb("gate_exp", [P, NC, EXP1]), sb("gate_rank", [P, NC, EXP1])
        p1, p2 = sb("gate_pairs", [P, NC, EXP1, EXP1]), sb("gate_pairs2", [P, NC, EXP1, EXP1])
        par_in, iota_s, own0, own = sem("gat_params_in"), sem("list_iotas"), sem("graph_dve_setup"), sem("graph_dve_steps")
        list_free, list_in, sort_s = sem("list_free"), sem("list_in"), sem("list_sorting")
        idx_s, gat, seen, seen_dve = sem("sources_ready"), sem("rows_gathered"), sem("pool_seen"), sem("dve_seen")
        dif_s, w_s, rows_s, rows_out, ends_in = (sem("exponents_ready"), sem("weights_ready"), sem("segment_rows_ready"),
                                                 sem("segment_rows_out"), sem("node_rows_in"))
        nd_s, ne_s = sem("rescale_exponents"), sem("rescales_ready")
        sq_a, sq_b, std_a, std_b, ex_a, ex_b = (sem("gate_centred"), sem("gate_squared"), sem("gate_var"),
                                                sem("gate_std"), sem("gate_logits"), sem("gate_exps"))
        PER, RPP = 128, LIST // 8 * 3
        fold = LIST // 16

        def per_node(x, n):
            return x.unsqueeze(3).to_broadcast([P, NC, HEADS, n])

        def passes(eng):
            return eng.value_load(G.passes[0:1, 0:1], min_val=1, max_val=NEDGE // PART)

        with nc.Block() as block:
            @block.sync
            def _(sp):
                for n, a in (("bias", A["L1_ffn_b_gat"]), ("gamma", A["L1_ffn_ln_gamma"]), ("beta", A["L1_ffn_ln_beta"])):
                    sp.dma_start(gp[n][:, :], a.rearrange("(o f) -> o f", o=1).to_broadcast([P, 16])).then_inc(par_in, 16)
                sp.dma_start(before[:, :], A["c_before"]).then_inc(par_in, 16)
                n = passes(sp)
                with sp.Fori(0, n) as k:
                    sp.wait_ge(list_free, k + 1)
                    sp.dma_start(L[:, NC:LIST], A["slots"].rearrange("(p s) o -> p (s o)", p=P)[:, bass.ds(k * PART, PART)]
                                 ).then_inc(list_in, 16)
                    sp.wait_ge(rows_s, k + 1)
                    sp.dma_start(A["ends"].rearrange("(p s) f -> p s f", p=P), R[:, :, :]).then_inc(rows_out, 16)

            @block.gpsimd
            def _(pool):
                pool.iota(marks_i[:, :], [[2 * NTOK + P, NC]], base=NTOK, channel_multiplier=1).then_inc(iota_s, 1)
                pool.iota(thr_i[:, :], [[2 * NTOK, NC]], base=0, channel_multiplier=0).then_inc(iota_s, 1)
                pool.iota(row_i[:, :], [[0, NC]], base=0, channel_multiplier=LIST).then_inc(iota_s, 1)
                n = passes(pool)
                m = pool.value_load(G.groups[0:1, 0:1], min_val=1, max_val=fold)
                with pool.Fori(0, n) as k:
                    pool.wait_ge(idx_s, k + 1)
                    pool.sem_inc(seen, 1)
                    for g in range(fold):
                        with pool.If(m + k * fold > g):
                            for j in range(16 * g, 16 * g + 16):
                                pool.indirect_dma_start(Gt[:, j, :], None, A["table"],
                                                        bass.IndirectOffsetOnAxis(ap=src_i[:, j:j + 1], axis=0)
                                                        ).then_inc(gat, 16)
                    pool.wait_ge(rows_out, 16 * k + 16)
                    pool.sem_inc(seen, 1)
                    for c in range(NC):
                        pool.indirect_dma_start(N[:, c, :], None, A["ends"],
                                                bass.IndirectOffsetOnAxis(ap=end_i[:, c:c + 1], axis=0)
                                                ).then_inc(ends_in, 16)

            @block.scalar
            def _(act):
                n = passes(act)
                with act.Fori(0, n) as k:
                    act.wait_ge(dif_s, k + 1)
                    act.activation(Wt[:, :, :], Wt[:, :, :], ACT.Exp).then_inc(w_s, 1)
                    act.wait_ge(nd_s, k + 1)
                    act.activation(zz[:, 0:2, :, :], zz[:, 0:2, :, :], ACT.Exp).then_inc(ne_s, 1)
                act.wait_ge(sq_a, 1)
                act.activation(t16[:, :, :], agg[:, :, :], ACT.Square).then_inc(sq_b, 1)
                act.wait_ge(std_a, 1)
                act.activation(s3[:, :], s2[:, :], ACT.Sqrt, bias=G.ln_eps[:, 0:1], scale=1.0 / 16).then_inc(std_b, 1)
                act.wait_ge(ex_a, 1)
                act.activation(ex[:, :, :], sc[:, :, :], ACT.Exp).then_inc(ex_b, 1)

            @block.vector
            def _(dve):
                o = Steps(dve, own0)
                dve.wait_ge(iota_s, 3)
                o.mark(dve.tensor_copy(marks[:, :], marks_i[:, :]))
                o.mark(dve.tensor_copy(thr[:, :], thr_i[:, :]))
                o.mark(dve.tensor_copy(rowf[:, :], row_i[:, :]))
                o.mark(dve.memset(first[:, :], 1.0))
                o.mark(dve.memset(Gt[:, :, :], 0.0))
                o.mark(dve.memset(cont[:, 0:1], 0.0))
                o.mark(dve.memset(contb[:, LIST - 1:LIST], 0.0))
                o.mark(dve.tensor_copy(den[:, :, :], G.n_far[:, :].unsqueeze(2).to_broadcast([P, NC, HEADS])))
                o.mark(dve.tensor_tensor(agg[:, :, :], G.n_far[:, :].unsqueeze(2).to_broadcast([P, NC, 16]),
                                         G.far[:, 0:16].unsqueeze(1).to_broadcast([P, NC, 16]), ALU.mult))
                o.then(dve.tensor_scalar(s1[:, :], G.n_far[:, :], 0.0, -BIG, ALU.is_equal, ALU.mult))
                o.then(dve.tensor_tensor(m_run[:, :, :], s1[:, :].unsqueeze(2).to_broadcast([P, NC, HEADS]),
                                         G.far[:, 16:20].unsqueeze(1).to_broadcast([P, NC, HEADS]), ALU.add))
                dve.sem_inc(list_free, 1)
                n = passes(dve)
                m = dve.value_load(G.groups[0:1, 0:1], min_val=1, max_val=fold)
                with dve.Fori(0, n) as k:
                    f = Steps(dve, own, k * PER)
                    dve.wait_ge(list_in, 16 * k + 16)
                    f.then(dve.tensor_copy(L[:, 0:NC], marks[:, :]))
                    dve.sem_inc(seen_dve, 1)
                    with dve.Fori(0, LIST // 8) as j:
                        r = Steps(dve, sort_s, k * RPP + j * 3)
                        r.then(dve.max(top[:, :], L[:, :]))
                        r.mark(dve.tensor_copy(K[:, bass.ds(j * 8, 8)], top[:, :]))
                        r.mark(dve.match_replace(L[:, :], top[:, :], L[:, :], -1.0))
                        r.wait()
                    dve.sem_inc(list_free, 1)
                    f.mark(dve.tensor_scalar(valid[:, :], K[:, :], 0.0, None, ALU.is_ge))
                    f.then(dve.tensor_copy(Ki[:, :], K[:, :]))
                    f.mark(dve.tensor_scalar(loc_i[:, :], Ki[:, :], 13, None, ALU.arith_shift_right))
                    f.mark(dve.tensor_scalar(self_i[:, :], Ki[:, :], 12, 1, ALU.arith_shift_right, ALU.bitwise_and))
                    f.then(dve.tensor_scalar(src_i[:, :], Ki[:, :], NTOK - 1, None, ALU.bitwise_and))
                    dve.sem_inc(idx_s, 1)
                    f.mark(dve.tensor_copy(loc[:, :], loc_i[:, :]))
                    f.then(dve.tensor_tensor(selfm[:, :], self_i[:, :], valid[:, :], ALU.mult))
                    f.mark(dve.tensor_tensor(cont[:, 1:LIST], loc[:, 1:LIST], loc[:, 0:LIST - 1], ALU.is_equal))
                    f.then(dve.tensor_tensor(contb[:, 0:LIST - 1], loc[:, 0:LIST - 1], loc[:, 1:LIST], ALU.is_equal))
                    f.mark(dve.tensor_scalar(mc[:, :], cont[:, :], 1.0, BIG, ALU.subtract, ALU.mult))
                    f.mark(dve.tensor_scalar(mb[:, :], contb[:, :], 1.0, BIG, ALU.subtract, ALU.mult))
                    f.then(dve.tensor_tensor(ge[:, :, :], K[:, :].unsqueeze(1).to_broadcast([P, NC, LIST]),
                                             thr[:, :].unsqueeze(2).to_broadcast([P, NC, LIST]), ALU.is_ge))
                    f.then(dve.tensor_reduce(endf[:, :], ge[:, :, :], AX_X, ALU.add))
                    f.then(dve.scalar_tensor_tensor(out=endf[:, :], in0=endf[:, :], scalar=-1.0, in1=rowf[:, :],
                                                    op0=ALU.add, op1=ALU.add))
                    f.then(dve.tensor_copy(end_i[:, :], endf[:, :]))
                    f.then(dve.scalar_tensor_tensor(out=valid[:, :], in0=selfm[:, :], scalar=-1.0, in1=valid[:, :],
                                                    op0=ALU.mult, op1=ALU.add))
                    f.then(dve.scalar_tensor_tensor(out=valid[:, :], in0=selfm[:, :], scalar=first[:, 0:1],
                                                    in1=valid[:, :], op0=ALU.mult, op1=ALU.add))
                    f.then(dve.memset(first[:, :], 0.0))
                    dve.wait_ge(gat, m * 256 + k * (16 * LIST))
                    f.mark(dve.tensor_copy(AS[:, :, :], Gt[:, :, 16:20].rearrange("p n h -> p h n")))
                    f.then(dve.tensor_tensor(Wt[:, :, :], Gt[:, :, 20:24].rearrange("p n h -> p h n"),
                                             selfm[:, :].unsqueeze(1).to_broadcast([P, HEADS, LIST]), ALU.mult))
                    for h in range(HEADS):
                        f.mark(dve.tensor_tensor_scan(AD[:, h, :], cont[:, :], Wt[:, h, :], 0.0, ALU.mult, ALU.add))
                        f.mark(dve.tensor_tensor_scan(MF[:, h, :], mc[:, :], AS[:, h, :], -BIG, ALU.add, ALU.max))
                        f.mark(dve.tensor_tensor_scan(MB[:, h, ::-1], mb[:, ::-1], AS[:, h, ::-1], -BIG, ALU.add,
                                                      ALU.max))
                    f.wait()
                    f.then(dve.tensor_tensor(MF[:, :, :], MF[:, :, :], MB[:, :, :], ALU.max))
                    f.mark(dve.tensor_copy(R[:, :, 20:24].rearrange("p n h -> p h n"), MF[:, :, :]))
                    f.mark(dve.tensor_tensor(AS[:, :, :], AS[:, :, :], AD[:, :, :], ALU.add))
                    f.then(dve.tensor_tensor(MB[:, :, :], MF[:, :, :], AD[:, :, :], ALU.add))
                    f.mark(dve.scalar_tensor_tensor(out=AS[:, :, :], in0=AS[:, :, :], scalar=0.2, in1=AS[:, :, :],
                                                    op0=ALU.mult, op1=ALU.max))
                    f.then(dve.scalar_tensor_tensor(out=MB[:, :, :], in0=MB[:, :, :], scalar=0.2, in1=MB[:, :, :],
                                                    op0=ALU.mult, op1=ALU.max))
                    f.then(dve.tensor_tensor(Wt[:, :, :], AS[:, :, :], MB[:, :, :], ALU.subtract))
                    dve.sem_inc(dif_s, 1)
                    dve.wait_ge(w_s, k + 1)
                    f.then(dve.tensor_tensor(Wt[:, :, :], Wt[:, :, :],
                                             valid[:, :].unsqueeze(1).to_broadcast([P, HEADS, LIST]), ALU.mult))
                    for h in range(HEADS):
                        f.mark(dve.tensor_tensor(MSG[:, 4 * h:4 * h + 4, :],
                                                 Gt[:, :, 4 * h:4 * h + 4].rearrange("p n f -> p f n"),
                                                 Wt[:, h:h + 1, :].to_broadcast([P, 4, LIST]), ALU.mult))
                    f.wait()
                    for q in range(16):
                        f.mark(dve.tensor_tensor_scan(R[:, :, q], cont[:, :], MSG[:, q, :], 0.0, ALU.mult, ALU.add))
                    for h in range(HEADS):
                        f.mark(dve.tensor_tensor_scan(R[:, :, 16 + h], cont[:, :], Wt[:, h, :], 0.0, ALU.mult,
                                                      ALU.add))
                    f.wait()
                    dve.sem_inc(rows_s, 1)
                    dve.wait_ge(ends_in, k * (16 * NC) + 16 * NC)
                    f.then(dve.tensor_tensor(m_new[:, :, :], m_run[:, :, :], N[:, :, 20:24], ALU.max))
                    for i, m in enumerate((m_run[:, :, :], N[:, :, 20:24], m_new[:, :, :])):
                        f.mark(dve.tensor_tensor(lr[i][:, :, :], m, G.tab[:, :, 20:24], ALU.add))
                    f.wait()
                    for i in range(3):
                        f.mark(dve.scalar_tensor_tensor(out=lr[i][:, :, :], in0=lr[i][:, :, :], scalar=0.2,
                                                        in1=lr[i][:, :, :], op0=ALU.mult, op1=ALU.max))
                    f.wait()
                    for i in range(2):
                        f.mark(dve.tensor_tensor(zz[:, i, :, :], lr[i][:, :, :], lr[2][:, :, :], ALU.subtract))
                    f.wait()
                    dve.sem_inc(nd_s, 1)
                    f.then(dve.tensor_copy(m_run[:, :, :], m_new[:, :, :]))
                    dve.wait_ge(ne_s, k + 1)
                    f.mark(dve.tensor_tensor(den[:, :, :], den[:, :, :], zz[:, 0, :, :], ALU.mult))
                    f.mark(dve.tensor_tensor(lr[0][:, :, :], N[:, :, 16:20], zz[:, 1, :, :], ALU.mult))
                    f.mark(dve.tensor_tensor(agg[:, :, :].rearrange("p c (h e) -> p c h e", e=4),
                                             agg[:, :, :].rearrange("p c (h e) -> p c h e", e=4),
                                             per_node(zz[:, 0, :, :], 4), ALU.mult))
                    f.then(dve.tensor_tensor(t16[:, :, :].rearrange("p c (h e) -> p c h e", e=4),
                                             N[:, :, 0:16].rearrange("p c (h e) -> p c h e", e=4),
                                             per_node(zz[:, 1, :, :], 4), ALU.mult))
                    f.mark(dve.tensor_tensor(den[:, :, :], den[:, :, :], lr[0][:, :, :], ALU.add))
                    f.then(dve.tensor_tensor(agg[:, :, :], agg[:, :, :], t16[:, :, :], ALU.add))
                    f.close(PER)
                dve.wait_ge(par_in, 64)
                b16 = [P, NC, 16]
                o.then(dve.tensor_scalar(den[:, :, :], den[:, :, :], 1e-16, None, ALU.add))
                o.then(dve.reciprocal(den[:, :, :], den[:, :, :]))
                o.then(dve.tensor_tensor(agg[:, :, :].rearrange("p c (h e) -> p c h e", e=4),
                                         agg[:, :, :].rearrange("p c (h e) -> p c h e", e=4),
                                         per_node(den[:, :, :], 4), ALU.mult))
                o.then(dve.tensor_tensor(agg[:, :, :], agg[:, :, :], gp["bias"][:, :].unsqueeze(1).to_broadcast(b16),
                                         ALU.add))
                o.then(dve.tensor_reduce(s1[:, :], agg[:, :, :], AX_X, ALU.add))
                o.then(dve.scalar_tensor_tensor(out=agg[:, :, :], in0=s1[:, :].unsqueeze(2).to_broadcast(b16),
                                                scalar=-1.0 / 16, in1=agg[:, :, :], op0=ALU.mult, op1=ALU.add))
                dve.sem_inc(sq_a, 1)
                dve.wait_ge(sq_b, 1)
                o.then(dve.tensor_reduce(s2[:, :], t16[:, :, :], AX_X, ALU.add))
                dve.sem_inc(std_a, 1)
                dve.wait_ge(std_b, 1)
                o.then(dve.reciprocal(s1[:, :], s3[:, :]))
                o.then(dve.tensor_tensor(agg[:, :, :], agg[:, :, :], s1[:, :].unsqueeze(2).to_broadcast(b16), ALU.mult))
                o.then(dve.tensor_tensor(agg[:, :, :], agg[:, :, :], gp["gamma"][:, :].unsqueeze(1).to_broadcast(b16),
                                         ALU.mult))
                o.then(dve.tensor_tensor(agg[:, :, :], agg[:, :, :], gp["beta"][:, :].unsqueeze(1).to_broadcast(b16),
                                         ALU.add))
                o.then(dve.tensor_reduce(sc[:, :, :], agg[:, :, :].rearrange("p c (h e) -> p c e h", e=4), AX_X,
                                         ALU.add))
                o.then(dve.tensor_scalar(sc[:, :, :], sc[:, :, :], 1.0 / HEADS, None, ALU.mult))
                other = sc[:, :, :].unsqueeze(2).to_broadcast([P, NC, EXP1, EXP1])
                mine = sc[:, :, :].unsqueeze(3).to_broadcast([P, NC, EXP1, EXP1])
                o.mark(dve.tensor_tensor(p1[:, :, :, :], other, mine, ALU.is_gt))
                o.mark(dve.tensor_tensor(p2[:, :, :, :], other, mine, ALU.is_equal))
                o.then(dve.tensor_reduce(s1[:, :], sc[:, :, :], AX_X, ALU.max))
                o.mark(dve.tensor_tensor(p2[:, :, :, :].rearrange("p c e f -> p c (e f)"),
                                         p2[:, :, :, :].rearrange("p c e f -> p c (e f)"),
                                         before[:, :].unsqueeze(1).to_broadcast(b16), ALU.mult))
                o.then(dve.tensor_tensor(sc[:, :, :], sc[:, :, :], s1[:, :].unsqueeze(2).to_broadcast([P, NC, EXP1]),
                                         ALU.subtract))
                dve.sem_inc(ex_a, 1)
                o.then(dve.tensor_tensor(p1[:, :, :, :], p1[:, :, :, :], p2[:, :, :, :], ALU.add))
                o.then(dve.tensor_reduce(rk[:, :, :], p1[:, :, :, :], AX_X, ALU.add))
                dve.wait_ge(ex_b, 1)
                o.then(dve.scalar_tensor_tensor(out=ex[:, :, :], in0=rk[:, :, :], scalar=2.0, in1=ex[:, :, :],
                                                op0=ALU.is_lt, op1=ALU.mult))
                o.then(dve.tensor_reduce(s2[:, :], ex[:, :, :], AX_X, ALU.add))
                o.then(dve.reciprocal(s2[:, :], s2[:, :]))
                o.then(dve.tensor_tensor(G.gates[:, :, :], ex[:, :, :],
                                         s2[:, :].unsqueeze(2).to_broadcast([P, NC, EXP1]), ALU.mult))


def combine(nc, G, A):
    with stage(nc, G) as st:
        R = st.sb("mix", [P, NC, D])
        Y = st.sb("mix_tmp", [P, NC, D])
        own, out_s = st.sem("mix_dve_steps"), st.sem("out_written")
        ln = LayerNorm(st, "ln4", R, G.tm, Y)
        with nc.Block() as block:
            @block.vector
            def _(dve):
                o = Steps(dve, own)
                for e in range(EXP1):
                    g = G.gates[:, :, e:e + 1].to_broadcast([P, NC, D])
                    o.then(dve.tensor_tensor(Y[:, :, :], G.xo[:, :, e * D:(e + 1) * D], g, ALU.mult))
                    o.then(dve.tensor_tensor(R[:, :, :], Y[:, :, :], G.tm[:, :, :] if e == 0 else R[:, :, :], ALU.add))
                ln.vector(dve)

            @block.scalar
            def _(act):
                ln.scalar(act, G.ln_eps[:, 0:1])

            @block.sync
            def _(sp):
                for g in range(LG):
                    sp.wait_ge(ln.normed, g + 1)
                    sp.dma_start(A["out"].rearrange("b t d -> (b t) d").rearrange("(c p) d -> p c d", p=P)[
                        :, g * LC:(g + 1) * LC, :], G.tm[:, g * LC:(g + 1) * LC, :]).then_inc(out_s, 16)
                sp.wait_ge(out_s, 16 * LG)


def program(nc, A):
    A["slots"] = nc.dram_tensor("bin_slots", [NSLOT, 1], F32).ap()
    A["table"] = nc.dram_tensor("node_table", [NTOK, ROW], F32).ap()
    A["ends"] = nc.dram_tensor("segment_table", [P * LIST, ROW], F32).ap()
    G = Shared()
    with stage(nc, G) as st:
        G.bank = [st.enter_context(nc.psum_tensor(f"bank{i}", [P, TILE], F32)) for i in range(8)]
        G.hT = st.sb("h_features", [D, NTOK])
        G.tm = st.sb("h_tokens", [P, NC, D])
        G.ident = st.sb("ident", [P, P])
        G.ln_eps = st.sb("ln_eps", [P, 1])
        G.rounds = st.sb("sort_rounds", [P, 1], I32)
        G.passes = st.sb("graph_passes", [P, 1], I32)
        G.groups = st.sb("first_groups", [P, 1], I32)
        G.n_bin = st.sb("n_bin", [P, 1])
        G.n_far = st.sb("n_far", [P, NC])
        tokens(nc, G, A)
        attention0(nc, G, A)
        experts0(nc, G, A)
        attention1(nc, G, A)
        fresh_semaphores(nc, G)
        with stage(nc, G) as keys:
            G.keys = keys.sb("edge_keys", [P, EW])
            graph_counts(nc, G, A)
            graph_sort(nc, G, A)
        graph_fill(nc, G, A)
        G.tab = st.sb("node_rows_own", [P, NC, ROW])
        G.far = st.sb("far_row", [P, ROW])
        G.gates = st.sb("gates", [P, NC, EXP1])
        G.xo = st.sb("expert_out", [P, NC, EXP1 * D])
        experts1(nc, G, A)
        graph_attention(nc, G, A)
        combine(nc, G, A)


_INS = ["x", "L0_tok_W", "L0_tok_b", "L0_attn_Q", "L0_attn_K", "L0_attn_VT", "L0_ffn_Wr", "L0_ffn_br", "L0_ffn_W1",
        "L0_ffn_W2", "L0_ffn_Wo", "L0_ffn_bo", "L1_attn_DxT", "L1_attn_DyT", "L1_attn_ET", "L1_ffn_W_gat",
        "L1_ffn_att_src", "L1_ffn_att_dst", "L1_ffn_b_gat", "L1_ffn_ln_gamma", "L1_ffn_ln_beta", "L1_ffn_W1",
        "L1_ffn_b1T", "L1_ffn_W2", "L1_ffn_b2", "L1_ffn_edge_index"]
_BN = ["b1", "g1", "be1", "m1", "v1", "b2", "g2", "be2", "m2", "v2"]


def layouts(inputs):
    a = {k: np.asarray(v) for k, v in inputs.items()}
    for name in ("L0_attn_V", "L1_attn_Dx", "L1_attn_Dy", "L1_attn_E", "L1_ffn_b1"):
        a[name + "T"] = np.ascontiguousarray(a[name].T)
    for n in _BN:
        a["bn_" + n] = np.ascontiguousarray(a["L0_ffn_" + n].reshape(NPAIR, 2 * 64).T)
    return a


def kernel(**inputs):
    import concourse.bacc as bacc
    from concourse.bass_utils import run_bass_kernel_spmd

    nc = bacc.Bacc("TRN2", target_bir_lowering=False, num_devices=1)
    consts = shape_constants()
    data = layouts(inputs)
    arrays, A = {}, {}

    def declare(name, a):
        arrays[f"in_{name}"] = np.ascontiguousarray(a)
        return nc.dram_tensor(f"in_{name}", a.shape, mybir.dt.from_np(a.dtype), kind="ExternalInput").ap()

    for name in _INS:
        A[name] = declare(name, data[name])
    for name in _BN:
        A["bn_" + name] = declare("bn_" + name, data["bn_" + name])
    for name in consts:
        A[name] = declare(name, consts[name])
    A["out"] = nc.dram_tensor("out_dram", (B, T, D), F32, kind="ExternalOutput").ap()
    program(nc, A)
    r = run_bass_kernel_spmd(nc, [arrays], core_ids=[0])
    return r.results[0]["out_dram"]
```

```python
from contextlib import ExitStack

import numpy as np

import concourse.bass as bass
from concourse import mybir

ALU = mybir.AluOpType
ACT = mybir.ActivationFunctionType
F32 = mybir.dt.float32
BF16 = mybir.dt.bfloat16
I32 = mybir.dt.int32
AX_X = mybir.AxisListType.X

B, IMG = 64, 84
T, D = 64, 64
NTOK = B * T
P = 128
NC = NTOK // P
TILE = 512
NT = NTOK // TILE
CPT = TILE // P
EXP0, NPAIR = 8, 4
NSTATE, NH2 = 256, 2
EXP1, HID1 = 4, 128
HEADS = 4
LN_EPS, BN_EPS, L1_EPS, DECAY = 1e-5, 1e-3, 1e-12, 0.97
NMAP, NOP = 7, 4
NEDGE = 262144
EW = NEDGE // P
FAR = NTOK - 1
SPREAD = 512
BIN_BITS = 18
NSLOT = P << BIN_BITS
SEG = 64
CAND = EW // SEG * 8 + 8
SORTED = 256
SHIFT = SORTED.bit_length() - 1
RB = SORTED // 16
EARLY_SORT = 20
EARLY = 4
PART = 256
ROW = 24
BIG = 1e30
MAP_OPS = [(0, 0), (1, 0), (0, 1), (1, 1), (3, 2), (2, 3), (3, 3)]


def resize_matrix(n):
    inv = n / 8.0
    kernel = max(inv, 1.0)
    sample = (np.arange(8) + 0.5) * inv - 0.5
    w = np.maximum(0.0, 1.0 - np.abs(sample[:, None] - np.arange(n)[None, :]) / kernel)
    return w / w.sum(axis=1, keepdims=True)


def haar(n, sign):
    m = np.zeros((n // 2, n))
    for k in range(n // 2):
        m[k, 2 * k], m[k, 2 * k + 1] = 1.0, sign
    return m * 0.7071067811865476


def haar_operators():
    half = IMG // 2
    low = haar(IMG, 1.0)
    return np.stack([resize_matrix(half // 2) @ haar(half, 1.0) @ low,
                     resize_matrix(half // 2) @ haar(half, -1.0) @ low,
                     resize_matrix(half) @ low,
                     resize_matrix(half) @ haar(IMG, -1.0)])


def shape_constants():
    ops = haar_operators()
    rows = ops.transpose(2, 0, 1).reshape(IMG, NOP * 8)
    cols = np.zeros((NMAP, 8, NOP, IMG))
    for m, (v, w) in enumerate(MAP_OPS):
        for j in range(8):
            cols[m, j, v] = ops[w, j]
    same = np.arange(P)[:, None] // T == np.arange(P)[None, :] // T
    t = np.arange(P) % T
    gap = t[None, :] - 1 - t[:, None]
    decay = np.where(same & (gap >= 0), DECAY ** np.maximum(gap, 0), 0.0)
    pick = np.zeros((EXP0, NPAIR, P))
    for e in range(EXP0):
        pick[e, e // 2, (e % 2) * 64:(e % 2) * 64 + 64] = 1.0
    return {
        "c_rows": rows.astype(np.float32),
        "c_cols": cols.reshape(NMAP, 8 * NOP, IMG).astype(np.float32),
        "c_other": np.where(same, 0.0, -1e30).astype(np.float32),
        "c_decay": decay.astype(np.float32),
        "c_pick": pick.astype(np.float32),
        "c_ident": np.eye(P, dtype=np.float32),
        "c_later": np.triu(np.ones((P, P), np.float32), 1),
        "c_hi_parity": (np.arange(64)[:, None] % 2 == np.arange(2)[None, :]).astype(np.float32),
        "c_hi_half": (np.arange(64)[:, None] // 2 == np.arange(NC)[None, :]).astype(np.float32),
        "c_before": np.tile((np.arange(4)[None, :] < np.arange(4)[:, None]).astype(np.float32).reshape(1, 16), (P, 1)),
    }


class Steps:

    def __init__(self, eng, sem, base=0):
        self.eng, self.sem, self.base, self.n = eng, sem, base, 0

    def then(self, ins):
        self.mark(ins)
        self.wait()

    def wait(self):
        self.eng.wait_ge(self.sem, self.base + self.n)

    def close(self, per):
        assert self.n < per
        self.wait()
        self.eng.sem_inc(self.sem, per - self.n)

    def mark(self, ins):
        ins.then_inc(self.sem, 1)
        self.n += 1
        return self.n


class Shared:

    def __init__(self):
        self.semaphores = []


def stage(nc, G):
    st = ExitStack()
    st.sb = lambda name, shape, dt=F32: st.enter_context(nc.sbuf_tensor(name, shape, dt))
    st.sem = lambda name: new_semaphore(nc, G, name)
    return st


def new_semaphore(nc, G, name):
    G.semaphores.append(nc.alloc_semaphore(name=name))
    return G.semaphores[-1]


def fresh_semaphores(nc, G):
    nc.all_engine_barrier()
    nc.clear_and_free_semaphores(G.semaphores)
    nc.all_engine_barrier()
    G.semaphores = []


LG = 4
LC = NC // LG


class LayerNorm:

    def __init__(self, st, name, x, out, sq, xc=None):
        self.src, self.out, self.sq = x, out, sq
        self.x = x if xc is None else xc
        self.sum = st.sb(name + "_sum", [P, NC])
        self.var = st.sb(name + "_var", [P, NC])
        self.centred = st.sem(name + "_centred")
        self.squared = st.sem(name + "_squared")
        self.var_ready = st.sem(name + "_var_ready")
        self.std_ready = st.sem(name + "_std_ready")
        self.normed = st.sem(name + "_normed")
        self.own = st.sem(name + "_dve_steps")

    def vector(self, dve):
        self.centre(dve)
        self.normalise(dve)

    def centre(self, dve):
        self.steps = own = Steps(dve, self.own)
        for g in range(LG):
            c = slice(g * LC, (g + 1) * LC)
            own.then(dve.tensor_reduce(self.sum[:, c], self.src[:, c, :], AX_X, ALU.add))
            dve.scalar_tensor_tensor(out=self.x[:, c, :], in0=self.sum[:, c].unsqueeze(2).to_broadcast([P, LC, D]),
                                     scalar=-1.0 / D, in1=self.src[:, c, :], op0=ALU.mult,
                                     op1=ALU.add).then_inc(self.centred, 1)

    def normalise(self, dve):
        own = self.steps
        for g in range(LG):
            c = slice(g * LC, (g + 1) * LC)
            dve.wait_ge(self.squared, g + 1)
            dve.tensor_reduce(self.var[:, c], self.sq[:, c, :], AX_X, ALU.add).then_inc(self.var_ready, 1)
        dve.wait_ge(self.std_ready, 1)
        own.then(dve.reciprocal(self.sum[:, :], self.var[:, :]))
        for g in range(LG):
            c = slice(g * LC, (g + 1) * LC)
            dve.tensor_tensor(self.out[:, c, :], self.x[:, c, :],
                              self.sum[:, c].unsqueeze(2).to_broadcast([P, LC, D]),
                              ALU.mult).then_inc(self.normed, 1)

    def scalar(self, act, eps):
        for g in range(LG):
            c = slice(g * LC, (g + 1) * LC)
            act.wait_ge(self.centred, g + 1)
            act.activation(self.sq[:, c, :], self.x[:, c, :], ACT.Square).then_inc(self.squared, 1)
        act.wait_ge(self.var_ready, LG)
        act.activation(self.var[:, :], self.var[:, :], ACT.Sqrt, bias=eps, scale=1.0 / D).then_inc(self.std_ready, 1)


class ToFeatures:

    def __init__(self, st, name, src, dst, ready, ready_per_group):
        self.src, self.dst, self.ready, self.per = src, dst, ready, ready_per_group
        self.turned = st.sem(name + "_turned")
        self.kept_act = st.sem(name + "_kept_by_act")
        self.kept_dve = st.sem(name + "_kept_by_dve")

    def tensor(self, pe, G):
        for k in range(NT):
            if self.per:
                pe.wait_ge(self.ready, k * CPT // LC + 1)
            for i in range(CPT):
                ins = pe.transpose(G.bank[k][0:D, i * P:(i + 1) * P], self.src[:, k * CPT + i, :], G.ident[:, :])
            ins.then_inc(self.turned, 1)

    def scalar(self, act, G):
        for k in range(0, NT, 2):
            act.wait_ge(self.turned, k + 1)
            act.copy(self.dst[:, k * TILE:(k + 1) * TILE], G.bank[k][0:D, :]).then_inc(self.kept_act, 1)

    def vector(self, dve, G):
        for k in range(1, NT, 2):
            dve.wait_ge(self.turned, k + 1)
            dve.tensor_copy(self.dst[:, k * TILE:(k + 1) * TILE], G.bank[k][0:D, :]).then_inc(self.kept_dve, 1)

    def wait(self, eng):
        eng.wait_ge(self.kept_act, NT // 2)
        eng.wait_ge(self.kept_dve, NT // 2)


def tokens_and_counts(nc, G, A):
    with stage(nc, G) as st:
        X = st.sb("images", [IMG, B, IMG])
        two = st.sb("col_ops_then_rows_done", [IMG, 8 * NOP * IMG])
        cols = two[0:NMAP, :].rearrange("m (q w) -> m q w", w=IMG)
        Y = two[:, 0:NOP * B * 8].rearrange("w (v b i) -> w v b i", v=NOP, b=B)
        rows = st.sb("row_ops", [IMG, NOP * 8])
        Wm = st.sb("embed_w", [NMAP, D])
        bias = st.sb("embed_b", [D, 1])
        Wj = st.sb("col_weights", [IMG, 8 * NOP, D])
        hi = st.sb("dst_hi", [P, EW], BF16)
        lo = st.sb("dst_lo", [P, EW], BF16)
        W = SPREAD // 2
        hot = [st.sb(f"dst_one_hot{u}", [P, P, W], BF16) for u in range(2)]
        spare = hot[1][:, :, :].rearrange("p v w -> p (v w)")
        e_i = spare[:, 0:4 * EW].bitcast(I32).rearrange("p (s w) -> p s w", s=2)
        srcf, dstf, tmp = (spare[:, (4 + 2 * i) * EW:(6 + 2 * i) * EW].bitcast(F32) for i in range(3))
        bin_i, loc_i = (spare[:, (10 + 2 * i) * EW:(12 + 2 * i) * EW].bitcast(I32) for i in range(2))
        zero = st.sb("zero_weights", [P, P], BF16)
        par = st.sb("hi_parity", [64, 2])
        half = st.sb("hi_half", [64, NC])
        split = st.sb("hist_split", [64, 2, 64])
        near_n = st.sb("near_count", [P, 1])
        near_max = st.sb("near_max", [P, 1])
        r_i = st.sb("rounds_tmp", [P, 1], I32)
        img_in = [st.sem(f"images_in{i}") for i in range(4)]
        par_in = st.sem("embed_params_in")
        rows_mm = st.sem("rows_mm")
        wj_mm = st.sem("col_weights_mm")
        y_kept = st.sem("rows_kept")
        wj_kept = st.sem("col_weights_kept")
        h_mm = st.sem("embed_mm")
        h_act = st.sem("embed_kept_act")
        e_in, c_in, own = st.sem("edges_in"), st.sem("hist_consts_in"), st.sem("counts_dve_steps")
        near_s, max_s = st.sem("near_counted"), st.sem("near_max_ready")
        hot_s, used_s, split_s, far_mm = (st.sem("one_hots"), st.sem("one_hots_used"), st.sem("hist_split_ready"),
                                          st.sem("far_mm"))
        zero_s = st.sem("zero_weights_ready")
        NS = EW // W
        xv = A["x"].rearrange("b o h w -> h (b o) w")
        ev = A["L1_ffn_edge_index"].rearrange("s (p w) -> s p w", p=P)
        with nc.Block() as block:
            @block.sync
            def _(sp):
                sp.dma_start(e_i[:, 0, :], ev[0]).then_inc(e_in, 16)
                sp.dma_start(e_i[:, 1, :], ev[1]).then_inc(e_in, 16)
                sp.dma_start(rows[:, :], A["c_rows"]).then_inc(par_in, 16)
                for i in range(0, 4, 2):
                    sp.dma_start(X[:, 16 * i:16 * i + 16, :], xv[:, 16 * i:16 * i + 16, :]).then_inc(img_in[i], 16)
                sp.dma_start(par[:, :], A["c_hi_parity"]).then_inc(c_in, 16)
                sp.dma_start(half[:, :], A["c_hi_half"]).then_inc(c_in, 16)
                sp.dma_start(G.ident[:, :], A["c_ident"]).then_inc(c_in, 16)

            @block.scalar
            def _(act):
                act.dma_start(cols[:, :, :], A["c_cols"]).then_inc(par_in, 16)
                act.dma_start(Wm[:, :], A["L0_tok_W"]).then_inc(par_in, 16)
                act.dma_start(bias[:, :], A["L0_tok_b"].rearrange("(d o) -> d o", o=1)).then_inc(par_in, 16)
                for i in range(1, 4, 2):
                    act.dma_start(X[:, 16 * i:16 * i + 16, :], xv[:, 16 * i:16 * i + 16, :]).then_inc(img_in[i], 16)
                for k in range(4):
                    act.wait_ge(wj_mm, k + 1)
                    act.copy(Wj[:, 8 * k:8 * k + 8, :], G.bank[4 + k][0:IMG, :]).then_inc(wj_kept, 1)
                for k in range(4):
                    act.wait_ge(rows_mm, k + 1)
                    act.copy(Y[:, :, 16 * k:16 * k + 16, :].rearrange("w v b i -> w b v i"),
                             G.bank[k][0:IMG, :].rearrange("w (b v i) -> w b v i", v=NOP, i=8)).then_inc(y_kept, 1)
                for j in range(8):
                    act.wait_ge(h_mm, j + 1)
                    act.activation(G.hT[:, :].rearrange("d (r j) -> d r j", j=8)[:, :, j], G.bank[j][0:D, :],
                                   ACT.Identity, bias=bias[:, 0:1]).then_inc(h_act, 1)

            @block.gpsimd
            def _(pool):
                pool.wait_ge(near_s, 1)
                pool.partition_all_reduce(near_max[:, :], near_n[:, :], P, bass.bass_isa.ReduceOp.max
                                          ).then_inc(max_s, 1)

            @block.tensor
            def _(pe):
                pe.wait_ge(par_in, 64)
                for k in range(4):
                    for q in range(8 * k, 8 * k + 8):
                        ins = pe.matmul(G.bank[4 + k][0:IMG, (q % 8) * D:(q % 8 + 1) * D], cols[:, q, :], Wm[:, :],
                                        start=True, stop=True)
                    ins.then_inc(wj_mm, 1)
                for k in range(4):
                    pe.wait_ge(img_in[k], 16)
                    for b in range(16):
                        ins = pe.matmul(G.bank[k][0:IMG, b * 32:(b + 1) * 32], X[:, 16 * k + b, :], rows[:, :],
                                        start=True, stop=True)
                    ins.then_inc(rows_mm, 1)
                pe.wait_ge(y_kept, 4)
                pe.wait_ge(wj_kept, 4)
                for j in range(8):
                    for v in range(NOP):
                        ins = pe.matmul(G.bank[j][0:D, :], Wj[:, j * NOP + v, :],
                                        Y[:, v, :, :].rearrange("w b i -> w (b i)"),
                                        start=(v == 0), stop=(v == NOP - 1))
                    ins.then_inc(h_mm, 1)
                pe.wait_ge(zero_s, 1)
                pe.wait_ge(h_act, 2)
                pe.matmul(G.bank[0][:, 0:64], zero[:, :], zero[:, 0:64], start=True, stop=True)
                with pe.Fori(0, NS // 2) as q:
                    for u in range(2):
                        pe.wait_ge(hot_s, q * 2 + (u + 1))
                        for e in range(W):
                            ins = pe.matmul(G.bank[0][:, 0:64], hot[u][:, :, e], hot[u][:, 64:P, e], start=False,
                                            stop=True, skip_group_check=True)
                        ins.then_inc(used_s, 1)
                pe.wait_ge(split_s, 2)
                pe.matmul(G.bank[1][:, 0:NC], split[:, :, :].rearrange("h r l -> h (r l)"), half[:, :], start=True,
                          stop=True).then_inc(far_mm, 1)

            @block.vector
            def _(dve):
                o = Steps(dve, own)
                dve.memset(zero[:, :], 0.0).then_inc(zero_s, 1)
                dve.wait_ge(e_in, 32)
                o.mark(dve.tensor_copy(srcf[:, :], e_i[:, 0, :]))
                o.then(dve.tensor_copy(dstf[:, :], e_i[:, 1, :]))
                o.then(dve.tensor_scalar(tmp[:, :], srcf[:, :], float(FAR), None, ALU.is_lt))
                o.mark(dve.tensor_scalar(bin_i[:, :], e_i[:, 1, :], P - 1, 5, ALU.bitwise_and, ALU.logical_shift_left))
                o.then(dve.tensor_scalar(loc_i[:, :], e_i[:, 1, :], 7, None, ALU.logical_shift_right))
                o.mark(dve.tensor_tensor(bin_i[:, :], bin_i[:, :], loc_i[:, :], ALU.bitwise_or))
                o.mark(dve.tensor_scalar(e_i[:, 0, :], e_i[:, 1, :], 6, None, ALU.logical_shift_right))
                o.then(dve.tensor_scalar(e_i[:, 1, :], e_i[:, 1, :], 63, None, ALU.bitwise_and))
                o.mark(dve.scalar_tensor_tensor(out=hi[:, :], in0=tmp[:, :], scalar=256.0, in1=e_i[:, 0, :],
                                                op0=ALU.mult, op1=ALU.add))
                o.then(dve.tensor_copy(lo[:, :], e_i[:, 1, :]))
                o.then(dve.scalar_tensor_tensor(out=tmp[:, :], in0=dstf[:, :], scalar=float(NTOK), in1=tmp[:, :],
                                                op0=ALU.is_lt, op1=ALU.mult))
                dve.tensor_reduce(near_n[:, :], tmp[:, :], AX_X, ALU.add).then_inc(near_s, 1)
                o.then(dve.scalar_tensor_tensor(out=srcf[:, :], in0=bin_i[:, :], scalar=float(NTOK), in1=srcf[:, :],
                                                op0=ALU.mult, op1=ALU.add))
                o.then(dve.scalar_tensor_tensor(out=srcf[:, :], in0=srcf[:, :], scalar=1.0, in1=tmp[:, :],
                                                op0=ALU.add, op1=ALU.mult))
                o.then(dve.tensor_scalar(G.keys[:, CAND:CAND + EW], srcf[:, :], -1.0, None, ALU.add))
                dve.wait_ge(max_s, 1)
                o.then(dve.tensor_scalar(near_max[:, :], near_max[:, :], 15.0, 16.0, ALU.add, ALU.max))
                o.then(dve.tensor_copy(r_i[:, :], near_max[:, :]))
                o.then(dve.tensor_scalar(G.rounds[:, :], r_i[:, :], 4, None, ALU.logical_shift_right))
                o.then(dve.tensor_scalar(r_i[:, :], r_i[:, :], SORTED - 16, None, ALU.add))
                o.then(dve.tensor_scalar(G.batches[:, :], r_i[:, :], SHIFT, None, ALU.logical_shift_right))

                def one_hots(u, q):
                    for v in range(64):
                        dve.tensor_scalar(hot[u][:, v, :], hi[:, bass.ds(q * W, W)], float(v), None, ALU.is_equal)
                    for v in range(64):
                        ins = dve.tensor_scalar(hot[u][:, 64 + v, :], lo[:, bass.ds(q * W, W)], float(v), None,
                                                ALU.is_equal)
                    ins.then_inc(hot_s, 1)

                for u in range(2):
                    one_hots(u, u)
                with dve.Fori(1, NS // 2) as q:
                    for u in range(2):
                        dve.wait_ge(used_s, q * 2 + (u - 1))
                        one_hots(u, q * 2 + u)
                dve.wait_ge(used_s, NS)
                dve.wait_ge(c_in, 48)
                for r in range(2):
                    ins = dve.tensor_scalar(split[:, r, :], G.bank[0][0:64, 0:64], par[:, r:r + 1], None, ALU.mult)
                    ins.then_inc(split_s, 1)
                dve.wait_ge(far_mm, 1)
                o.then(dve.tensor_copy(G.n_far[:, :], G.bank[1][:, 0:NC]))


def attention0(nc, G, A):
    with stage(nc, G) as st:
        Qw = st.sb("q_w", [D, D])
        Kw = st.sb("k_w", [D, D])
        IV = st.sb("ident_v", [D, 2 * D])
        GT = st.sb("g_t", [D, D])
        Z = st.sb("z", [D, NTOK])
        HV = st.sb("h_and_v", [P, NC, 2 * D])
        other = st.sb("other_image", [P, P])
        S = st.sb("scores", [P, NC, P])
        ET = st.sb("probs_t", [P, NC, P])
        nmax = st.sb("neg_max", [P, NC])
        rmax = st.sb("row_max", [P, NC])
        rsum = st.sb("row_sum", [P, NC])
        rinv = st.sb("row_inv", [P, NC])
        R = st.sb("attn_sum", [P, NC, D])
        par_in = st.sem("attn0_params_in")
        g_mm = st.sem("g_mm")
        g_kept = st.sem("g_kept")
        z_mm, z_act, z_dve = st.sem("z_mm"), st.sem("z_kept_act"), st.sem("z_kept_dve")
        hv_mm, hv_act, hv_dve = st.sem("hv_mm"), st.sem("hv_kept_act"), st.sem("hv_kept_dve")
        s_mm, s_max, s_neg, s_exp = st.sem("scores_mm"), st.sem("scores_max"), st.sem("scores_neg"), st.sem("probs")
        t_mm, t_act, t_dve = st.sem("probs_turned"), st.sem("probs_t_act"), st.sem("probs_t_dve")
        o_mm = st.sem("attn_out_mm")
        own = st.sem("attn0_dve_steps")
        rinv_s = st.sem("row_inv_ready")
        ln = LayerNorm(st, "ln0", R, G.tm, S[:, 0:NC // 2, :].rearrange("p c (u d) -> p (c u) d", u=2))
        tf = ToFeatures(st, "ln0_turn", G.tm, G.hT, ln.normed, True)
        scat = st.sem("slots_written_0")
        with nc.Block() as block:
            @block.gpsimd
            def _(pool):
                scatter_last_batch(G, A, pool, scat, range(0, EARLY))

            @block.sync
            def _(sp):
                sp.dma_start(Qw[:, :], A["L0_attn_Q"]).then_inc(par_in, 16)
                sp.dma_start(Kw[:, :], A["L0_attn_K"]).then_inc(par_in, 16)
                sp.dma_start(IV[:, 0:D], A["c_ident"][0:D, 0:D]).then_inc(par_in, 16)
                sp.dma_start(IV[:, D:2 * D], A["L0_attn_VT"]).then_inc(par_in, 16)
                sp.dma_start(other[:, :], A["c_other"]).then_inc(par_in, 16)

            @block.tensor
            def _(pe):
                pe.wait_ge(par_in, 80)
                pe.matmul(G.bank[0][0:D, 0:D], Qw[:, :], Kw[:, :], start=True, stop=True).then_inc(g_mm, 1)
                pe.wait_ge(g_kept, 1)
                for k in range(NT):
                    pe.matmul(G.bank[k][0:D, :], GT[:, :], G.hT[:, k * TILE:(k + 1) * TILE],
                              start=True, stop=True).then_inc(z_mm, 1)
                for k in range(NT):
                    pe.wait_ge(z_dve if k % 2 else z_act, k // 2 + 1)
                    for i in range(CPT):
                        c = k * CPT + i
                        ins = pe.matmul(G.bank[k][:, i * P:(i + 1) * P], G.hT[:, c * P:(c + 1) * P], IV[:, :],
                                        start=True, stop=True)
                    ins.then_inc(hv_mm, 1)
                for k in range(NT):
                    pe.wait_ge(hv_dve if k % 2 else hv_act, k // 2 + 1)
                    for i in range(CPT):
                        c = slice((k * CPT + i) * P, (k * CPT + i + 1) * P)
                        ins = pe.matmul(G.bank[k][:, i * P:(i + 1) * P], Z[:, c], G.hT[:, c], start=True, stop=True)
                    ins.then_inc(s_mm, 1)
                for k in range(NT):
                    pe.wait_ge(s_exp, (k + 1) * CPT)
                    for i in range(CPT):
                        ins = pe.transpose(G.bank[k][:, i * P:(i + 1) * P], S[:, k * CPT + i, :], G.ident[:, :])
                    ins.then_inc(t_mm, 1)
                for k in range(4):
                    pe.wait_ge(t_act, k + 1)
                    pe.wait_ge(t_dve, k + 1)
                    for i in range(8):
                        c = 8 * k + i
                        ins = pe.matmul(G.bank[k][:, i * D:(i + 1) * D], ET[:, c, :], HV[:, c, D:2 * D],
                                        start=True, stop=True)
                    ins.then_inc(o_mm, 1)
                tf.tensor(pe, G)

            @block.scalar
            def _(act):
                for k in range(0, NT, 2):
                    act.wait_ge(z_mm, k + 1)
                    act.copy(Z[:, k * TILE:(k + 1) * TILE], G.bank[k][0:D, :]).then_inc(z_act, 1)
                for k in range(0, NT, 2):
                    act.wait_ge(hv_mm, k + 1)
                    act.copy(HV[:, k * CPT:(k + 1) * CPT, :], G.bank[k][:, :]).then_inc(hv_act, 1)
                for k in range(NT):
                    act.wait_ge(s_neg, k + 1)
                    for c in range(k * CPT, (k + 1) * CPT):
                        act.activation(S[:, c, :], S[:, c, :], ACT.Exp, bias=nmax[:, c:c + 1],
                                       accum_out=rsum[:, c:c + 1]).then_inc(s_exp, 1)
                for k in range(0, NT, 2):
                    act.wait_ge(t_mm, k + 1)
                    act.copy(ET[:, k * CPT:(k + 1) * CPT, :], G.bank[k][:, :]).then_inc(t_act, 1)
                ln.scalar(act, G.ln_eps[:, 0:1])
                tf.scalar(act, G)

            @block.vector
            def _(dve):
                o = Steps(dve, own)
                dve.memset(G.ln_eps[:, :], LN_EPS)
                dve.wait_ge(g_mm, 1)
                dve.tensor_copy(GT[:, :], G.bank[0][0:D, 0:D]).then_inc(g_kept, 1)
                for k in range(1, NT, 2):
                    dve.wait_ge(z_mm, k + 1)
                    dve.tensor_copy(Z[:, k * TILE:(k + 1) * TILE], G.bank[k][0:D, :]).then_inc(z_dve, 1)
                for k in range(1, NT, 2):
                    dve.wait_ge(hv_mm, k + 1)
                    dve.tensor_copy(HV[:, k * CPT:(k + 1) * CPT, :], G.bank[k][:, :]).then_inc(hv_dve, 1)
                dve.wait_ge(par_in, 80)
                for k in range(NT):
                    dve.wait_ge(s_mm, k + 1)
                    for i in range(CPT):
                        c = k * CPT + i
                        ins = dve.tensor_tensor_reduce(out=S[:, c, :], in0=G.bank[k][:, i * P:(i + 1) * P],
                                                       in1=other[:, :], scale=1.0, scalar=-3e38, op0=ALU.add,
                                                       op1=ALU.max, accum_out=rmax[:, c:c + 1])
                        ins.then_inc(s_max, 1)
                    dve.wait_ge(s_max, (k + 1) * CPT)
                    dve.tensor_scalar(nmax[:, k * CPT:(k + 1) * CPT], rmax[:, k * CPT:(k + 1) * CPT], -1.0, None,
                                      ALU.mult).then_inc(s_neg, 1)
                for k in range(1, NT, 2):
                    dve.wait_ge(t_mm, k + 1)
                    dve.tensor_copy(ET[:, k * CPT:(k + 1) * CPT, :], G.bank[k][:, :]).then_inc(t_dve, 1)
                dve.wait_ge(s_exp, NC)
                o.then(dve.reciprocal(rinv[:, :], rsum[:, :]))
                for k in range(4):
                    c = slice(8 * k, 8 * k + 8)
                    dve.wait_ge(o_mm, k + 1)
                    o.then(dve.tensor_tensor(R[:, c, :], G.bank[k][:, :].rearrange("p (c d) -> p c d", d=D),
                                             rinv[:, c].unsqueeze(2).to_broadcast([P, 8, D]), ALU.mult))
                    o.then(dve.tensor_tensor(R[:, c, :], R[:, c, :], HV[:, c, 0:D], ALU.add))
                ln.vector(dve)
                tf.vector(dve, G)


def experts0(nc, G, A):
    with stage(nc, G) as st:
        W1 = st.sb("e0_w1", [D, NPAIR, P])
        W2 = st.sb("e0_w2", [P, NPAIR, P])
        Wo = st.sb("e0_wo", [P, NPAIR, D])
        bo = st.sb("e0_bo", [EXP0, D])
        Wr = st.sb("e0_wr", [D, EXP0])
        br = st.sb("e0_br", [1, EXP0])
        ones = st.sb("e0_ones", [1, P])
        pick = st.sb("e0_pick", [EXP0, NPAIR, P])
        par = {n: st.sb("e0_" + n, [P, NPAIR]) for n in
               ("b1", "g1", "be1", "m1", "v1", "b2", "g2", "be2", "m2", "v2", "A1", "B1", "A2", "B2", "t1", "t2")}
        feat = st.sb("e0_feat", [D, 2, T])
        glog = st.sb("e0_gate_logits", [P, EXP0])
        gate = st.sb("e0_gate", [P, EXP0])
        gm = st.sb("e0_gate_max", [P, 1])
        gs = st.sb("e0_gate_sum", [P, 1])
        gi = st.sb("e0_gate_inv", [P, 1])
        gT = st.sb("e0_gate_t", [EXP0, P])
        wrep = st.sb("e0_gate_rows", [P, NPAIR, T])
        bn_eps = st.sb("e0_bn_eps", [P, 1])
        H1 = st.sb("e0_h1", [P, 2, TILE])
        H2 = st.sb("e0_h2", [P, 2, TILE])
        H2w = st.sb("e0_h2w", [P, 2, NPAIR, TILE])
        R = st.sb("e0_sum", [P, NC, D])
        sq = st.sb("e0_sq", [P, NC, D])
        w_in, zero_s, bn_in = st.sem("e0_weights_in"), st.sem("e0_zeroed"), st.sem("e0_bn_in")
        w2_in = st.sem("e0_w2_in")
        own, var_s, std_s, ab_s = st.sem("e0_dve_steps"), st.sem("e0_bn_var"), st.sem("e0_bn_std"), st.sem("e0_bn_fold")
        feat_s, log_mm, neg_s, exp_s = st.sem("e0_feat_s"), st.sem("e0_log_mm"), st.sem("e0_neg"), st.sem("e0_exp")
        gate_s, gT_mm, gT_s, rep_mm, rep_s = (st.sem("e0_gate_s"), st.sem("e0_gt_mm"), st.sem("e0_gt_s"),
                                              st.sem("e0_rep_mm"), st.sem("e0_rep_s"))
        l1_mm, l1_s, l2_mm, l2_s, gw_s, o_mm, o_s = (st.sem("e0_l1_mm"), st.sem("e0_l1_relu"), st.sem("e0_l2_mm"),
                                                     st.sem("e0_l2_relu"), st.sem("e0_gated"), st.sem("e0_out_mm"),
                                                     st.sem("e0_out_kept"))
        ln = LayerNorm(st, "ln1", R, G.tm, sq)
        tf = ToFeatures(st, "ln1_turn", G.tm, G.hT, ln.normed, True)
        scat = st.sem("slots_written_1")
        NW = 6 + 2 * NPAIR
        with nc.Block() as block:
            @block.gpsimd
            def _(pool):
                pool.memset(W2[:, :, :], 0.0).then_inc(zero_s, 1)
                scatter_last_batch(G, A, pool, scat, range(EARLY, RB))

            @block.sync
            def _(sp):
                sp.dma_start(W1[:, :, :].rearrange("d q (e h) -> d (q e) h", e=2),
                             A["L0_ffn_W1"].rearrange("e d h -> d e h")).then_inc(w_in, 16)
                sp.dma_start(Wo[:, :, :], A["L0_ffn_Wo"].rearrange("(q e) h d -> (e h) q d", e=2)).then_inc(w_in, 16)
                sp.dma_start(bo[:, :], A["L0_ffn_bo"]).then_inc(w_in, 16)
                sp.dma_start(Wr[:, :], A["L0_ffn_Wr"]).then_inc(w_in, 16)
                sp.dma_start(br[:, :], A["L0_ffn_br"].rearrange("(o e) -> o e", o=1)).then_inc(w_in, 16)
                sp.dma_start(pick[:, :, :], A["c_pick"]).then_inc(w_in, 16)
                sp.wait_ge(zero_s, 1)
                w2v = A["L0_ffn_W2"].rearrange("(q e) h k -> e h q k", e=2)
                for e in range(2):
                    sp.dma_start(W2[e * D:(e + 1) * D, :, e * D:(e + 1) * D], w2v[e]).then_inc(w2_in, 16)
                for n in ("b1", "g1", "be1", "m1", "v1", "b2", "g2", "be2", "m2", "v2"):
                    sp.dma_start(par[n][:, :], A["bn_" + n]).then_inc(bn_in, 16)

            @block.tensor
            def _(pe):
                pe.wait_ge(w_in, 96)
                pe.wait_ge(feat_s, 2)
                pe.matmul(G.bank[7][:, 0:EXP0], feat[:, :, :].rearrange("d r f -> d (r f)"), Wr[:, :], start=True,
                          stop=False)
                pe.matmul(G.bank[7][:, 0:EXP0], ones[:, :], br[:, :], start=False, stop=True).then_inc(log_mm, 1)
                pe.wait_ge(gate_s, 1)
                pe.transpose(G.bank[6][0:EXP0, 0:P], gate[:, :], G.ident[:, :]).then_inc(gT_mm, 1)
                pe.wait_ge(gT_s, 1)
                for q in range(NPAIR):
                    ins = pe.matmul(G.bank[7][:, 64 + q * T:64 + (q + 1) * T], pick[:, q, :], gT[:, 0:T], start=True,
                                    stop=True)
                ins.then_inc(rep_mm, 1)
                pe.wait_ge(w2_in, 32)

                def layer1(n):
                    k, q = n // NPAIR, n % NPAIR
                    if n >= 2:
                        pe.wait_ge(l1_s, n - 1)
                    pe.matmul(G.bank[n % 2][:, :], W1[:, q, :], G.hT[:, k * TILE:(k + 1) * TILE], start=True,
                              stop=True).then_inc(l1_mm, 1)

                def layer2(n):
                    pe.wait_ge(l1_s, n + 1)
                    if n >= 2:
                        pe.wait_ge(l2_s, n - 1)
                    pe.matmul(G.bank[2 + n % 2][:, :], W2[:, n % NPAIR, :], H1[:, n % 2, :], start=True,
                              stop=True).then_inc(l2_mm, 1)

                def out(k):
                    pe.wait_ge(gw_s, NPAIR * (k + 1))
                    if k >= 2:
                        pe.wait_ge(o_s, k - 1)
                    for i in range(CPT):
                        to = G.bank[4 + k % 2][:, i * D:(i + 1) * D]
                        for q in range(NPAIR):
                            pe.matmul(to, H2w[:, k % 2, q, i * P:(i + 1) * P], Wo[:, q, :], start=(q == 0), stop=False)
                        ins = pe.matmul(to, gT[:, :], bo[:, :], start=False, stop=True)
                    ins.then_inc(o_mm, 1)

                N = NT * NPAIR
                for n in range(N + 1):
                    if n < N:
                        layer1(n)
                    if n >= 1:
                        layer2(n - 1)
                    if n >= 3 and (n - 3) % NPAIR == 0 and n > 3:
                        out((n - 3) // NPAIR - 1)
                out(NT - 1)
                tf.tensor(pe, G)

            @block.scalar
            def _(act):
                for i in (1, 2):
                    act.wait_ge(bn_in, 160)
                    act.wait_ge(var_s, 1)
                    act.activation(par[f"t{i}"][:, :], par[f"v{i}"][:, :], ACT.Sqrt,
                                   bias=bn_eps[:, 0:1]).then_inc(std_s, 1)
                act.wait_ge(neg_s, 1)
                act.activation(gate[:, :], glog[:, :], ACT.Exp, bias=gm[:, 0:1], accum_out=gs[:, 0:1]
                               ).then_inc(exp_s, 1)
                act.wait_ge(ab_s, 2)
                N = NT * NPAIR
                for n in range(N + 1):
                    if n < N:
                        act.wait_ge(l1_mm, n + 1)
                        if n >= 2:
                            act.wait_ge(l2_mm, n - 1)
                        act.activation(H1[:, n % 2, :], G.bank[n % 2][:, :], ACT.Relu, bias=par["B1"][:, n % 4:n % 4 + 1],
                                       scale=par["A1"][:, n % 4:n % 4 + 1]).then_inc(l1_s, 1)
                    if n >= 1:
                        m = n - 1
                        act.wait_ge(l2_mm, m + 1)
                        if m >= 2:
                            act.wait_ge(gw_s, m - 1)
                        act.activation(H2[:, m % 2, :], G.bank[2 + m % 2][:, :], ACT.Relu,
                                       bias=par["B2"][:, m % 4:m % 4 + 1],
                                       scale=par["A2"][:, m % 4:m % 4 + 1]).then_inc(l2_s, 1)
                ln.scalar(act, G.ln_eps[:, 0:1])
                tf.scalar(act, G)

            def residual(dve, k):
                dve.wait_ge(o_mm, k + 1)
                c = slice(k * CPT, (k + 1) * CPT)
                dve.tensor_tensor(R[:, c, :], G.bank[4 + k % 2][:, 0:CPT * D].rearrange("p (c d) -> p c d", d=D),
                                  G.tm[:, c, :], ALU.add).then_inc(o_s, 1)

            @block.vector
            def _(dve):
                o = Steps(dve, own)
                dve.memset(bn_eps[:, :], BN_EPS).then_inc(var_s, 1)
                dve.memset(ones[:, :], 1.0).then_inc(feat_s, 1)
                o.then(dve.tensor_reduce(feat[:, 0, :], G.hT[:, :].rearrange("d (b f) -> d f b", f=T), AX_X, ALU.add))
                o.then(dve.tensor_scalar(feat[:, 0, :], feat[:, 0, :], 1.0 / B, None, ALU.mult))
                dve.tensor_copy(feat[:, 1, :], feat[:, 0, :]).then_inc(feat_s, 1)
                dve.wait_ge(std_s, 2)
                for i in "12":
                    A_, B_, t_ = par["A" + i], par["B" + i], par["t" + i]
                    o.then(dve.reciprocal(A_[:, :], t_[:, :]))
                    o.then(dve.tensor_tensor(A_[:, :], A_[:, :], par["g" + i][:, :], ALU.mult))
                    o.then(dve.tensor_tensor(B_[:, :], par["b" + i][:, :], par["m" + i][:, :], ALU.subtract))
                    o.then(dve.tensor_tensor(B_[:, :], B_[:, :], A_[:, :], ALU.mult))
                    dve.tensor_tensor(B_[:, :], B_[:, :], par["be" + i][:, :], ALU.add).then_inc(ab_s, 1)
                dve.wait_ge(log_mm, 1)
                o.then(dve.tensor_copy(glog[:, :], G.bank[7][:, 0:EXP0]))
                dve.tensor_reduce(gm[:, :], glog[:, :], AX_X, ALU.max, negate=True).then_inc(neg_s, 1)
                dve.wait_ge(exp_s, 1)
                o.then(dve.reciprocal(gi[:, :], gs[:, :]))
                dve.tensor_scalar(gate[:, :], gate[:, :], gi[:, 0:1], None, ALU.mult).then_inc(gate_s, 1)
                dve.wait_ge(gT_mm, 1)
                dve.tensor_copy(gT[:, :], G.bank[6][0:EXP0, 0:P]).then_inc(gT_s, 1)
                dve.wait_ge(rep_mm, 1)
                o.then(dve.tensor_copy(wrep[:, :, :], G.bank[7][:, 64:64 + NPAIR * T]))
                for n in range(NT * NPAIR):
                    k, q = n // NPAIR, n % NPAIR
                    dve.wait_ge(l2_s, n + 1)
                    if q == 0 and k >= 2:
                        dve.wait_ge(o_mm, k - 1)
                    dve.tensor_tensor(H2w[:, k % 2, q, :].rearrange("p (b f) -> p b f", f=T),
                                      H2[:, n % 2, :].rearrange("p (b f) -> p b f", f=T),
                                      wrep[:, q:q + 1, :].to_broadcast([P, TILE // T, T]), ALU.mult).then_inc(gw_s, 1)
                    if q == NPAIR - 1 and k >= 1:
                        residual(dve, k - 1)
                residual(dve, NT - 1)
                dve.wait_ge(o_s, NT)
                ln.vector(dve)
                tf.vector(dve, G)


def load_list(G, A, eng, k, list_in):
    eng.dma_start(G.raw[:, :], A["slots"].rearrange("(p s) o -> p (s o)", p=P)[:, bass.ds(k * PART, PART)]
                  ).then_inc(list_in, 16)


def sort_list(G, dve, o, rounds, seen=None):
    for j in rounds:
        top = G.sorted[:, 8 * j:8 * j + 8]
        o.then(dve.max(top, G.raw[:, :]))
        if seen is not None:
            dve.sem_inc(seen, 1)
        o.then(dve.match_replace(G.raw[:, :], top, G.raw[:, :], -1.0))
        if seen is not None:
            dve.sem_inc(seen, 1)


def read_list(G, dve, o):
    o.mark(dve.tensor_scalar(G.valid[:, :], G.sorted[:, :], 0.0, None, ALU.is_ge))
    o.then(dve.tensor_copy(G.key_i[:, :], G.sorted[:, :]))
    o.mark(dve.tensor_scalar(G.place_i[:, :], G.key_i[:, :], 13, None, ALU.arith_shift_right))
    o.then(dve.tensor_scalar(G.src_i[:, :], G.key_i[:, :], NTOK - 1, None, ALU.bitwise_and))


def attention1(nc, G, A):
    with stage(nc, G) as st:
        DxT = st.sb("dx_t", [D, NSTATE])
        DyT = st.sb("dy_t", [D, NSTATE])
        Ew = st.sb("e_w", [P, NH2, D])
        decay = st.sb("decay", [P, P])
        ones = st.sb("ones_col", [P, 1])
        X = st.sb("state_x", [P, NH2, NTOK])
        CH = [NC, P]
        tok_sum = st.sb("token_sums", [P, NC])
        u = st.sb("step_sums", CH)
        first = st.sb("step_is_first", CH)
        peak = st.sb("step_peak", CH)
        small = st.sb("step_small", CH)
        gain = st.sb("step_gain", CH)
        grown = st.sb("step_grown", CH)
        total = st.sb("step_total", CH)
        rates = st.sb("step_rates", [NC, 2, P])
        SM = st.sb("masked_scores", [P, NC, P])
        lnv = st.sb("lnv", [P, NC, D])
        xa = st.sb("xa", [P, NC, D])
        xb = st.sb("xb", [P, NC, D])
        par_in = st.sem("attn1_params_in")
        ones_s = st.sem("attn1_ones")
        u_mm, u_s, sum_mm, sum_s = st.sem("u_mm"), st.sem("u_relu"), st.sem("sum_mm"), st.sem("sum_kept")
        own, x_s = st.sem("attn1_dve_steps"), st.sem("state_x_ready")
        list_in, turn_mm, rate_s, spread_mm = (st.sem("first_list_in"), st.sem("sums_turned"), st.sem("rates_ready"),
                                               st.sem("rates_spread"))
        st_mm, sm_s, a_mm, a_s = st.sem("st_mm"), st.sem("sm_masked"), st.sem("a_mm"), st.sem("a_kept")
        y_mm, y_s, v_mm, v_s = st.sem("y_mm"), st.sem("y_s"), st.sem("v_mm"), st.sem("v_kept")
        lnv_n = LayerNorm(st, "lnv_n", G.tm, lnv, xb, xc=xa)
        lna = LayerNorm(st, "lna_n", xa, xb, lnv)
        lnw = LayerNorm(st, "lnw_n", xa, xb, lnv)
        lnh = LayerNorm(st, "lnh_n", xa, G.tm, lnv)
        ta = ToFeatures(st, "a_turn", xb, G.hT, lna.normed, True)
        th = ToFeatures(st, "ln3_turn", G.tm, G.hT, lnh.normed, True)
        with nc.Block() as block:
            @block.sync
            def _(sp):
                load_list(G, A, sp, 0, list_in)
                sp.dma_start(DxT[:, :], A["L1_attn_DxT"]).then_inc(par_in, 16)
                sp.dma_start(DyT[:, :], A["L1_attn_DyT"]).then_inc(par_in, 16)
                sp.dma_start(Ew[:, :, :], A["L1_attn_ET"].rearrange("(g p) d -> p g d", g=NH2)).then_inc(par_in, 16)
                sp.dma_start(decay[:, :], A["c_decay"]).then_inc(par_in, 16)

            @block.tensor
            def _(pe):
                pe.wait_ge(par_in, 64)
                pe.wait_ge(ones_s, 1)

                def sums(k):
                    pe.wait_ge(u_s, 2 * k + 2)
                    for c in range(k * CPT, (k + 1) * CPT):
                        for g in range(NH2):
                            ins = pe.matmul(G.bank[4][:, c:c + 1], X[:, g, c * P:(c + 1) * P], ones[:, :],
                                            start=(g == 0), stop=(g == NH2 - 1))
                    return ins

                for k in range(NT):
                    for g in range(NH2):
                        n = 2 * k + g
                        if n >= 4:
                            pe.wait_ge(u_s, n - 3)
                        pe.matmul(G.bank[n % 4][:, :], DxT[:, g * P:(g + 1) * P], G.hT[:, k * TILE:(k + 1) * TILE],
                                  start=True, stop=True).then_inc(u_mm, 1)
                    if k:
                        sums(k - 1)
                sums(NT - 1).then_inc(sum_mm, 1)
                pe.wait_ge(sum_s, 1)
                pe.transpose(G.bank[5][0:NC, 0:P], tok_sum[:, :], G.ident[:, :]).then_inc(turn_mm, 1)
                pe.wait_ge(rate_s, 1)

                def spread(k):
                    for i in range(CPT):
                        c = k * CPT + i
                        ins = pe.matmul(G.bank[2 * (k % 2) + i // 2][:, (i % 2) * 2 * P:(i % 2 + 1) * 2 * P],
                                        G.ident[0:NC, c:c + 1].to_broadcast([NC, P]),
                                        rates[:, :, :].rearrange("c r t -> c (r t)"), start=True, stop=True)
                    ins.then_inc(spread_mm, 1)

                spread(0)
                spread(1)
                for k in range(NT):
                    pe.wait_ge(x_s, k + 1)
                    if k >= 4:
                        pe.wait_ge(sm_s, k - 3)
                    for i in range(CPT):
                        c = slice((k * CPT + i) * P, (k * CPT + i + 1) * P)
                        for g in range(NH2):
                            ins = pe.matmul(G.bank[4 + k % 4][:, i * P:(i + 1) * P], X[:, g, c], X[:, g, c],
                                            start=(g == 0), stop=(g == NH2 - 1))
                    ins.then_inc(st_mm, 1)
                    if k + 2 < NT:
                        spread(k + 2)
                for k in range(4):
                    pe.wait_ge(sm_s, 2 * k + 2)
                    pe.wait_ge(lnv_n.normed, k + 1)
                    for i in range(8):
                        c = 8 * k + i
                        ins = pe.matmul(G.bank[k][:, i * D:(i + 1) * D], SM[:, c, :], lnv[:, c, :], start=True, stop=True)
                    ins.then_inc(a_mm, 1)
                ta.tensor(pe, G)
                for k in range(NT):
                    pe.wait_ge(ta.kept_dve if k % 2 else ta.kept_act, k // 2 + 1)
                    for g in range(NH2):
                        n = 2 * k + g
                        if n == 0:
                            ta.wait(pe)
                        if n >= 8:
                            pe.wait_ge(y_s, n - 7)
                        pe.matmul(G.bank[n % 8][:, :], DyT[:, g * P:(g + 1) * P], G.hT[:, k * TILE:(k + 1) * TILE],
                                  start=True, stop=True).then_inc(y_mm, 1)
                for k in range(4):
                    if k == 0:
                        pe.wait_ge(y_s, 16)
                    for i in range(8):
                        c = 8 * k + i
                        for g in range(NH2):
                            ins = pe.matmul(G.bank[k][:, i * D:(i + 1) * D], X[:, g, c * P:(c + 1) * P], Ew[:, g, :],
                                            start=(g == 0), stop=(g == NH2 - 1))
                    ins.then_inc(v_mm, 1)
                th.tensor(pe, G)

            @block.scalar
            def _(act):
                for n in range(2 * NT):
                    act.wait_ge(u_mm, n + 1)
                    act.activation(X[:, n % 2, (n // 2) * TILE:(n // 2 + 1) * TILE], G.bank[n % 4][:, :],
                                   ACT.Relu).then_inc(u_s, 1)
                lnv_n.scalar(act, G.ln_eps[:, 0:1])
                act.wait_ge(sum_mm, 1)
                act.copy(tok_sum[:, :], G.bank[4][:, 0:NC]).then_inc(sum_s, 1)
                lna.scalar(act, G.ln_eps[:, 0:1])
                ta.scalar(act, G)
                lnw.scalar(act, G.ln_eps[:, 0:1])
                lnh.scalar(act, G.ln_eps[:, 0:1])
                th.scalar(act, G)

            @block.vector
            def _(dve):
                o = Steps(dve, own)
                dve.memset(ones[:, :], 1.0).then_inc(ones_s, 1)
                lnv_n.centre(dve)
                dve.wait_ge(list_in, 16)
                sort_list(G, dve, o, range(0, EARLY_SORT))
                lnv_n.normalise(dve)
                o.mark(dve.memset(first[:, :], 1.0))
                o.wait()
                o.then(dve.memset(first[:, ::T], 0.0))
                def by_image(x, a, b):
                    return x[:, :].rearrange("c (b t) -> c b t", t=T)[:, :, a:b]

                dve.wait_ge(turn_mm, 1)
                o.then(dve.tensor_copy(u[:, :], G.bank[5][0:NC, 0:P]))
                o.then(dve.tensor_tensor_scan(peak[:, :], first[:, :], u[:, :], 0.0, ALU.mult, ALU.max))
                o.then(dve.tensor_scalar(small[:, :], peak[:, :], L1_EPS, DECAY / L1_EPS - 1.0, ALU.is_lt, ALU.mult))
                o.mark(dve.tensor_copy(by_image(gain, 1, 5), by_image(small, 0, 4)))
                o.mark(dve.scalar_tensor_tensor(out=by_image(gain, 5, T), in0=by_image(peak, 0, T - 5), scalar=0.0,
                                                in1=by_image(small, 4, T - 1), op0=ALU.is_equal, op1=ALU.mult))
                o.mark(dve.memset(gain[:, ::T], -1.0))
                o.wait()
                o.then(dve.tensor_scalar(gain[:, :], gain[:, :], 1.0, None, ALU.add))
                o.then(dve.tensor_tensor_scan(grown[:, :], gain[:, :], u[:, :], 0.0, ALU.mult, ALU.add))
                o.then(dve.tensor_scalar(grown[:, :], grown[:, :], L1_EPS, DECAY / L1_EPS, ALU.min, ALU.mult))
                o.mark(dve.tensor_copy(by_image(total, 0, 1), by_image(u, 0, 1)))
                o.mark(dve.tensor_tensor(by_image(total, 1, T), by_image(grown, 0, T - 1), by_image(u, 1, T),
                                         ALU.add))
                o.wait()
                o.then(dve.tensor_scalar(total[:, :], total[:, :], L1_EPS, None, ALU.max))
                o.then(dve.reciprocal(rates[:, 0, :], total[:, :]))
                o.then(dve.scalar_tensor_tensor(out=rates[:, 1, :], in0=rates[:, 0, :], scalar=DECAY, in1=first[:, :],
                                                op0=ALU.mult, op1=ALU.mult))
                dve.sem_inc(rate_s, 1)

                def mask(k):
                    dve.wait_ge(st_mm, k + 1)
                    dve.tensor_tensor(SM[:, k * CPT:(k + 1) * CPT, :],
                                      G.bank[4 + k % 4][:, :].rearrange("p (c t) -> p c t", t=P),
                                      decay[:, :].unsqueeze(1).to_broadcast([P, CPT, P]), ALU.mult).then_inc(sm_s, 1)

                for k in range(NT):
                    dve.wait_ge(spread_mm, k + 1)
                    for h in range(2):
                        bank = G.bank[2 * (k % 2) + h]
                        r3 = bank[:, :].rearrange("p (c r t) -> p c r t", c=2, r=2)
                        x3 = [X[:, g, k * TILE + h * 2 * P:k * TILE + (h + 1) * 2 * P].rearrange("p (c t) -> p c t", t=P)
                              for g in range(NH2)]
                        for g in range(NH2):
                            o.mark(dve.tensor_tensor(x3[g], x3[g], r3[:, :, 0, :], ALU.mult))
                        o.wait()
                        for g in range(NH2):
                            for c in range(2):
                                o.mark(dve.tensor_tensor_scan(x3[g][:, c, :], r3[:, c, 1, :], x3[g][:, c, :], 0.0,
                                                              ALU.mult, ALU.add))
                    o.wait()
                    dve.sem_inc(x_s, 1)
                    if k:
                        mask(k - 1)
                mask(NT - 1)
                sort_list(G, dve, o, range(EARLY_SORT, PART // 8))
                read_list(G, dve, o)
                for k in range(4):
                    dve.wait_ge(a_mm, k + 1)
                    dve.tensor_copy(xa[:, 8 * k:8 * k + 8, :], G.bank[k][:, :].rearrange("p (c d) -> p c d", d=D)
                                    ).then_inc(a_s, 1)
                dve.wait_ge(a_s, 4)
                lna.vector(dve)
                ta.vector(dve, G)
                for n in range(2 * NT):
                    x = X[:, n % 2, (n // 2) * TILE:(n // 2 + 1) * TILE]
                    dve.wait_ge(y_mm, n + 1)
                    dve.scalar_tensor_tensor(out=x, in0=G.bank[n % 8][:, :], scalar=0.0, in1=x, op0=ALU.max,
                                             op1=ALU.mult).then_inc(y_s, 1)
                for k in range(4):
                    dve.wait_ge(v_mm, k + 1)
                    dve.tensor_copy(xa[:, 8 * k:8 * k + 8, :], G.bank[k][:, :].rearrange("p (c d) -> p c d", d=D)
                                    ).then_inc(v_s, 1)
                dve.wait_ge(v_s, 4)
                lnw.vector(dve)
                dve.wait_ge(lnw.normed, LG)
                o.then(dve.tensor_tensor(xa[:, :, :], xb[:, :, :], G.tm[:, :, :], ALU.add))
                lnh.vector(dve)
                th.vector(dve, G)


def batch_rounds(G, eng):
    return (eng.value_load(G.rounds[0:1, 0:1], min_val=1, max_val=EW // 16),
            eng.value_load(G.batches[0:1, 0:1], min_val=1, max_val=EW // SORTED))


def scatter_round(G, A, pool, j, scat):
    for t in range(16 * j, 16 * j + 16):
        pool.indirect_dma_start(A["slots"], bass.IndirectOffsetOnAxis(ap=G.slot_idx[:, t:t + 1], axis=0),
                                G.slot_key[:, t:t + 1], None, bounds_check=NSLOT - 1,
                                oob_is_err=False).then_inc(scat, 16)


def scatter_last_batch(G, A, pool, scat, rounds):
    m, n = batch_rounds(G, pool)
    for j in rounds:
        with pool.If(m - n * RB > j - RB):
            scatter_round(G, A, pool, j, scat)
    for j in rounds:
        with pool.If(m - n * RB > j - RB):
            if j == rounds[-1]:
                pool.wait_ge(scat, 256 * len(rounds))
            else:
                with pool.If(m - n * RB < j + 2 - RB):
                    pool.wait_ge(scat, 256 * (j - rounds[0] + 1))


def graph_sort(nc, G, A):
    with stage(nc, G) as st:
        iota = st.sb("bins_iota", [P, P], BF16)
        later_f = st.sb("later_f32", [P, P])
        later = st.sb("later", [P, P], BF16)
        upto = st.sb("upto", [P, P], BF16)
        zero = st.sb("zero_bf", [P, P], BF16)
        none = st.sb("empty_slots", [P, PART])
        sk = st.sb("sorted_keys", [P, SORTED])
        k_i = st.sb("key_i", [P, SORTED], I32)
        full_i = st.sb("bin_raw_i", [P, SORTED], I32)
        bin_i = st.sb("bin_i", [P, SORTED], I32)
        loc_i = st.sb("loc_i", [P, SORTED], I32)
        pad = st.sb("pad_f", [P, SORTED])
        pad_i = st.sb("pad_i", [P, SORTED], I32)
        bin_f = st.sb("bin_f", [P, SORTED])
        cont = st.sb("same_bin_as_before", [P, SORTED])
        pos = st.sb("place_in_run", [P, SORTED])
        rank = st.sb("rank_f", [P, SORTED])
        rank_i = st.sb("rank_i", [P, SORTED], I32)
        hot = st.sb("bin_one_hot", [P, SORTED, P], BF16)
        prod = st.sb("rank_prod", [P, 16, P])
        left = st.sb("left_keys", [P, 8])
        left_max = st.sb("left_max", [P, 1])
        left_i = st.sb("left_i", [P, 1], I32)
        tmax = st.sb("bin_max", [P, 1])
        tmx = st.sb("bin_max_all", [P, 1])
        p_i = st.sb("parts_i", [P, 1], I32)
        iota_s, c_in, none_s, none_in = st.sem("iota_s"), st.sem("later_in"), st.sem("empty_ready"), st.sem("emptied")
        tri_s, own0, own, hot_s = (st.sem("triangles"), st.sem("sort_dve_setup"), st.sem("sort_dve_steps"),
                                   st.sem("bin_one_hots"))
        rank_mm, read_s, sum_mm = st.sem("rank_mm"), st.sem("ranks_read"), st.sem("totals_mm")
        idx_s, scat, free = st.sem("slot_index_ready"), st.sem("slots_written"), st.sem("slot_buffers_free")
        cnt_s, cmax_s, seen = st.sem("bin_counted"), st.sem("bin_max_ready"), st.sem("slot_index_seen")
        left_s, lmax_s, seen_pe, seen_dve = (st.sem("left_ready"), st.sem("left_max_ready"), st.sem("ranks_read_seen"),
                                             st.sem("sort_dve_seen"))
        PER = 512
        cand, near, both = G.keys[:, 0:CAND], G.keys[:, CAND:CAND + EW], G.keys[:, :]
        with nc.Block() as block:
            @block.gpsimd
            def _(pool):
                pool.iota(iota[:, :], [[1, P]], base=0, channel_multiplier=0,
                          allow_small_or_imprecise_dtypes=True).then_inc(iota_s, 1)
                pool.wait_ge(left_s, 1)
                pool.partition_all_reduce(left_max[:, :], left[:, 0:1], P, bass.bass_isa.ReduceOp.max
                                          ).then_inc(lmax_s, 1)
                pool.wait_ge(none_in, 16)
                m, n = batch_rounds(G, pool)
                with pool.Fori(0, n) as b:
                    pool.wait_ge(idx_s, b + 1)
                    pool.sem_inc(seen, 1)
                    with pool.If(n - b > 1):
                        for j in range(RB):
                            scatter_round(G, A, pool, j, scat)
                        pool.wait_ge(scat, b * (16 * SORTED) + 16 * SORTED)
                        pool.sem_inc(free, 1)
                pool.wait_ge(cnt_s, 1)
                pool.partition_all_reduce(tmx[:, :], tmax[:, :], P, bass.bass_isa.ReduceOp.max).then_inc(cmax_s, 1)

            @block.sync
            def _(sp):
                sp.dma_start(later_f[:, :], A["c_later"]).then_inc(c_in, 16)
                sp.wait_ge(none_s, 1)
                sp.dma_start(A["slots"].rearrange("(p s) o -> p (s o)", p=P)[:, 0:PART], none[:, :]).then_inc(none_in, 16)
                sp.wait_ge(none_in, 16)

            @block.tensor
            def _(pe):
                pe.wait_ge(tri_s, 2)
                count = G.bank[0][:, 0:P]

                def add(weights, x, start=False):
                    return pe.matmul(count, weights, x, start=start, stop=True, skip_group_check=True)

                add(zero[:, :], zero[:, :], start=True)
                m, n = batch_rounds(G, pe)
                with pe.Fori(0, n) as b:
                    for j in range(RB):
                        with pe.If(m - b * RB > j):
                            pe.wait_ge(hot_s, b * RB + (j + 1))
                            for t in range(16 * j, 16 * j + 16):
                                add(later[:, :], hot[:, t, :])
                    add(zero[:, :], zero[:, :]).then_inc(rank_mm, 1)
                    pe.wait_ge(read_s, b + 1)
                    pe.sem_inc(seen_pe, 1)
                    for j in range(RB):
                        with pe.If(m - b * RB > j):
                            for t in range(16 * j, 16 * j + 16):
                                add(upto[:, :], hot[:, t, :])
                    add(zero[:, :], zero[:, :]).then_inc(sum_mm, 1)

            @block.vector
            def _(dve):
                dve.memset(none[:, :], -1.0).then_inc(none_s, 1)
                dve.memset(zero[:, :], 0.0).then_inc(tri_s, 1)
                f0 = Steps(dve, own0)
                for g in range(EW // SEG):
                    f0.mark(dve.max(cand[:, 8 * g:8 * g + 8], near[:, SEG * g:SEG * (g + 1)]))
                f0.wait()
                for g in range(EW // SEG):
                    x = near[:, SEG * g:SEG * (g + 1)]
                    f0.mark(dve.match_replace(x, cand[:, 8 * g:8 * g + 8], x, -1.0))
                f0.wait()
                f0.then(dve.max(cand[:, CAND - 8:CAND], near[:, :]))
                f0.then(dve.match_replace(near[:, :], cand[:, CAND - 8:CAND], near[:, :], -1.0))
                dve.max(left[:, :], near[:, :]).then_inc(left_s, 1)
                dve.wait_ge(c_in, 16)
                dve.tensor_copy(later[:, :], later_f[:, :])
                dve.tensor_scalar(upto[:, :], later_f[:, :], -1.0, 1.0, ALU.mult, ALU.add).then_inc(tri_s, 1)
                f0.mark(dve.memset(cont[:, 0:1], 0.0))
                dve.wait_ge(lmax_s, 1)
                f0.then(dve.tensor_scalar(left_max[:, :], left_max[:, :], 0.0, None, ALU.is_ge))
                f0.then(dve.tensor_copy(left_i[:, :], left_max[:, :]))
                dve.wait_ge(iota_s, 1)
                m, n = batch_rounds(G, dve)
                wide = dve.value_load(left_i[0:1, 0:1], min_val=0, max_val=1)
                with dve.Fori(0, n) as b:
                    o = Steps(dve, own, b * PER)

                    def rounds_of(work):
                        for j in range(RB):
                            at = o.n
                            with dve.If(m - b * RB > j):
                                work(j)
                                o.wait()
                                dve.sem_inc(seen_dve, 1)
                            with dve.If(m - b * RB < j + 1):
                                dve.wait_ge(own, o.base + at)
                                dve.sem_inc(own, o.n - at)

                    def sort_round(keys):
                        def work(j):
                            for h in range(2):
                                top = sk[:, 16 * j + 8 * h:16 * j + 8 * h + 8]
                                o.then(dve.max(top, keys))
                                dve.sem_inc(seen_dve, 1)
                                o.then(dve.match_replace(keys, top, keys, -1.0))
                                dve.sem_inc(seen_dve, 1)
                        return work

                    o.mark(dve.memset(sk[:, :], -1.0))
                    o.mark(dve.memset(rank[:, :], 0.0))
                    o.wait()
                    dve.sem_inc(seen_dve, 1)
                    for is_wide, keys in ((0, cand), (1, both)):
                        at = o.n
                        with dve.If(wide > 0) if is_wide else dve.If(wide < 1):
                            rounds_of(sort_round(keys))
                        with dve.If(wide < 1) if is_wide else dve.If(wide > 0):
                            dve.wait_ge(own, o.base + at)
                            dve.sem_inc(own, o.n - at)
                    o.wait()
                    o.mark(dve.tensor_scalar(pad[:, :], sk[:, :], 0.0, None, ALU.is_lt))
                    o.then(dve.tensor_copy(k_i[:, :], sk[:, :]))
                    o.then(dve.tensor_scalar(full_i[:, :], k_i[:, :], 17, None, ALU.arith_shift_right))
                    dve.wait_ge(sum_mm, b)
                    o.then(dve.tensor_copy(bin_f[:, :], full_i[:, :]))
                    dve.sem_inc(seen_dve, 1)

                    def one_hots(j):
                        for t in range(16 * j, 16 * j + 16):
                            ins = dve.tensor_scalar(hot[:, t, :], iota[:, :], bin_f[:, t:t + 1], None, ALU.is_equal)
                        o.then(ins)
                        dve.sem_inc(hot_s, 1)

                    at = b * RB
                    for j in range(RB):
                        here = o.n
                        with dve.If(m - b * RB > j):
                            one_hots(j)
                        with dve.If(m - b * RB < j + 1):
                            dve.wait_ge(own, o.base + here)
                            dve.sem_inc(own, 1)
                            dve.sem_inc(hot_s, 1)
                    o.wait()
                    o.mark(dve.tensor_copy(pad_i[:, :], pad[:, :]))
                    o.mark(dve.tensor_scalar(bin_i[:, :], full_i[:, :], P - 1, BIN_BITS, ALU.bitwise_and,
                                             ALU.logical_shift_left))
                    o.mark(dve.tensor_scalar(loc_i[:, :], k_i[:, :], 12, NC - 1, ALU.arith_shift_right,
                                             ALU.bitwise_and))
                    o.mark(dve.tensor_tensor(cont[:, 1:SORTED], bin_f[:, 1:SORTED], bin_f[:, 0:SORTED - 1],
                                             ALU.is_equal))
                    o.then(dve.tensor_scalar(k_i[:, :], k_i[:, :], NTOK - 1, None, ALU.bitwise_and))
                    o.mark(dve.tensor_scalar(loc_i[:, :], loc_i[:, :], 13, None, ALU.logical_shift_left))
                    o.mark(dve.tensor_scalar(pad_i[:, :], pad_i[:, :], BIN_BITS + 8, None, ALU.logical_shift_left))
                    o.then(dve.tensor_tensor_scan(pos[:, :], cont[:, :], cont[:, :], 0.0, ALU.mult, ALU.add))
                    o.mark(dve.tensor_tensor(k_i[:, :], k_i[:, :], loc_i[:, :], ALU.bitwise_or))
                    o.then(dve.tensor_tensor(bin_i[:, :], bin_i[:, :], pad_i[:, :], ALU.bitwise_or))
                    dve.wait_ge(free, b)
                    o.then(dve.tensor_copy(G.slot_key[:, :], k_i[:, :]))
                    dve.wait_ge(rank_mm, b + 1)
                    dve.sem_inc(seen_dve, 1)

                    def look_up(j):
                        for t in range(16):
                            c = 16 * j + t
                            o.mark(dve.tensor_tensor_reduce(out=prod[:, t, :], in0=G.bank[0][:, 0:P],
                                                            in1=hot[:, c, :], scale=1.0, scalar=0.0, op0=ALU.mult,
                                                            op1=ALU.add, accum_out=rank[:, c:c + 1]))

                    rounds_of(look_up)
                    o.wait()
                    dve.sem_inc(read_s, 1)
                    o.then(dve.tensor_tensor(rank[:, :], rank[:, :], pos[:, :], ALU.add))
                    o.then(dve.tensor_copy(rank_i[:, :], rank[:, :]))
                    o.then(dve.tensor_tensor(G.slot_idx[:, :], rank_i[:, :], bin_i[:, :], ALU.bitwise_or))
                    dve.sem_inc(idx_s, 1)
                    o.close(PER)
                f = Steps(dve, cnt_s, 0)
                dve.wait_ge(sum_mm, n)
                dve.tensor_tensor_reduce(out=prod[:, 0, :], in0=G.bank[0][:, 0:P], in1=G.ident[:, :], scale=1.0,
                                         scalar=0.0, op0=ALU.mult, op1=ALU.add, accum_out=G.n_bin[:, 0:1]
                                         ).then_inc(tri_s, 1)
                dve.wait_ge(tri_s, 3)
                f.then(dve.tensor_copy(tmax[:, :], G.n_bin[:, :]))
                dve.wait_ge(cmax_s, 1)
                f.then(dve.tensor_scalar(tmax[:, :], tmx[:, :], float(PART), 1.0, ALU.min, ALU.max))
                f.then(dve.tensor_scalar(tmax[:, :], tmax[:, :], 15.0, None, ALU.add))
                f.then(dve.tensor_copy(p_i[:, :], tmax[:, :]))
                f.then(dve.tensor_scalar(G.groups[:, :], p_i[:, :], 4, None, ALU.logical_shift_right))
                f.then(dve.tensor_scalar(tmx[:, :], tmx[:, :], 1.0, None, ALU.max))
                f.then(dve.tensor_scalar(tmx[:, :], tmx[:, :], 1.0 / PART, 0.5 - 0.5 / PART, ALU.mult, ALU.add))
                f.then(dve.tensor_copy(p_i[:, :], tmx[:, :]))
                f.then(dve.tensor_copy(G.passes[:, :], p_i[:, :]))


def graph_fill(nc, G, A):
    with stage(nc, G) as st:
        base = st.sb("fill_base", [P, 8])
        slot = st.sb("fill_slot", [P, 8])
        full = st.sb("fill_full", [P, 8])
        f_i = st.sb("fill_full_i", [P, 8], I32)
        s_i = st.sb("fill_slot_i", [P, 8], I32)
        bin_i = st.sb("fill_bin", [P, 8], I32)
        idx = st.sb("fill_index", [P, 8], I32)
        minus = st.sb("fill_value", [P, 8])
        own, idx_s, out_s, iota_s = (st.sem("fill_dve_steps"), st.sem("fill_index_ready"), st.sem("fill_written"),
                                     st.sem("fill_iota"))
        done, seen = st.sem("fill_done"), st.sem("fill_index_seen")
        per = PART // 8
        with nc.Block() as block:
            @block.gpsimd
            def _(pool):
                pool.iota(s_i[:, :], [[1, 8]], base=0, channel_multiplier=0).then_inc(iota_s, 1)
                pool.iota(bin_i[:, :], [[0, 8]], base=0, channel_multiplier=1).then_inc(iota_s, 1)
                n = pool.value_load(G.passes[0:1, 0:1], min_val=1, max_val=NEDGE // PART)
                with pool.If(n > 1):
                    with pool.Fori(0, (n - 1) * per) as i:
                        pool.wait_ge(idx_s, i + 1)
                        pool.sem_inc(seen, 1)
                        for t in range(8):
                            pool.indirect_dma_start(A["slots"], bass.IndirectOffsetOnAxis(ap=idx[:, t:t + 1], axis=0),
                                                    minus[:, t:t + 1], None, bounds_check=NSLOT - 1,
                                                    oob_is_err=False).then_inc(out_s, 16)
                        pool.wait_ge(out_s, i * 128 + 128)
                        pool.sem_inc(done, 1)

            @block.vector
            def _(dve):
                dve.wait_ge(iota_s, 2)
                o = Steps(dve, own)
                o.mark(dve.memset(minus[:, :], -1.0))
                o.mark(dve.tensor_scalar(bin_i[:, :], bin_i[:, :], BIN_BITS, None, ALU.logical_shift_left))
                o.then(dve.tensor_copy(slot[:, :], s_i[:, :]))
                o.then(dve.tensor_scalar(slot[:, :], slot[:, :], float(PART), None, ALU.add))
                start, PER = o.n, 16
                n = dve.value_load(G.passes[0:1, 0:1], min_val=1, max_val=NEDGE // PART)
                with dve.If(n > 1):
                    with dve.Fori(0, (n - 1) * per) as i:
                        r = Steps(dve, own, i * PER + start)
                        r.then(dve.tensor_scalar(full[:, :], slot[:, :], G.n_bin[:, 0:1], None, ALU.is_lt))
                        r.mark(dve.tensor_copy(f_i[:, :], full[:, :]))
                        r.then(dve.tensor_copy(s_i[:, :], slot[:, :]))
                        r.mark(dve.tensor_scalar(f_i[:, :], f_i[:, :], BIN_BITS + 8, None, ALU.logical_shift_left))
                        r.then(dve.tensor_tensor(s_i[:, :], s_i[:, :], bin_i[:, :], ALU.bitwise_or))
                        r.then(dve.tensor_tensor(idx[:, :], s_i[:, :], f_i[:, :], ALU.bitwise_or))
                        dve.sem_inc(idx_s, 1)
                        r.then(dve.tensor_scalar(slot[:, :], slot[:, :], 8.0, None, ALU.add))
                        dve.wait_ge(done, i + 1)
                        r.close(PER)


def graph_and_experts(nc, G, A):
    with stage(nc, G) as st:
        sb, sem = st.sb, st.sem
        W1 = sb("e1_w1", [D, EXP1, HID1])
        b1 = sb("e1_b1", [HID1, EXP1])
        W2 = sb("e1_w2", [HID1, EXP1, D])
        b2 = sb("e1_b2", [1, 2, EXP1 * D])
        ones = sb("e1_ones", [1, P])
        Wg = sb("gat_w", [D, ROW])
        att = sb("gat_att", [D, 2, HEADS * EXP1])
        wa = sb("gat_w_att", [D, 2, HEADS * EXP1])
        w_in, e_in, wg_s = sem("gat_weights_in"), sem("e1_weights_in"), sem("gat_w_ready")
        tab_mm, tab_s, tab_out, far_in = sem("table_mm"), sem("table_kept"), sem("table_out"), sem("far_row_in")
        l1_mm, gelu_s, l2_mm, x_s = sem("e1_l1_mm"), sem("e1_gelu"), sem("e1_l2_mm"), sem("e1_out_kept")
        thr_i = sb("node_thresholds_i", [P, NC], I32)
        thr = sb("node_thresholds", [P, NC])
        row_i = sb("list_row_i", [P, NC], I32)
        rowf = sb("list_row", [P, NC])
        loc = sb("list_node", [P, PART])
        cont = sb("same_as_before", [P, PART])
        contb = sb("same_as_after", [P, PART])
        mc = sb("before_penalty", [P, PART])
        mb = sb("after_penalty", [P, PART])
        endf = sb("segment_end", [P, NC])
        have = sb("node_has_edges", [P, NC])
        no = sb("no_edges_penalty", [P, NC])
        end_i = sb("segment_end_i", [P, NC], I32)
        Gt = sb("gathered", [P, PART, ROW])
        AS = sb("edge_src", [P, HEADS, PART])
        AD = sb("edge_dst", [P, HEADS, PART])
        MF = sb("edge_max", [P, HEADS, PART])
        MB = sb("edge_max_back", [P, HEADS, PART])
        Wt = sb("edge_weight", [P, HEADS, PART])
        MSG = sb("edge_msg", [P, 16, PART])
        ge = MSG[:, :, :].rearrange("p f n -> p (f n)").bitcast(BF16).rearrange("p (c n) -> p c n", c=NC)
        R = sb("segment_rows", [P, PART, ROW])
        HH = R[:, :, :].rearrange("p n f -> p (n f)")[:, 0:2 * EXP1 * TILE].rearrange("p (u e t) -> p u e t", u=2,
                                                                                      e=EXP1)
        N = sb("node_rows", [P, NC, ROW])
        m_run = sb("node_max", [P, NC, HEADS])
        m_new = sb("node_max_new", [P, NC, HEADS])
        den = sb("node_den", [P, NC, HEADS])
        agg = sb("node_agg", [P, NC, 16])
        lr = [sb(f"node_lrelu{i}", [P, NC, HEADS]) for i in range(3)]
        zz = sb("node_z", [P, 3, NC, HEADS])
        t16 = sb("node_t16", [P, NC, 16])
        gp = {n: sb("gat_" + n, [P, 16]) for n in ("bias", "gamma", "beta")}
        before = sb("expert_before", [P, 16])
        s1, s2, s3 = sb("gate_s1", [P, NC]), sb("gate_s2", [P, NC]), sb("gate_s3", [P, NC])
        sc, ex, rk = sb("gate_scores", [P, NC, EXP1]), sb("gate_exp", [P, NC, EXP1]), sb("gate_rank", [P, NC, EXP1])
        p1, p2 = sb("gate_pairs", [P, NC, EXP1, EXP1]), sb("gate_pairs2", [P, NC, EXP1, EXP1])
        list_ready = sem("list_ready")
        par_in, iota_s, own0, own = sem("gat_params_in"), sem("list_iotas"), sem("graph_dve_setup"), sem("graph_dve_steps")
        list_free, list_in, sort_s = sem("list_free"), sem("list_in"), sem("list_sorting")
        gat, gt_s, seen, seen_dve = sem("rows_gathered"), sem("gathered_zeroed"), sem("pool_seen"), sem("dve_seen")
        dif_s, w_s, rows_s, rows_out, ends_in = (sem("exponents_ready"), sem("weights_ready"), sem("segment_rows_ready"),
                                                 sem("segment_rows_out"), sem("node_rows_in"))
        nd_s, ne_s = sem("rescale_exponents"), sem("rescales_ready")
        sq_a, sq_b, std_a, std_b, ex_a, ex_b = (sem("gate_centred"), sem("gate_squared"), sem("gate_var"),
                                                sem("gate_std"), sem("gate_logits"), sem("gate_exps"))
        PER, RPP = 512, PART // 8 * 2 + 8
        fold = PART // 16

        def per_node(x, n):
            return x.unsqueeze(3).to_broadcast([P, NC, HEADS, n])

        def passes(eng):
            return eng.value_load(G.passes[0:1, 0:1], min_val=1, max_val=NEDGE // PART)

        with nc.Block() as block:
            @block.sync
            def _(sp):
                sp.dma_start(Wg[:, 0:16], A["L1_ffn_W_gat"]).then_inc(w_in, 16)
                for i, n in enumerate((A["L1_ffn_att_src"], A["L1_ffn_att_dst"])):
                    sp.dma_start(att[:, i, :], n.rearrange("(o h) e -> o (h e)", o=1).to_broadcast([D, 16])
                                 ).then_inc(w_in, 16)
                sp.dma_start(W1[:, :, :], A["L1_ffn_W1"].rearrange("e d h -> d e h")).then_inc(e_in, 16)
                sp.dma_start(b1[:, :], A["L1_ffn_b1T"]).then_inc(e_in, 16)
                sp.dma_start(W2[:, :, :], A["L1_ffn_W2"].rearrange("e h d -> h e d")).then_inc(e_in, 16)
                for i in range(2):
                    sp.dma_start(b2[:, i, :], A["L1_ffn_b2"].rearrange("(o e) d -> o (e d)", o=1)).then_inc(e_in, 16)
                sp.wait_ge(tab_s, 2)
                sp.dma_start(A["table"].rearrange("(c p) f -> p c f", p=P), G.tab[:, :, :]).then_inc(tab_out, 16)
                sp.wait_ge(tab_out, 16)
                sp.dma_start(G.far[:, :], A["table"][FAR:FAR + 1, :].to_broadcast([P, ROW])).then_inc(far_in, 16)
                for n, a in (("bias", A["L1_ffn_b_gat"]), ("gamma", A["L1_ffn_ln_gamma"]), ("beta", A["L1_ffn_ln_beta"])):
                    sp.dma_start(gp[n][:, :], a.rearrange("(o f) -> o f", o=1).to_broadcast([P, 16])).then_inc(par_in, 16)
                sp.dma_start(before[:, :], A["c_before"]).then_inc(par_in, 16)
                n = passes(sp)
                with sp.Fori(0, n) as k:
                    with sp.If(k > 0):
                        sp.wait_ge(list_free, k)
                        load_list(G, A, sp, k, list_in)
                    sp.wait_ge(rows_s, k + 1)
                    sp.dma_start(A["ends"].rearrange("(p s) f -> p s f", p=P), R[:, :, :]).then_inc(rows_out, 16)

            @block.gpsimd
            def _(pool):
                pool.iota(thr_i[:, :], [[2 * NTOK, NC]], base=0, channel_multiplier=0).then_inc(iota_s, 1)
                pool.iota(row_i[:, :], [[0, NC]], base=0, channel_multiplier=PART).then_inc(iota_s, 1)
                pool.wait_ge(gt_s, 1)
                pool.wait_ge(tab_out, 16)
                n = passes(pool)
                m = pool.value_load(G.groups[0:1, 0:1], min_val=1, max_val=fold)
                with pool.Fori(0, n) as k:
                    pool.wait_ge(list_ready, k + 1)
                    pool.sem_inc(seen, 1)
                    for g in range(fold):
                        with pool.If(m + k * fold > g):
                            for j in range(16 * g, 16 * g + 16):
                                pool.indirect_dma_start(Gt[:, j, :], None, A["table"],
                                                        bass.IndirectOffsetOnAxis(ap=G.src_i[:, j:j + 1], axis=0)
                                                        ).then_inc(gat, 16)
                    pool.wait_ge(rows_out, 16 * k + 16)
                    pool.sem_inc(seen, 1)
                    for c in range(NC):
                        pool.indirect_dma_start(N[:, c, :], None, A["ends"],
                                                bass.IndirectOffsetOnAxis(ap=end_i[:, c:c + 1], axis=0)
                                                ).then_inc(ends_in, 16)

            @block.tensor
            def _(pe):
                pe.wait_ge(wg_s, 1)
                for h in range(2):
                    for i in range(16):
                        c = 16 * h + i
                        ins = pe.matmul(G.bank[h][:, i * ROW:(i + 1) * ROW], G.hT[:, c * P:(c + 1) * P], Wg[:, :],
                                        start=True, stop=True)
                    ins.then_inc(tab_mm, 1)
                pe.wait_ge(e_in, 80)

                def layer2(k):
                    pe.wait_ge(gelu_s, EXP1 * (k + 1))
                    for h in range(2):
                        n = 2 * k + h
                        if n >= 2:
                            pe.wait_ge(x_s, n - 1)
                        pe.matmul(G.bank[6 + h][:, :], ones[:, :], b2[:, :, :].rearrange("o i f -> o (i f)"),
                                  start=True, stop=True)
                        for i in range(2):
                            for e in range(EXP1):
                                ins = pe.matmul(G.bank[6 + h][:, (i * EXP1 + e) * D:(i * EXP1 + e + 1) * D],
                                                HH[:, k % 2, e, (2 * h + i) * P:(2 * h + i + 1) * P], W2[:, e, :],
                                                start=False, stop=True, skip_group_check=True)
                        ins.then_inc(l2_mm, 1)

                for k in range(NT):
                    for e in range(EXP1):
                        n = k * EXP1 + e
                        if n >= EXP1:
                            pe.wait_ge(gelu_s, n - EXP1 + 1)
                        pe.matmul(G.bank[2 + n % 4][:, :], W1[:, e, :], G.hT[:, k * TILE:(k + 1) * TILE], start=True,
                                  stop=True).then_inc(l1_mm, 1)
                    if k:
                        layer2(k - 1)
                layer2(NT - 1)

            def keep_experts(act, k):
                for n in (2 * k, 2 * k + 1):
                    act.wait_ge(l2_mm, n + 1)
                    act.copy(G.xo[:, 2 * n:2 * n + 2, :], G.bank[6 + n % 2][:, :]).then_inc(x_s, 1)

            @block.scalar
            def _(act):
                act.wait_ge(e_in, 80)
                for n in range(NT * EXP1):
                    k, e = n // EXP1, n % EXP1
                    act.wait_ge(l1_mm, n + 1)
                    if k >= 2 and e == 0:
                        act.wait_ge(l2_mm, 2 * (k - 1))
                    act.activation(HH[:, k % 2, e, :], G.bank[2 + n % 4][:, :], ACT.Gelu, bias=b1[:, e:e + 1]
                                   ).then_inc(gelu_s, 1)
                    if k and e == EXP1 - 1:
                        keep_experts(act, k - 1)
                keep_experts(act, NT - 1)
                act.wait_ge(nd_s, 1)
                act.activation(zz[:, 0:2, :, :], zz[:, 0:2, :, :], ACT.Exp).then_inc(ne_s, 1)
                n = passes(act)
                with act.Fori(0, n) as k:
                    act.wait_ge(dif_s, k + 1)
                    act.activation(Wt[:, :, :], Wt[:, :, :], ACT.Exp).then_inc(w_s, 1)
                    act.wait_ge(nd_s, k + 2)
                    act.activation(zz[:, 0:2, :, :], zz[:, 0:2, :, :], ACT.Exp).then_inc(ne_s, 1)
                act.wait_ge(sq_a, 1)
                act.activation(t16[:, :, :], agg[:, :, :], ACT.Square).then_inc(sq_b, 1)
                act.wait_ge(std_a, 1)
                act.activation(s3[:, :], s2[:, :], ACT.Sqrt, bias=G.ln_eps[:, 0:1], scale=1.0 / 16).then_inc(std_b, 1)
                act.wait_ge(ex_a, 1)
                act.activation(ex[:, :, :], sc[:, :, :], ACT.Exp).then_inc(ex_b, 1)

            @block.vector
            def _(dve):
                o = Steps(dve, own0)
                dve.memset(Gt[:, :, :], 0.0).then_inc(gt_s, 1)
                dve.sem_inc(list_ready, 1)
                dve.sem_inc(sort_s, RPP)
                o.mark(dve.memset(ones[:, :], 1.0))
                dve.wait_ge(w_in, 48)
                o.then(dve.tensor_tensor(wa[:, :, :], att[:, :, :], Wg[:, 0:16].unsqueeze(1).to_broadcast([D, 2, 16]),
                                         ALU.mult))
                dve.tensor_reduce(Wg[:, 16:24], wa[:, :, :].rearrange("d s (h e) -> d (s h) e", e=EXP1), AX_X,
                                  ALU.add).then_inc(wg_s, 1)
                for h in range(2):
                    dve.wait_ge(tab_mm, h + 1)
                    dve.tensor_copy(G.tab[:, 16 * h:16 * h + 16, :], G.bank[h][:, 0:16 * ROW].rearrange(
                        "p (c f) -> p c f", f=ROW)).then_inc(tab_s, 1)
                dve.wait_ge(tab_s, 2)
                dve.wait_ge(iota_s, 2)
                o.mark(dve.tensor_copy(thr[:, :], thr_i[:, :]))
                o.mark(dve.tensor_copy(rowf[:, :], row_i[:, :]))
                o.mark(dve.memset(cont[:, 0:1], 0.0))
                o.mark(dve.memset(contb[:, PART - 1:PART], 0.0))
                o.mark(dve.memset(N[:, :, 16:20], 1.0))
                o.mark(dve.tensor_copy(N[:, :, 0:16], G.tab[:, :, 0:16]))
                o.mark(dve.tensor_copy(N[:, :, 20:24], G.tab[:, :, 16:20]))
                o.mark(dve.tensor_copy(den[:, :, :], G.n_far[:, :].unsqueeze(2).to_broadcast([P, NC, HEADS])))
                dve.wait_ge(far_in, 16)
                o.mark(dve.tensor_tensor(agg[:, :, :], G.n_far[:, :].unsqueeze(2).to_broadcast([P, NC, 16]),
                                         G.far[:, 0:16].unsqueeze(1).to_broadcast([P, NC, 16]), ALU.mult))
                o.then(dve.tensor_scalar(s1[:, :], G.n_far[:, :], 0.0, -BIG, ALU.is_equal, ALU.mult))
                o.then(dve.tensor_tensor(m_run[:, :, :], s1[:, :].unsqueeze(2).to_broadcast([P, NC, HEADS]),
                                         G.far[:, 16:20].unsqueeze(1).to_broadcast([P, NC, HEADS]), ALU.add))

                def merge(f, step):
                    f.then(dve.tensor_tensor(m_new[:, :, :], m_run[:, :, :], N[:, :, 20:24], ALU.max))
                    for i, m in enumerate((m_run[:, :, :], N[:, :, 20:24], m_new[:, :, :])):
                        f.mark(dve.tensor_tensor(lr[i][:, :, :], m, G.tab[:, :, 20:24], ALU.add))
                    f.wait()
                    for i in range(3):
                        f.mark(dve.scalar_tensor_tensor(out=lr[i][:, :, :], in0=lr[i][:, :, :], scalar=0.2,
                                                        in1=lr[i][:, :, :], op0=ALU.mult, op1=ALU.max))
                    f.wait()
                    for i in range(2):
                        f.mark(dve.tensor_tensor(zz[:, i, :, :], lr[i][:, :, :], lr[2][:, :, :], ALU.subtract))
                    f.wait()
                    dve.sem_inc(nd_s, 1)
                    f.then(dve.tensor_copy(m_run[:, :, :], m_new[:, :, :]))
                    dve.wait_ge(ne_s, step + 1)
                    f.mark(dve.tensor_tensor(den[:, :, :], den[:, :, :], zz[:, 0, :, :], ALU.mult))
                    f.mark(dve.tensor_tensor(lr[0][:, :, :], N[:, :, 16:20], zz[:, 1, :, :], ALU.mult))
                    f.mark(dve.tensor_tensor(agg[:, :, :].rearrange("p c (h e) -> p c h e", e=4),
                                             agg[:, :, :].rearrange("p c (h e) -> p c h e", e=4),
                                             per_node(zz[:, 0, :, :], 4), ALU.mult))
                    f.then(dve.tensor_tensor(t16[:, :, :].rearrange("p c (h e) -> p c h e", e=4),
                                             N[:, :, 0:16].rearrange("p c (h e) -> p c h e", e=4),
                                             per_node(zz[:, 1, :, :], 4), ALU.mult))
                    f.mark(dve.tensor_tensor(den[:, :, :], den[:, :, :], lr[0][:, :, :], ALU.add))
                    f.then(dve.tensor_tensor(agg[:, :, :], agg[:, :, :], t16[:, :, :], ALU.add))

                merge(o, 0)
                n = passes(dve)
                m = dve.value_load(G.groups[0:1, 0:1], min_val=1, max_val=fold)
                with dve.Fori(0, n) as k:
                    f = Steps(dve, own, k * PER)
                    with dve.If(k > 0):
                        r = Steps(dve, sort_s, k * RPP)
                        dve.wait_ge(list_in, 16 * k)
                        dve.sem_inc(seen_dve, 1)
                        sort_list(G, dve, r, range(PART // 8), seen_dve)
                        read_list(G, dve, r)
                        r.close(RPP)
                        dve.sem_inc(list_ready, 1)
                    f.then(dve.tensor_copy(loc[:, :], G.place_i[:, :]))
                    f.mark(dve.tensor_tensor(cont[:, 1:PART], loc[:, 1:PART], loc[:, 0:PART - 1], ALU.is_equal))
                    f.then(dve.tensor_tensor(contb[:, 0:PART - 1], loc[:, 0:PART - 1], loc[:, 1:PART], ALU.is_equal))
                    f.mark(dve.tensor_scalar(mc[:, :], cont[:, :], 1.0, BIG, ALU.subtract, ALU.mult))
                    f.mark(dve.tensor_scalar(mb[:, :], contb[:, :], 1.0, BIG, ALU.subtract, ALU.mult))
                    f.then(dve.tensor_tensor(ge[:, :, :], G.sorted[:, :].unsqueeze(1).to_broadcast([P, NC, PART]),
                                             thr[:, :].unsqueeze(2).to_broadcast([P, NC, PART]), ALU.is_ge))
                    f.then(dve.tensor_reduce(endf[:, :], ge[:, :, :], AX_X, ALU.add))
                    f.mark(dve.tensor_tensor(have[:, 0:NC - 1], endf[:, 0:NC - 1], endf[:, 1:NC], ALU.is_gt))
                    f.then(dve.tensor_scalar(have[:, NC - 1:NC], endf[:, NC - 1:NC], 0.0, None, ALU.is_gt))
                    f.mark(dve.tensor_scalar(no[:, :], have[:, :], 1.0, BIG, ALU.subtract, ALU.mult))
                    f.then(dve.tensor_scalar(endf[:, :], endf[:, :], 1.0, 1.0, ALU.max, ALU.subtract))
                    f.then(dve.tensor_tensor(endf[:, :], endf[:, :], rowf[:, :], ALU.add))
                    f.then(dve.tensor_copy(end_i[:, :], endf[:, :]))
                    f.then(dve.memset(AD[:, :, :], 0.0))
                    for c in range(NC):
                        own_score = (Wt, MB)[c % 2]
                        for h in range(HEADS):
                            f.mark(dve.tensor_scalar(own_score[:, h, :], loc[:, :], float(c),
                                                     G.tab[:, c, 20 + h:21 + h], ALU.is_equal, ALU.mult))
                        f.wait()
                        f.mark(dve.tensor_tensor(AD[:, :, :], AD[:, :, :], own_score[:, :, :], ALU.add))
                    f.wait()
                    dve.wait_ge(gat, m * 256 + k * (16 * PART))
                    f.then(dve.tensor_copy(AS[:, :, :], Gt[:, :, 16:20].rearrange("p n h -> p h n")))
                    for h in range(HEADS):
                        f.mark(dve.tensor_tensor_scan(MF[:, h, :], mc[:, :], AS[:, h, :], -BIG, ALU.add, ALU.max))
                        f.mark(dve.tensor_tensor_scan(MB[:, h, ::-1], mb[:, ::-1], AS[:, h, ::-1], -BIG, ALU.add,
                                                      ALU.max))
                    f.wait()
                    f.then(dve.tensor_tensor(MF[:, :, :], MF[:, :, :], MB[:, :, :], ALU.max))
                    dve.wait_ge(x_s, 2 * NT)
                    f.mark(dve.tensor_copy(R[:, :, 20:24].rearrange("p n h -> p h n"), MF[:, :, :]))
                    f.mark(dve.tensor_tensor(AS[:, :, :], AS[:, :, :], AD[:, :, :], ALU.add))
                    f.then(dve.tensor_tensor(MB[:, :, :], MF[:, :, :], AD[:, :, :], ALU.add))
                    f.mark(dve.scalar_tensor_tensor(out=AS[:, :, :], in0=AS[:, :, :], scalar=0.2, in1=AS[:, :, :],
                                                    op0=ALU.mult, op1=ALU.max))
                    f.then(dve.scalar_tensor_tensor(out=MB[:, :, :], in0=MB[:, :, :], scalar=0.2, in1=MB[:, :, :],
                                                    op0=ALU.mult, op1=ALU.max))
                    f.then(dve.tensor_tensor(Wt[:, :, :], AS[:, :, :], MB[:, :, :], ALU.subtract))
                    dve.sem_inc(dif_s, 1)
                    dve.wait_ge(w_s, k + 1)
                    f.then(dve.tensor_tensor(Wt[:, :, :], Wt[:, :, :],
                                             G.valid[:, :].unsqueeze(1).to_broadcast([P, HEADS, PART]), ALU.mult))
                    for h in range(HEADS):
                        f.mark(dve.tensor_tensor(MSG[:, 4 * h:4 * h + 4, :],
                                                 Gt[:, :, 4 * h:4 * h + 4].rearrange("p n f -> p f n"),
                                                 Wt[:, h:h + 1, :].to_broadcast([P, 4, PART]), ALU.mult))
                    f.wait()
                    for q in range(16):
                        f.mark(dve.tensor_tensor_scan(R[:, :, q], cont[:, :], MSG[:, q, :], 0.0, ALU.mult, ALU.add))
                    for h in range(HEADS):
                        f.mark(dve.tensor_tensor_scan(R[:, :, 16 + h], cont[:, :], Wt[:, h, :], 0.0, ALU.mult,
                                                      ALU.add))
                    f.wait()
                    dve.sem_inc(rows_s, 1)
                    dve.wait_ge(ends_in, k * (16 * NC) + 16 * NC)
                    f.then(dve.tensor_tensor(N[:, :, :], N[:, :, :], have[:, :].unsqueeze(2).to_broadcast([P, NC, ROW]),
                                             ALU.mult))
                    f.then(dve.tensor_tensor(N[:, :, 20:24], N[:, :, 20:24],
                                             no[:, :].unsqueeze(2).to_broadcast([P, NC, HEADS]), ALU.add))
                    merge(f, k + 1)
                    dve.sem_inc(list_free, 1)
                    f.close(PER)
                dve.wait_ge(par_in, 64)
                b16 = [P, NC, 16]
                o.then(dve.tensor_scalar(den[:, :, :], den[:, :, :], 1e-16, None, ALU.add))
                o.then(dve.reciprocal(den[:, :, :], den[:, :, :]))
                o.then(dve.tensor_tensor(agg[:, :, :].rearrange("p c (h e) -> p c h e", e=4),
                                         agg[:, :, :].rearrange("p c (h e) -> p c h e", e=4),
                                         per_node(den[:, :, :], 4), ALU.mult))
                o.then(dve.tensor_tensor(agg[:, :, :], agg[:, :, :], gp["bias"][:, :].unsqueeze(1).to_broadcast(b16),
                                         ALU.add))
                o.then(dve.tensor_reduce(s1[:, :], agg[:, :, :], AX_X, ALU.add))
                o.then(dve.scalar_tensor_tensor(out=agg[:, :, :], in0=s1[:, :].unsqueeze(2).to_broadcast(b16),
                                                scalar=-1.0 / 16, in1=agg[:, :, :], op0=ALU.mult, op1=ALU.add))
                dve.sem_inc(sq_a, 1)
                dve.wait_ge(sq_b, 1)
                o.then(dve.tensor_reduce(s2[:, :], t16[:, :, :], AX_X, ALU.add))
                dve.sem_inc(std_a, 1)
                dve.wait_ge(std_b, 1)
                o.then(dve.reciprocal(s1[:, :], s3[:, :]))
                o.then(dve.tensor_tensor(agg[:, :, :], agg[:, :, :], s1[:, :].unsqueeze(2).to_broadcast(b16), ALU.mult))
                o.then(dve.tensor_tensor(agg[:, :, :], agg[:, :, :], gp["gamma"][:, :].unsqueeze(1).to_broadcast(b16),
                                         ALU.mult))
                o.then(dve.tensor_tensor(agg[:, :, :], agg[:, :, :], gp["beta"][:, :].unsqueeze(1).to_broadcast(b16),
                                         ALU.add))
                o.then(dve.tensor_reduce(sc[:, :, :], agg[:, :, :].rearrange("p c (h e) -> p c e h", e=4), AX_X,
                                         ALU.add))
                o.then(dve.tensor_scalar(sc[:, :, :], sc[:, :, :], 1.0 / HEADS, None, ALU.mult))
                other = sc[:, :, :].unsqueeze(2).to_broadcast([P, NC, EXP1, EXP1])
                mine = sc[:, :, :].unsqueeze(3).to_broadcast([P, NC, EXP1, EXP1])
                o.mark(dve.tensor_tensor(p1[:, :, :, :], other, mine, ALU.is_gt))
                o.mark(dve.tensor_tensor(p2[:, :, :, :], other, mine, ALU.is_equal))
                o.then(dve.tensor_reduce(s1[:, :], sc[:, :, :], AX_X, ALU.max))
                o.mark(dve.tensor_tensor(p2[:, :, :, :].rearrange("p c e f -> p c (e f)"),
                                         p2[:, :, :, :].rearrange("p c e f -> p c (e f)"),
                                         before[:, :].unsqueeze(1).to_broadcast(b16), ALU.mult))
                o.then(dve.tensor_tensor(sc[:, :, :], sc[:, :, :], s1[:, :].unsqueeze(2).to_broadcast([P, NC, EXP1]),
                                         ALU.subtract))
                dve.sem_inc(ex_a, 1)
                o.then(dve.tensor_tensor(p1[:, :, :, :], p1[:, :, :, :], p2[:, :, :, :], ALU.add))
                o.then(dve.tensor_reduce(rk[:, :, :], p1[:, :, :, :], AX_X, ALU.add))
                dve.wait_ge(ex_b, 1)
                o.then(dve.scalar_tensor_tensor(out=ex[:, :, :], in0=rk[:, :, :], scalar=2.0, in1=ex[:, :, :],
                                                op0=ALU.is_lt, op1=ALU.mult))
                o.then(dve.tensor_reduce(s2[:, :], ex[:, :, :], AX_X, ALU.add))
                o.then(dve.reciprocal(s2[:, :], s2[:, :]))
                o.then(dve.tensor_tensor(G.gates[:, :, :], ex[:, :, :],
                                         s2[:, :].unsqueeze(2).to_broadcast([P, NC, EXP1]), ALU.mult))


def combine(nc, G, A):
    with stage(nc, G) as st:
        R = st.sb("mix", [P, NC, D])
        Y = st.sb("mix_tmp", [P, NC, D])
        own, out_s = st.sem("mix_dve_steps"), st.sem("out_written")
        ln = LayerNorm(st, "ln4", R, G.tm, Y)
        with nc.Block() as block:
            @block.vector
            def _(dve):
                o = Steps(dve, own)
                for e in range(EXP1):
                    g = G.gates[:, :, e:e + 1].to_broadcast([P, NC, D])
                    o.then(dve.tensor_tensor(Y[:, :, :], G.xo[:, :, e * D:(e + 1) * D], g, ALU.mult))
                    o.then(dve.tensor_tensor(R[:, :, :], Y[:, :, :], G.tm[:, :, :] if e == 0 else R[:, :, :], ALU.add))
                ln.vector(dve)

            @block.scalar
            def _(act):
                ln.scalar(act, G.ln_eps[:, 0:1])

            @block.sync
            def _(sp):
                for g in range(LG):
                    sp.wait_ge(ln.normed, g + 1)
                    sp.dma_start(A["out"].rearrange("b t d -> (b t) d").rearrange("(c p) d -> p c d", p=P)[
                        :, g * LC:(g + 1) * LC, :], G.tm[:, g * LC:(g + 1) * LC, :]).then_inc(out_s, 16)
                sp.wait_ge(out_s, 16 * LG)


def program(nc, A):
    A["slots"] = nc.dram_tensor("bin_slots", [NSLOT, 1], F32).ap()
    A["table"] = nc.dram_tensor("node_table", [NTOK, ROW], F32).ap()
    A["ends"] = nc.dram_tensor("segment_table", [P * PART, ROW], F32).ap()
    G = Shared()
    with stage(nc, G) as st:
        G.bank = [st.enter_context(nc.psum_tensor(f"bank{i}", [P, TILE], F32)) for i in range(8)]
        G.hT = st.sb("h_features", [D, NTOK])
        G.ident = st.sb("ident", [P, P])
        G.ln_eps = st.sb("ln_eps", [P, 1])
        G.rounds = st.sb("sort_rounds", [P, 1], I32)
        G.batches = st.sb("sort_batches", [P, 1], I32)
        G.slot_key = st.sb("slot_key", [P, SORTED])
        G.slot_idx = st.sb("slot_index", [P, SORTED], I32)
        G.passes = st.sb("graph_passes", [P, 1], I32)
        G.groups = st.sb("first_groups", [P, 1], I32)
        G.n_bin = st.sb("n_bin", [P, 1])
        G.n_far = st.sb("n_far", [P, NC])
        with stage(nc, G) as keys:
            G.keys = keys.sb("edge_keys", [P, CAND + EW])
            tokens_and_counts(nc, G, A)
            graph_sort(nc, G, A)
        G.tm = st.sb("h_tokens", [P, NC, D])
        G.raw = st.sb("list_raw", [P, PART])
        G.sorted = st.sb("list_sorted", [P, PART])
        G.valid = st.sb("list_valid", [P, PART])
        G.key_i = st.sb("list_key_i", [P, PART], I32)
        G.place_i = st.sb("list_place_i", [P, PART], I32)
        G.src_i = st.sb("list_src_i", [P, PART], I32)
        attention0(nc, G, A)
        experts0(nc, G, A)
        fresh_semaphores(nc, G)
        attention1(nc, G, A)
        graph_fill(nc, G, A)
        G.tab = st.sb("node_rows_own", [P, NC, ROW])
        G.far = st.sb("far_row", [P, ROW])
        G.gates = st.sb("gates", [P, NC, EXP1])
        G.xo = st.sb("expert_out", [P, NC, EXP1 * D])
        graph_and_experts(nc, G, A)
        combine(nc, G, A)


_INS = ["x", "L0_tok_W", "L0_tok_b", "L0_attn_Q", "L0_attn_K", "L0_attn_VT", "L0_ffn_Wr", "L0_ffn_br", "L0_ffn_W1",
        "L0_ffn_W2", "L0_ffn_Wo", "L0_ffn_bo", "L1_attn_DxT", "L1_attn_DyT", "L1_attn_ET", "L1_ffn_W_gat",
        "L1_ffn_att_src", "L1_ffn_att_dst", "L1_ffn_b_gat", "L1_ffn_ln_gamma", "L1_ffn_ln_beta", "L1_ffn_W1",
        "L1_ffn_b1T", "L1_ffn_W2", "L1_ffn_b2", "L1_ffn_edge_index"]
_BN = ["b1", "g1", "be1", "m1", "v1", "b2", "g2", "be2", "m2", "v2"]


def layouts(inputs):
    a = {k: np.asarray(v) for k, v in inputs.items()}
    for name in ("L0_attn_V", "L1_attn_Dx", "L1_attn_Dy", "L1_attn_E", "L1_ffn_b1"):
        a[name + "T"] = np.ascontiguousarray(a[name].T)
    for n in _BN:
        a["bn_" + n] = np.ascontiguousarray(a["L0_ffn_" + n].reshape(NPAIR, 2 * 64).T)
    return a


def kernel(**inputs):
    import concourse.bacc as bacc
    from concourse.bass_utils import run_bass_kernel_spmd

    nc = bacc.Bacc("TRN2", target_bir_lowering=False, num_devices=1)
    consts = shape_constants()
    data = layouts(inputs)
    arrays, A = {}, {}

    def declare(name, a):
        arrays[f"in_{name}"] = np.ascontiguousarray(a)
        return nc.dram_tensor(f"in_{name}", a.shape, mybir.dt.from_np(a.dtype), kind="ExternalInput").ap()

    for name in _INS:
        A[name] = declare(name, data[name])
    for name in _BN:
        A["bn_" + name] = declare("bn_" + name, data["bn_" + name])
    for name in consts:
        A[name] = declare(name, consts[name])
    A["out"] = nc.dram_tensor("out_dram", (B, T, D), F32, kind="ExternalOutput").ap()
    program(nc, A)
    r = run_bass_kernel_spmd(nc, [arrays], core_ids=[0])
    return r.results[0]["out_dram"]
```

```python
from contextlib import ExitStack

import numpy as np

import concourse.bass as bass
from concourse import mybir

ALU = mybir.AluOpType
ACT = mybir.ActivationFunctionType
F32 = mybir.dt.float32
BF16 = mybir.dt.bfloat16
I32 = mybir.dt.int32
AX_X = mybir.AxisListType.X

B, IMG = 64, 84
T, D = 64, 64
NTOK = B * T
P = 128
NC = NTOK // P
TILE = 512
NT = NTOK // TILE
CPT = TILE // P
EXP0, NPAIR = 8, 4
NSTATE, NH2 = 256, 2
EXP1, HID1 = 4, 128
HEADS = 4
LN_EPS, BN_EPS, L1_EPS, DECAY = 1e-5, 1e-3, 1e-12, 0.97
NMAP, NOP = 7, 4
NEDGE = 262144
EW = NEDGE // P
FAR = NTOK - 1
SPREAD = 512
BIN_BITS = 18
NSLOT = P << BIN_BITS
HELP = 17
SEG = 64
CAND = EW // SEG * 8 + 8
SORTED = 256
SHIFT = SORTED.bit_length() - 1
RB = SORTED // 16
EARLY_SORT = 14
ALWAYS = 10
ASKED = ((10,), (11, 12), (13, 14, 15))
EARLY, MIDDLE = 1, 9
PART = 256
ROW = 24
BIG = 1e30
MAP_OPS = [(0, 0), (1, 0), (0, 1), (1, 1), (3, 2), (2, 3), (3, 3)]


def resize_matrix(n):
    inv = n / 8.0
    kernel = max(inv, 1.0)
    sample = (np.arange(8) + 0.5) * inv - 0.5
    w = np.maximum(0.0, 1.0 - np.abs(sample[:, None] - np.arange(n)[None, :]) / kernel)
    return w / w.sum(axis=1, keepdims=True)


def haar(n, sign):
    m = np.zeros((n // 2, n))
    for k in range(n // 2):
        m[k, 2 * k], m[k, 2 * k + 1] = 1.0, sign
    return m * 0.7071067811865476


def haar_operators():
    half = IMG // 2
    low = haar(IMG, 1.0)
    return np.stack([resize_matrix(half // 2) @ haar(half, 1.0) @ low,
                     resize_matrix(half // 2) @ haar(half, -1.0) @ low,
                     resize_matrix(half) @ low,
                     resize_matrix(half) @ haar(IMG, -1.0)])


def shape_constants():
    ops = haar_operators()
    rows = ops.transpose(2, 0, 1).reshape(IMG, NOP * 8)
    cols = np.zeros((NMAP, 8, NOP, IMG))
    for m, (v, w) in enumerate(MAP_OPS):
        for j in range(8):
            cols[m, j, v] = ops[w, j]
    same = np.arange(P)[:, None] // T == np.arange(P)[None, :] // T
    t = np.arange(P) % T
    gap = t[None, :] - 1 - t[:, None]
    decay = np.where(same & (gap >= 0), DECAY ** np.maximum(gap, 0), 0.0)
    pick = np.zeros((EXP0, NPAIR, P))
    for e in range(EXP0):
        pick[e, e // 2, (e % 2) * 64:(e % 2) * 64 + 64] = 1.0
    return {
        "c_rows": rows.astype(np.float32),
        "c_cols": cols.reshape(NMAP, 8 * NOP, IMG).astype(np.float32),
        "c_other": np.where(same, 0.0, -1e30).astype(np.float32),
        "c_decay": decay.astype(np.float32),
        "c_pick": pick.astype(np.float32),
        "c_ident": np.eye(P, dtype=np.float32),
        "c_later": np.triu(np.ones((P, P), np.float32), 1),
        "c_hi_parity": (np.arange(64)[:, None] % 2 == np.arange(2)[None, :]).astype(np.float32),
        "c_hi_half": (np.arange(64)[:, None] // 2 == np.arange(NC)[None, :]).astype(np.float32),
        "c_before": np.tile((np.arange(4)[None, :] < np.arange(4)[:, None]).astype(np.float32).reshape(1, 16), (P, 1)),
    }


class Steps:

    def __init__(self, eng, sem, base=0):
        self.eng, self.sem, self.base, self.n = eng, sem, base, 0

    def then(self, ins):
        self.mark(ins)
        self.wait()

    def wait(self):
        self.eng.wait_ge(self.sem, self.base + self.n)

    def close(self, per):
        assert self.n < per
        self.wait()
        self.eng.sem_inc(self.sem, per - self.n)

    def mark(self, ins):
        ins.then_inc(self.sem, 1)
        self.n += 1
        return self.n


class Shared:

    def __init__(self):
        self.semaphores = []


def stage(nc, G):
    st = ExitStack()
    st.sb = lambda name, shape, dt=F32: st.enter_context(nc.sbuf_tensor(name, shape, dt))
    st.sem = lambda name: new_semaphore(nc, G, name)
    return st


def new_semaphore(nc, G, name):
    G.semaphores.append(nc.alloc_semaphore(name=name))
    return G.semaphores[-1]


def fresh_semaphores(nc, G):
    nc.all_engine_barrier()
    nc.clear_and_free_semaphores(G.semaphores)
    nc.all_engine_barrier()
    G.semaphores = []


LG = 4
LC = NC // LG


class LayerNorm:

    def __init__(self, st, name, x, out, sq, xc=None):
        self.src, self.out, self.sq = x, out, sq
        self.x = x if xc is None else xc
        self.sum = st.sb(name + "_sum", [P, NC])
        self.var = st.sb(name + "_var", [P, NC])
        self.centred = st.sem(name + "_centred")
        self.squared = st.sem(name + "_squared")
        self.var_ready = st.sem(name + "_var_ready")
        self.std_ready = st.sem(name + "_std_ready")
        self.normed = st.sem(name + "_normed")
        self.own = st.sem(name + "_dve_steps")

    def vector(self, dve):
        self.centre(dve)
        self.normalise(dve)

    def centre(self, dve, groups=range(LG)):
        if groups[0] == 0:
            self.steps = Steps(dve, self.own)
        own = self.steps
        for g in groups:
            c = slice(g * LC, (g + 1) * LC)
            own.then(dve.tensor_reduce(self.sum[:, c], self.src[:, c, :], AX_X, ALU.add))
            dve.scalar_tensor_tensor(out=self.x[:, c, :], in0=self.sum[:, c].unsqueeze(2).to_broadcast([P, LC, D]),
                                     scalar=-1.0 / D, in1=self.src[:, c, :], op0=ALU.mult,
                                     op1=ALU.add).then_inc(self.centred, 1)

    def normalise(self, dve):
        own = self.steps
        for g in range(LG):
            c = slice(g * LC, (g + 1) * LC)
            dve.wait_ge(self.squared, g + 1)
            dve.tensor_reduce(self.var[:, c], self.sq[:, c, :], AX_X, ALU.add).then_inc(self.var_ready, 1)
        dve.wait_ge(self.std_ready, 1)
        own.then(dve.reciprocal(self.sum[:, :], self.var[:, :]))
        for g in range(LG):
            c = slice(g * LC, (g + 1) * LC)
            dve.tensor_tensor(self.out[:, c, :], self.x[:, c, :],
                              self.sum[:, c].unsqueeze(2).to_broadcast([P, LC, D]),
                              ALU.mult).then_inc(self.normed, 1)

    def scalar(self, act, eps):
        for g in range(LG):
            c = slice(g * LC, (g + 1) * LC)
            act.wait_ge(self.centred, g + 1)
            act.activation(self.sq[:, c, :], self.x[:, c, :], ACT.Square).then_inc(self.squared, 1)
        act.wait_ge(self.var_ready, LG)
        act.activation(self.var[:, :], self.var[:, :], ACT.Sqrt, bias=eps, scale=1.0 / D).then_inc(self.std_ready, 1)


class ToFeatures:

    def __init__(self, st, name, src, dst, ready, ready_per_group):
        self.src, self.dst, self.ready, self.per = src, dst, ready, ready_per_group
        self.turned = st.sem(name + "_turned")
        self.kept_act = st.sem(name + "_kept_by_act")
        self.kept_dve = st.sem(name + "_kept_by_dve")

    def tensor(self, pe, G):
        for k in range(NT):
            if self.per:
                pe.wait_ge(self.ready, k * CPT // LC + 1)
            for i in range(CPT):
                ins = pe.transpose(G.bank[k][0:D, i * P:(i + 1) * P], self.src[:, k * CPT + i, :], G.ident[:, :])
            ins.then_inc(self.turned, 1)

    def scalar(self, act, G):
        for k in range(0, NT, 2):
            act.wait_ge(self.turned, k + 1)
            act.copy(self.dst[:, k * TILE:(k + 1) * TILE], G.bank[k][0:D, :]).then_inc(self.kept_act, 1)

    def vector(self, dve, G):
        for k in range(1, NT, 2):
            dve.wait_ge(self.turned, k + 1)
            dve.tensor_copy(self.dst[:, k * TILE:(k + 1) * TILE], G.bank[k][0:D, :]).then_inc(self.kept_dve, 1)

    def wait(self, eng):
        eng.wait_ge(self.kept_act, NT // 2)
        eng.wait_ge(self.kept_dve, NT // 2)


def tokens_and_counts(nc, G, A):
    with stage(nc, G) as st:
        room = st.sb("images_then_gaps", [P, B * IMG])
        X = room[0:IMG, :].rearrange("h (b w) -> h b w", w=IMG)
        two = st.sb("col_ops_then_rows_done", [IMG, 8 * NOP * IMG])
        cols = two[0:NMAP, :].rearrange("m (q w) -> m q w", w=IMG)
        Y = two[:, 0:NOP * B * 8].rearrange("w (v b i) -> w v b i", v=NOP, b=B)
        rows = st.sb("row_ops", [IMG, NOP * 8])
        Wm = st.sb("embed_w", [NMAP, D])
        bias = st.sb("embed_b", [D, 1])
        Wj = st.sb("col_weights", [IMG, 8 * NOP, D])
        hi = st.sb("dst_hi", [P, EW], BF16)
        lo = st.sb("dst_lo", [P, EW], BF16)
        W = SPREAD // 2
        hot = [st.sb(f"dst_one_hot{u}", [P, P, W], BF16) for u in range(2)]
        spare = hot[1][:, :, :].rearrange("p v w -> p (v w)")
        e_i = spare[:, 0:4 * EW].bitcast(I32).rearrange("p (s w) -> p s w", s=2)
        srcf, dstf, tmp = (spare[:, (4 + 2 * i) * EW:(6 + 2 * i) * EW].bitcast(F32) for i in range(3))
        bin_i, loc_i = (spare[:, (10 + 2 * i) * EW:(12 + 2 * i) * EW].bitcast(I32) for i in range(2))
        zero = st.sb("zero_weights", [P, P], BF16)
        gap = room[:, 0:HELP * W].bitcast(BF16).rearrange("p (u i w) -> p u i w", u=2, i=HELP)
        minus_v = st.sb("minus_values", [P, HELP])
        one = st.sb("one_col", [P, 1])
        par = st.sb("hi_parity", [64, 2])
        half = st.sb("hi_half", [64, NC])
        split = st.sb("hist_split", [64, 2, 64])
        near_n = st.sb("near_count", [P, 1])
        near_max = st.sb("near_max", [P, 1])
        left = st.sb("left_keys", [P, 8])
        left_max = st.sb("left_max", [P, 1])
        left_s, lmax_s = st.sem("left_ready"), st.sem("left_max_ready")
        r_i = st.sb("rounds_tmp", [P, 1], I32)
        img_in = [st.sem(f"images_in{i}") for i in range(4)]
        par_in = st.sem("embed_params_in")
        rows_mm = st.sem("rows_mm")
        wj_mm = st.sem("col_weights_mm")
        y_kept = st.sem("rows_kept")
        wj_kept = st.sem("col_weights_kept")
        h_mm = st.sem("embed_mm")
        h_act = st.sem("embed_kept_act")
        e_in, c_in, own = st.sem("edges_in"), st.sem("hist_consts_in"), st.sem("counts_dve_steps")
        near_s, max_s = st.sem("near_counted"), st.sem("near_max_ready")
        hot_s, used_s, split_s, far_mm = (st.sem("one_hots"), st.sem("one_hots_used"), st.sem("hist_split_ready"),
                                          st.sem("far_mm"))
        zero_s = st.sem("zero_weights_ready")
        help_s, gap_s, hot_act, seen_act = (st.sem("help_constants"), st.sem("lo_gaps"), st.sem("one_hots_by_act"),
                                            st.sem("act_seen"))
        float_s, lo_ready, key_ready = st.sem("edges_as_floats"), st.sem("lo_ready"), st.sem("keys_plus_one_ready")
        NS = EW // W
        xv = A["x"].rearrange("b o h w -> h (b o) w")
        ev = A["L1_ffn_edge_index"].rearrange("s (p w) -> s p w", p=P)
        with nc.Block() as block:
            @block.sync
            def _(sp):
                sp.dma_start(e_i[:, 0, :], ev[0]).then_inc(e_in, 16)
                sp.dma_start(e_i[:, 1, :], ev[1]).then_inc(e_in, 16)
                sp.dma_start(rows[:, :], A["c_rows"]).then_inc(par_in, 16)
                for i in range(0, 4, 2):
                    sp.dma_start(X[:, 16 * i:16 * i + 16, :], xv[:, 16 * i:16 * i + 16, :]).then_inc(img_in[i], 16)
                sp.dma_start(par[:, :], A["c_hi_parity"]).then_inc(c_in, 16)
                sp.dma_start(half[:, :], A["c_hi_half"]).then_inc(c_in, 16)
                sp.dma_start(G.ident[:, :], A["c_ident"]).then_inc(c_in, 16)

            @block.scalar
            def _(act):
                act.dma_start(cols[:, :, :], A["c_cols"]).then_inc(par_in, 16)
                act.dma_start(Wm[:, :], A["L0_tok_W"]).then_inc(par_in, 16)
                act.dma_start(bias[:, :], A["L0_tok_b"].rearrange("(d o) -> d o", o=1)).then_inc(par_in, 16)
                for i in range(1, 4, 2):
                    act.dma_start(X[:, 16 * i:16 * i + 16, :], xv[:, 16 * i:16 * i + 16, :]).then_inc(img_in[i], 16)
                act.wait_ge(e_in, 32)
                act.copy(srcf[:, :], e_i[:, 0, :]).then_inc(float_s, 1)
                act.copy(dstf[:, :], e_i[:, 1, :]).then_inc(float_s, 1)
                act.wait_ge(lo_ready, 1)
                act.copy(lo[:, :], e_i[:, 1, :]).then_inc(float_s, 1)
                act.wait_ge(key_ready, 1)
                act.activation(G.keys[:, CAND:CAND + EW], srcf[:, :], ACT.Copy, bias=-1.0).then_inc(float_s, 1)
                for k in range(4):
                    act.wait_ge(wj_mm, k + 1)
                    act.copy(Wj[:, 8 * k:8 * k + 8, :], G.bank[4 + k][0:IMG, :]).then_inc(wj_kept, 1)
                for k in range(4):
                    act.wait_ge(rows_mm, k + 1)
                    act.copy(Y[:, :, 16 * k:16 * k + 16, :].rearrange("w v b i -> w b v i"),
                             G.bank[k][0:IMG, :].rearrange("w (b v i) -> w b v i", v=NOP, i=8)).then_inc(y_kept, 1)
                for j in range(8):
                    act.wait_ge(h_mm, j + 1)
                    act.activation(G.hT[:, :].rearrange("d (r j) -> d r j", j=8)[:, :, j], G.bank[1 + j % 7][0:D, :],
                                   ACT.Identity, bias=bias[:, 0:1]).then_inc(h_act, 1)
                act.wait_ge(help_s, 2)
                with act.Fori(1, NS // 2) as q:
                    for u in range(2):
                        act.wait_ge(used_s, q * 2 + (u - 1))
                        act.sem_inc(seen_act, 1)
                        for i in range(HELP):
                            act.activation(gap[:, u, i, :], lo[:, bass.ds((q * 2 + u) * W, W)], ACT.Square,
                                           bias=minus_v[:, i:i + 1]).then_inc(gap_s, 1)
                        act.wait_ge(gap_s, q * (2 * HELP) + (u - 1) * HELP)
                        for i in range(HELP):
                            ins = act.activation(hot[u][:, P - HELP + i, :], gap[:, u, i, :], ACT.Relu,
                                                 bias=one[:, 0:1], scale=-1.0)
                        ins.then_inc(hot_act, 1)

            @block.gpsimd
            def _(pool):
                for i in range(HELP):
                    ins = pool.memset(minus_v[:, i:i + 1], -float(64 - HELP + i))
                ins.then_inc(help_s, 1)
                pool.memset(one[:, :], 1.0).then_inc(help_s, 1)
                pool.wait_ge(near_s, 1)
                pool.partition_all_reduce(near_max[:, :], near_n[:, :], P, bass.bass_isa.ReduceOp.max
                                          ).then_inc(max_s, 1)
                pool.wait_ge(left_s, 1)
                pool.partition_all_reduce(left_max[:, :], left[:, 0:1], P, bass.bass_isa.ReduceOp.max
                                          ).then_inc(lmax_s, 1)

            @block.tensor
            def _(pe):
                pe.wait_ge(par_in, 64)
                for k in range(4):
                    for q in range(8 * k, 8 * k + 8):
                        ins = pe.matmul(G.bank[4 + k][0:IMG, (q % 8) * D:(q % 8 + 1) * D], cols[:, q, :], Wm[:, :],
                                        start=True, stop=True)
                    ins.then_inc(wj_mm, 1)
                for k in range(4):
                    pe.wait_ge(img_in[k], 16)
                    for b in range(16):
                        ins = pe.matmul(G.bank[k][0:IMG, b * 32:(b + 1) * 32], X[:, 16 * k + b, :], rows[:, :],
                                        start=True, stop=True)
                    ins.then_inc(rows_mm, 1)
                pe.wait_ge(y_kept, 4)
                pe.wait_ge(wj_kept, 4)

                def embed(j):
                    if j == 7:
                        pe.wait_ge(h_act, 1)
                    for v in range(NOP):
                        ins = pe.matmul(G.bank[1 + j % 7][0:D, :], Wj[:, j * NOP + v, :],
                                        Y[:, v, :, :].rearrange("w b i -> w (b i)"),
                                        start=(v == 0), stop=(v == NOP - 1))
                    ins.then_inc(h_mm, 1)

                def count(u):
                    for e in range(W):
                        ins = pe.matmul(G.bank[0][:, 0:64], hot[u][:, :, e], hot[u][:, 64:P, e], start=False,
                                        stop=True, skip_group_check=True)
                    ins.then_inc(used_s, 1)

                for j in range(4):
                    embed(j)
                pe.wait_ge(zero_s, 1)
                pe.matmul(G.bank[0][:, 0:64], zero[:, :], zero[:, 0:64], start=True, stop=True)
                pe.wait_ge(hot_s, 1)
                count(0)
                for j in range(4, 8):
                    embed(j)
                pe.wait_ge(hot_s, 2)
                count(1)
                with pe.Fori(1, NS // 2) as q:
                    for u in range(2):
                        pe.wait_ge(hot_s, q * 2 + (u + 1))
                        pe.wait_ge(hot_act, q * 2 + (u - 1))
                        count(u)
                pe.wait_ge(h_act, 8)
                pe.wait_ge(split_s, 2)
                pe.matmul(G.bank[1][:, 0:NC], split[:, :, :].rearrange("h r l -> h (r l)"), half[:, :], start=True,
                          stop=True).then_inc(far_mm, 1)

            @block.vector
            def _(dve):
                o = Steps(dve, own)
                dve.memset(zero[:, :], 0.0).then_inc(zero_s, 1)
                dve.wait_ge(e_in, 32)
                dve.wait_ge(float_s, 2)
                o.then(dve.tensor_scalar(tmp[:, :], srcf[:, :], float(FAR), None, ALU.is_lt))
                o.mark(dve.tensor_scalar(bin_i[:, :], e_i[:, 1, :], P - 1, 5, ALU.bitwise_and, ALU.logical_shift_left))
                o.then(dve.tensor_scalar(loc_i[:, :], e_i[:, 1, :], 7, None, ALU.logical_shift_right))
                o.mark(dve.tensor_tensor(bin_i[:, :], bin_i[:, :], loc_i[:, :], ALU.bitwise_or))
                o.mark(dve.tensor_scalar(e_i[:, 0, :], e_i[:, 1, :], 6, None, ALU.logical_shift_right))
                o.then(dve.tensor_scalar(e_i[:, 1, :], e_i[:, 1, :], 63, None, ALU.bitwise_and))
                o.then(dve.scalar_tensor_tensor(out=hi[:, :], in0=tmp[:, :], scalar=256.0, in1=e_i[:, 0, :],
                                                op0=ALU.mult, op1=ALU.add))
                dve.sem_inc(lo_ready, 1)
                o.then(dve.scalar_tensor_tensor(out=tmp[:, :], in0=dstf[:, :], scalar=float(NTOK), in1=tmp[:, :],
                                                op0=ALU.is_lt, op1=ALU.mult))
                dve.tensor_reduce(near_n[:, :], tmp[:, :], AX_X, ALU.add).then_inc(near_s, 1)
                o.then(dve.scalar_tensor_tensor(out=srcf[:, :], in0=bin_i[:, :], scalar=float(NTOK), in1=srcf[:, :],
                                                op0=ALU.mult, op1=ALU.add))
                o.then(dve.scalar_tensor_tensor(out=srcf[:, :], in0=srcf[:, :], scalar=1.0, in1=tmp[:, :],
                                                op0=ALU.add, op1=ALU.mult))
                dve.sem_inc(key_ready, 1)
                dve.wait_ge(max_s, 1)
                o.then(dve.tensor_scalar(near_max[:, :], near_max[:, :], 15.0, 16.0, ALU.add, ALU.max))
                o.then(dve.tensor_copy(r_i[:, :], near_max[:, :]))
                o.then(dve.tensor_scalar(G.rounds[:, :], r_i[:, :], 4, None, ALU.logical_shift_right))
                o.then(dve.tensor_scalar(r_i[:, :], r_i[:, :], SORTED - 16, None, ALU.add))
                o.then(dve.tensor_scalar(G.batches[:, :], r_i[:, :], SHIFT, None, ALU.logical_shift_right))

                def one_hots(u, q, n_lo):
                    for v in range(64):
                        dve.tensor_scalar(hot[u][:, v, :], hi[:, bass.ds(q * W, W)], float(v), None, ALU.is_equal)
                    for v in range(n_lo):
                        ins = dve.tensor_scalar(hot[u][:, 64 + v, :], lo[:, bass.ds(q * W, W)], float(v), None,
                                                ALU.is_equal)
                    ins.then_inc(hot_s, 1)

                dve.wait_ge(float_s, 4)
                for u in range(2):
                    one_hots(u, u, 64)
                cand, near = G.keys[:, 0:CAND], G.keys[:, CAND:CAND + EW]
                for g in range(EW // SEG):
                    o.mark(dve.max(cand[:, 8 * g:8 * g + 8], near[:, SEG * g:SEG * (g + 1)]))
                o.wait()
                for g in range(EW // SEG):
                    x = near[:, SEG * g:SEG * (g + 1)]
                    o.mark(dve.match_replace(x, cand[:, 8 * g:8 * g + 8], x, -1.0))
                o.wait()
                with dve.Fori(1, NS // 2) as q:
                    for u in range(2):
                        dve.wait_ge(used_s, q * 2 + (u - 1))
                        one_hots(u, q * 2 + u, 64 - HELP)
                o.then(dve.max(cand[:, CAND - 8:CAND], near[:, :]))
                o.then(dve.match_replace(near[:, :], cand[:, CAND - 8:CAND], near[:, :], -1.0))
                dve.max(left[:, :], near[:, :]).then_inc(left_s, 1)
                dve.wait_ge(lmax_s, 1)
                o.then(dve.tensor_scalar(left_max[:, :], left_max[:, :], 0.0, None, ALU.is_ge))
                o.then(dve.tensor_copy(G.wide[:, :], left_max[:, :]))
                dve.wait_ge(used_s, NS)
                dve.wait_ge(c_in, 48)
                for r in range(2):
                    ins = dve.tensor_scalar(split[:, r, :], G.bank[0][0:64, 0:64], par[:, r:r + 1], None, ALU.mult)
                    ins.then_inc(split_s, 1)
                dve.wait_ge(far_mm, 1)
                o.then(dve.tensor_copy(G.n_far[:, :], G.bank[1][:, 0:NC]))


def batch_rounds(G, eng):
    return (eng.value_load(G.rounds[0:1, 0:1], min_val=1, max_val=EW // 16),
            eng.value_load(G.batches[0:1, 0:1], min_val=1, max_val=EW // SORTED))


def scatter_round(G, A, pool, j, scat):
    for t in range(16 * j, 16 * j + 16):
        pool.indirect_dma_start(A["slots"], bass.IndirectOffsetOnAxis(ap=G.slot_idx[:, t:t + 1], axis=0),
                                G.slot_key[:, t:t + 1], None, bounds_check=NSLOT - 1,
                                oob_is_err=False).then_inc(scat, 16)


def scatter_last_batch(G, A, pool, scat, rounds):
    m, n = batch_rounds(G, pool)
    for j in rounds:
        with pool.If(m - n * RB > j - RB):
            scatter_round(G, A, pool, j, scat)


def wait_for_scatter(G, pool, scat, rounds):
    m, n = batch_rounds(G, pool)
    for j in rounds:
        with pool.If(m - n * RB > j - RB):
            if j == rounds[-1]:
                pool.wait_ge(scat, 256 * len(rounds))
            else:
                with pool.If(m - n * RB < j + 2 - RB):
                    pool.wait_ge(scat, 256 * (j - rounds[0] + 1))


def attention0_and_sort(nc, G, A):
    with stage(nc, G) as st:
        Qw = st.sb("q_w", [D, D])
        Kw = st.sb("k_w", [D, D])
        IV = st.sb("ident_v", [D, 2 * D])
        GT = st.sb("g_t", [D, D])
        Z = st.sb("z", [D, NTOK])
        HV = st.sb("h_and_v", [P, NC, 2 * D])
        other = st.sb("other_image", [P, P])
        S = st.sb("scores", [P, NC, P])
        ET = st.sb("probs_t", [P, NC, P])
        nmax = st.sb("neg_max", [P, NC])
        rmax = st.sb("row_max", [P, NC])
        rsum = st.sb("row_sum", [P, NC])
        rinv = st.sb("row_inv", [P, NC])
        R = st.sb("attn_sum", [P, NC, D])
        par_in = st.sem("attn0_params_in")
        g_mm = st.sem("g_mm")
        g_kept = st.sem("g_kept")
        z_mm, z_act, hv_mm, hv_act = st.sem("z_mm"), st.sem("z_kept"), st.sem("hv_mm"), st.sem("hv_kept")
        s_mm, s_max, s_neg, s_exp = st.sem("scores_mm"), st.sem("scores_max"), st.sem("scores_neg"), st.sem("probs")
        t_mm, t_act = st.sem("probs_turned"), st.sem("probs_t_kept")
        o_mm = st.sem("attn_out_mm")
        own_a = st.sem("attn0_dve_steps")
        ln = LayerNorm(st, "ln0", R, G.tm, S[:, 0:NC // 2, :].rearrange("p c (u d) -> p (c u) d", u=2))
        tf = ToFeatures(st, "ln0_turn", G.tm, G.hT, ln.normed, True)
        iota = st.sb("bins_iota", [P, P], BF16)
        later_f = st.sb("later_f32", [P, P])
        later = st.sb("later", [P, P], BF16)
        upto = st.sb("upto", [P, P], BF16)
        zero = st.sb("zero_bf", [P, P], BF16)
        ones = st.sb("ones_bf", [P, P], BF16)
        none = st.sb("empty_slots", [P, PART])
        sk = st.sb("sorted_keys", [P, SORTED])
        k_i = st.sb("key_i", [P, SORTED], I32)
        full_i = st.sb("bin_raw_i", [P, SORTED], I32)
        bin_i = st.sb("bin_i", [P, SORTED], I32)
        loc_i = st.sb("loc_i", [P, SORTED], I32)
        pad = st.sb("pad_f", [P, SORTED])
        pad_i = st.sb("pad_i", [P, SORTED], I32)
        bin_f = st.sb("bin_f", [P, SORTED])
        bin_b = st.sb("bin_bf16", [P, SORTED], BF16)
        cont = st.sb("same_bin_as_before", [P, SORTED])
        pos = st.sb("place_in_run", [P, SORTED])
        rank = st.sb("rank_f", [P, SORTED])
        rank_i = st.sb("rank_i", [P, SORTED], I32)
        hot = st.sb("bin_one_hot", [P, SORTED, P], BF16)
        prod = st.sb("rank_prod", [P, 16, P], F32)
        tmax = st.sb("bin_max", [P, 1])
        tmx = st.sb("bin_max_all", [P, 1])
        p_i = st.sb("parts_i", [P, 1], I32)
        iota_s, c_in, none_s, none_in = st.sem("iota_s"), st.sem("later_in"), st.sem("empty_ready"), st.sem("emptied")
        tri_s, own0, own, hot_s = (st.sem("triangles"), st.sem("sort_dve_setup"), st.sem("sort_dve_steps"),
                                   st.sem("bin_one_hots"))
        rank_mm, read_s, sum_mm = st.sem("rank_mm"), st.sem("ranks_read"), st.sem("totals_mm")
        idx_s, scat, free = st.sem("slot_index_ready"), st.sem("slots_written"), st.sem("slot_buffers_free")
        cnt_s, cmax_s, seen = st.sem("bin_counted"), st.sem("bin_max_ready"), st.sem("slot_index_seen")
        seen_dve = st.sem("sort_dve_seen")
        PER = 512
        cand, both = G.keys[:, 0:CAND], G.keys[:, :]
        scat_last = st.sem("slots_written_0")
        with nc.Block() as block:
            @block.gpsimd
            def _(pool):
                pool.iota(iota[:, :], [[1, P]], base=0, channel_multiplier=0,
                          allow_small_or_imprecise_dtypes=True).then_inc(iota_s, 1)
                pool.wait_ge(none_in, 16)
                m, n = batch_rounds(G, pool)
                with pool.Fori(0, n) as b:
                    pool.wait_ge(idx_s, b + 1)
                    pool.sem_inc(seen, 1)
                    with pool.If(n - b > 1):
                        for j in range(RB):
                            scatter_round(G, A, pool, j, scat)
                        pool.wait_ge(scat, b * (16 * SORTED) + 16 * SORTED)
                        pool.sem_inc(free, 1)
                pool.wait_ge(cnt_s, 1)
                pool.partition_all_reduce(tmx[:, :], tmax[:, :], P, bass.bass_isa.ReduceOp.max).then_inc(cmax_s, 1)
                scatter_last_batch(G, A, pool, scat_last, range(0, EARLY))
                wait_for_scatter(G, pool, scat_last, range(0, EARLY))

            @block.sync
            def _(sp):
                sp.dma_start(Qw[:, :], A["L0_attn_Q"]).then_inc(par_in, 16)
                sp.dma_start(Kw[:, :], A["L0_attn_K"]).then_inc(par_in, 16)
                sp.dma_start(IV[:, 0:D], A["c_ident"][0:D, 0:D]).then_inc(par_in, 16)
                sp.dma_start(IV[:, D:2 * D], A["L0_attn_VT"]).then_inc(par_in, 16)
                sp.dma_start(other[:, :], A["c_other"]).then_inc(par_in, 16)
                sp.dma_start(later_f[:, :], A["c_later"]).then_inc(c_in, 16)
                sp.wait_ge(none_s, 1)
                sp.dma_start(A["slots"].rearrange("(p s) o -> p (s o)", p=P)[:, 0:PART], none[:, :]).then_inc(none_in, 16)
                sp.wait_ge(none_in, 16)

            @block.tensor
            def _(pe):
                pe.wait_ge(par_in, 80)
                pe.matmul(G.bank[0][0:D, 0:D], Qw[:, :], Kw[:, :], start=True, stop=True).then_inc(g_mm, 1)
                pe.wait_ge(g_kept, 1)
                for k in range(NT):
                    pe.matmul(G.bank[k][0:D, :], GT[:, :], G.hT[:, k * TILE:(k + 1) * TILE],
                              start=True, stop=True).then_inc(z_mm, 1)
                for k in range(NT):
                    pe.wait_ge(z_act, k + 1)
                    for i in range(CPT):
                        c = slice((k * CPT + i) * P, (k * CPT + i + 1) * P)
                        ins = pe.matmul(G.bank[k][:, i * P:(i + 1) * P], Z[:, c], G.hT[:, c], start=True, stop=True)
                    ins.then_inc(s_mm, 1)
                for k in range(NT):
                    pe.wait_ge(s_max, (k + 1) * CPT)
                    for i in range(CPT):
                        c = k * CPT + i
                        ins = pe.matmul(G.bank[k][:, i * P:(i + 1) * P], G.hT[:, c * P:(c + 1) * P], IV[:, :],
                                        start=True, stop=True)
                    ins.then_inc(hv_mm, 1)
                pe.wait_ge(tri_s, 2)
                pe.wait_ge(hv_act, NT)
                count, total = G.bank[6][:, 0:P], G.bank[7][:, 0:P]
                pe.matmul(total, zero[:, :], zero[:, :], start=True, stop=True)

                def add(weights, x, start=False):
                    return pe.matmul(count, weights, x, start=start, stop=True, skip_group_check=True)

                add(zero[:, :], zero[:, :], start=True)
                m, n = batch_rounds(G, pe)
                with pe.Fori(0, n) as b:
                    def count_round(j):
                        pe.wait_ge(hot_s, b * RB + (j + 1))
                        for t in range(16 * j, 16 * j + 16):
                            add(later[:, :], hot[:, t, :])

                    for j in range(ALWAYS):
                        count_round(j)
                    for js in ASKED:
                        with pe.If(m - b * RB > js[0]):
                            for j in js:
                                count_round(j)
                    add(zero[:, :], zero[:, :]).then_inc(rank_mm, 1)

                    def total_rounds(js):
                        for t in range(16 * js[0], 16 * js[-1] + 16):
                            pe.matmul(total, ones[:, :], hot[:, t, :], start=False, stop=True, skip_group_check=True)

                    total_rounds(range(ALWAYS))
                    for js in ASKED:
                        with pe.If(m - b * RB > js[0]):
                            total_rounds(js)
                    with pe.If(n - b > 1):
                        pe.wait_ge(read_s, b + 1)
                        for t in range(SORTED):
                            add(upto[:, :], hot[:, t, :])
                    pe.matmul(total, zero[:, :], zero[:, :], start=False, stop=True, skip_group_check=True
                              ).then_inc(sum_mm, 1)
                for k in range(NT):
                    pe.wait_ge(s_exp, (k + 1) * CPT)
                    if k >= 6:
                        pe.wait_ge(t_act, k - 5)
                    for i in range(CPT):
                        ins = pe.transpose(G.bank[k % 6][:, i * P:(i + 1) * P], S[:, k * CPT + i, :], G.ident[:, :])
                    ins.then_inc(t_mm, 1)
                for k in range(4):
                    pe.wait_ge(t_act, NT)
                    for i in range(8):
                        c = 8 * k + i
                        ins = pe.matmul(G.bank[k][:, i * D:(i + 1) * D], ET[:, c, :], HV[:, c, D:2 * D],
                                        start=True, stop=True)
                    ins.then_inc(o_mm, 1)
                tf.tensor(pe, G)

            @block.scalar
            def _(act):
                act.wait_ge(g_mm, 1)
                act.copy(GT[:, :], G.bank[0][0:D, 0:D]).then_inc(g_kept, 1)
                for k in range(NT):
                    act.wait_ge(z_mm, k + 1)
                    act.copy(Z[:, k * TILE:(k + 1) * TILE], G.bank[k][0:D, :]).then_inc(z_act, 1)
                for k in range(NT):
                    act.wait_ge(hv_mm, k + 1)
                    act.copy(HV[:, k * CPT:(k + 1) * CPT, :], G.bank[k][:, :]).then_inc(hv_act, 1)
                for k in range(NT):
                    act.wait_ge(s_neg, k + 1)
                    for c in range(k * CPT, (k + 1) * CPT):
                        act.activation(S[:, c, :], S[:, c, :], ACT.Exp, bias=nmax[:, c:c + 1],
                                       accum_out=rsum[:, c:c + 1]).then_inc(s_exp, 1)
                for k in range(NT):
                    act.wait_ge(t_mm, k + 1)
                    act.copy(ET[:, k * CPT:(k + 1) * CPT, :], G.bank[k % 6][:, :]).then_inc(t_act, 1)
                ln.scalar(act, G.ln_eps[:, 0:1])
                tf.scalar(act, G)

            @block.vector
            def _(dve):
                dve.memset(none[:, :], -1.0).then_inc(none_s, 1)
                dve.memset(ones[:, :], 1.0)
                dve.memset(zero[:, :], 0.0).then_inc(tri_s, 1)
                f0 = Steps(dve, own0)
                dve.wait_ge(c_in, 16)
                dve.tensor_copy(later[:, :], later_f[:, :])
                dve.tensor_scalar(upto[:, :], later_f[:, :], -1.0, 1.0, ALU.mult, ALU.add).then_inc(tri_s, 1)
                f0.mark(dve.memset(cont[:, 0:1], 0.0))
                f0.wait()
                dve.wait_ge(iota_s, 1)
                m, n = batch_rounds(G, dve)
                wide = dve.value_load(G.wide[0:1, 0:1], min_val=0, max_val=1)

                def rounds_of(o, b, work):
                    for j in range(ALWAYS):
                        work(j)
                    o.wait()
                    dve.sem_inc(seen_dve, 1)
                    for js in ASKED:
                        at, j = o.n, js[0]
                        with dve.If(m - b * RB > j):
                            for i in js:
                                work(i)
                            o.wait()
                            dve.sem_inc(seen_dve, 1)
                        with dve.If(m - b * RB < j + 1):
                            dve.wait_ge(o.sem, o.base + at)
                            dve.sem_inc(o.sem, o.n - at)

                def sort_batch(o, b):
                    def sort_round(keys):
                        def work(j):
                            for h in range(2):
                                top = sk[:, 16 * j + 8 * h:16 * j + 8 * h + 8]
                                o.then(dve.max(top, keys))
                                dve.sem_inc(seen_dve, 1)
                                o.then(dve.match_replace(keys, top, keys, -1.0))
                                dve.sem_inc(seen_dve, 1)
                        return work

                    o.then(dve.memset(sk[:, :], -1.0))
                    dve.sem_inc(seen_dve, 1)
                    for is_wide, keys in ((0, cand), (1, both)):
                        at = o.n
                        with dve.If(wide > 0) if is_wide else dve.If(wide < 1):
                            rounds_of(o, b, sort_round(keys))
                        with dve.If(wide < 1) if is_wide else dve.If(wide > 0):
                            dve.wait_ge(o.sem, o.base + at)
                            dve.sem_inc(o.sem, o.n - at)
                    o.wait()

                sort_batch(f0, 0)
                oa = Steps(dve, own_a)
                dve.memset(G.ln_eps[:, :], LN_EPS)
                dve.wait_ge(par_in, 80)
                for k in range(NT):
                    dve.wait_ge(s_mm, k + 1)
                    for i in range(CPT):
                        c = k * CPT + i
                        ins = dve.tensor_tensor_reduce(out=S[:, c, :], in0=G.bank[k][:, i * P:(i + 1) * P],
                                                       in1=other[:, :], scale=1.0, scalar=-3e38, op0=ALU.add,
                                                       op1=ALU.max, accum_out=rmax[:, c:c + 1])
                        ins.then_inc(s_max, 1)
                    dve.wait_ge(s_max, (k + 1) * CPT)
                    dve.tensor_scalar(nmax[:, k * CPT:(k + 1) * CPT], rmax[:, k * CPT:(k + 1) * CPT], -1.0, None,
                                      ALU.mult).then_inc(s_neg, 1)
                with dve.Fori(0, n) as b:
                    o = Steps(dve, own, b * PER)
                    o.then(dve.memset(rank[:, :], 0.0))
                    o.mark(dve.tensor_scalar(pad[:, :], sk[:, :], 0.0, None, ALU.is_lt))
                    o.then(dve.tensor_copy(k_i[:, :], sk[:, :]))
                    o.then(dve.tensor_scalar(full_i[:, :], k_i[:, :], 17, None, ALU.arith_shift_right))
                    dve.wait_ge(sum_mm, b)
                    o.mark(dve.tensor_copy(bin_f[:, :], full_i[:, :]))
                    o.then(dve.tensor_copy(bin_b[:, :], full_i[:, :]))
                    dve.sem_inc(seen_dve, 1)

                    def one_hots(j):
                        c = slice(16 * j, 16 * j + 16)
                        o.then(dve.tensor_tensor(hot[:, c, :], iota[:, :].unsqueeze(1).to_broadcast([P, 16, P]),
                                                 bin_b[:, c].unsqueeze(2).to_broadcast([P, 16, P]), ALU.is_equal))
                        dve.sem_inc(hot_s, 1)

                    for j in range(ALWAYS):
                        one_hots(j)
                    dve.sem_inc(seen_dve, 1)
                    for js in ASKED:
                        here = o.n
                        with dve.If(m - b * RB > js[0]):
                            for j in js:
                                one_hots(j)
                            dve.sem_inc(seen_dve, 1)
                        with dve.If(m - b * RB < js[0] + 1):
                            dve.wait_ge(own, o.base + here)
                            dve.sem_inc(own, len(js))
                            dve.sem_inc(hot_s, len(js))
                    o.wait()
                    o.mark(dve.tensor_copy(pad_i[:, :], pad[:, :]))
                    o.mark(dve.tensor_scalar(bin_i[:, :], full_i[:, :], P - 1, BIN_BITS, ALU.bitwise_and,
                                             ALU.logical_shift_left))
                    o.mark(dve.tensor_scalar(loc_i[:, :], k_i[:, :], 12, NC - 1, ALU.arith_shift_right,
                                             ALU.bitwise_and))
                    o.mark(dve.tensor_tensor(cont[:, 1:SORTED], bin_f[:, 1:SORTED], bin_f[:, 0:SORTED - 1],
                                             ALU.is_equal))
                    o.then(dve.tensor_scalar(k_i[:, :], k_i[:, :], NTOK - 1, None, ALU.bitwise_and))
                    o.mark(dve.tensor_scalar(loc_i[:, :], loc_i[:, :], 13, None, ALU.logical_shift_left))
                    o.mark(dve.tensor_scalar(pad_i[:, :], pad_i[:, :], BIN_BITS + 8, None, ALU.logical_shift_left))
                    o.then(dve.tensor_tensor_scan(pos[:, :], cont[:, :], cont[:, :], 0.0, ALU.mult, ALU.add))
                    o.mark(dve.tensor_tensor(k_i[:, :], k_i[:, :], loc_i[:, :], ALU.bitwise_or))
                    o.then(dve.tensor_tensor(bin_i[:, :], bin_i[:, :], pad_i[:, :], ALU.bitwise_or))
                    dve.wait_ge(free, b)
                    o.then(dve.tensor_copy(G.slot_key[:, :], k_i[:, :]))
                    dve.wait_ge(rank_mm, b + 1)
                    dve.sem_inc(seen_dve, 1)

                    def look_up(j):
                        o.wait()
                        for t in range(16):
                            c = 16 * j + t
                            o.mark(dve.tensor_tensor_reduce(out=prod[:, t, :], in0=G.bank[6][:, 0:P],
                                                            in1=hot[:, c, :], scale=1.0, scalar=0.0, op0=ALU.mult,
                                                            op1=ALU.add, accum_out=rank[:, c:c + 1]))

                    rounds_of(o, b, look_up)
                    o.wait()
                    dve.sem_inc(read_s, 1)
                    o.then(dve.tensor_tensor(rank[:, :], rank[:, :], pos[:, :], ALU.add))
                    o.then(dve.tensor_copy(rank_i[:, :], rank[:, :]))
                    o.then(dve.tensor_tensor(G.slot_idx[:, :], rank_i[:, :], bin_i[:, :], ALU.bitwise_or))
                    dve.sem_inc(idx_s, 1)
                    at = o.n
                    with dve.If(n - b > 1):
                        sort_batch(o, b + 1)
                        dve.sem_inc(seen_dve, 1)
                    with dve.If(n - b < 2):
                        dve.wait_ge(own, o.base + at)
                        dve.sem_inc(own, o.n - at)
                    o.close(PER)
                f = Steps(dve, cnt_s, 0)
                dve.wait_ge(sum_mm, n)
                dve.tensor_tensor_reduce(out=prod[:, 0, :], in0=G.bank[7][:, 0:P], in1=G.ident[:, :], scale=1.0,
                                         scalar=0.0, op0=ALU.mult, op1=ALU.add, accum_out=G.n_bin[:, 0:1]
                                         ).then_inc(tri_s, 1)
                dve.wait_ge(tri_s, 3)
                f.then(dve.tensor_copy(tmax[:, :], G.n_bin[:, :]))
                dve.wait_ge(cmax_s, 1)
                f.then(dve.tensor_scalar(tmax[:, :], tmx[:, :], float(PART), 1.0, ALU.min, ALU.max))
                f.then(dve.tensor_scalar(tmax[:, :], tmax[:, :], 15.0, None, ALU.add))
                f.then(dve.tensor_copy(p_i[:, :], tmax[:, :]))
                f.then(dve.tensor_scalar(G.groups[:, :], p_i[:, :], 4, None, ALU.logical_shift_right))
                f.then(dve.tensor_scalar(tmx[:, :], tmx[:, :], 1.0, None, ALU.max))
                f.then(dve.tensor_scalar(tmx[:, :], tmx[:, :], 1.0 / PART, 0.5 - 0.5 / PART, ALU.mult, ALU.add))
                f.then(dve.tensor_copy(p_i[:, :], tmx[:, :]))
                f.then(dve.tensor_copy(G.passes[:, :], p_i[:, :]))
                dve.wait_ge(s_exp, NC)
                oa.then(dve.reciprocal(rinv[:, :], rsum[:, :]))
                for k in range(4):
                    c = slice(8 * k, 8 * k + 8)
                    dve.wait_ge(o_mm, k + 1)
                    oa.then(dve.tensor_tensor(R[:, c, :], G.bank[k][:, :].rearrange("p (c d) -> p c d", d=D),
                                             rinv[:, c].unsqueeze(2).to_broadcast([P, 8, D]), ALU.mult))
                    oa.then(dve.tensor_tensor(R[:, c, :], R[:, c, :], HV[:, c, 0:D], ALU.add))
                ln.vector(dve)
                tf.vector(dve, G)


def experts0(nc, G, A):
    with stage(nc, G) as st:
        W1 = st.sb("e0_w1", [D, NPAIR, P])
        W2 = st.sb("e0_w2", [P, NPAIR, P])
        Wo = st.sb("e0_wo", [P, NPAIR, D])
        bo = st.sb("e0_bo", [EXP0, D])
        Wr = st.sb("e0_wr", [D, EXP0])
        br = st.sb("e0_br", [1, EXP0])
        ones = st.sb("e0_ones", [1, P])
        pick = st.sb("e0_pick", [EXP0, NPAIR, P])
        par = {n: st.sb("e0_" + n, [P, NPAIR]) for n in
               ("b1", "g1", "be1", "m1", "v1", "b2", "g2", "be2", "m2", "v2", "A1", "B1", "A2", "B2", "t1", "t2")}
        feat = st.sb("e0_feat", [D, 2, T])
        glog = st.sb("e0_gate_logits", [P, EXP0])
        gate = st.sb("e0_gate", [P, EXP0])
        gm = st.sb("e0_gate_max", [P, 1])
        gs = st.sb("e0_gate_sum", [P, 1])
        gi = st.sb("e0_gate_inv", [P, 1])
        gT = st.sb("e0_gate_t", [EXP0, P])
        wrep = st.sb("e0_gate_rows", [P, NPAIR, T])
        bn_eps = st.sb("e0_bn_eps", [P, 1])
        H1 = st.sb("e0_h1", [P, 2, TILE])
        H2 = st.sb("e0_h2", [P, 2, TILE])
        H2w = st.sb("e0_h2w", [P, 2, NPAIR, TILE])
        R = st.sb("e0_sum", [P, NC, D])
        sq = st.sb("e0_sq", [P, NC, D])
        w_in, zero_s, bn_in = st.sem("e0_weights_in"), st.sem("e0_zeroed"), st.sem("e0_bn_in")
        w2_in = st.sem("e0_w2_in")
        own, var_s, std_s, ab_s = st.sem("e0_dve_steps"), st.sem("e0_bn_var"), st.sem("e0_bn_std"), st.sem("e0_bn_fold")
        feat_s, log_mm, neg_s, exp_s = st.sem("e0_feat_s"), st.sem("e0_log_mm"), st.sem("e0_neg"), st.sem("e0_exp")
        gate_s, gT_mm, gT_s, rep_mm, rep_s = (st.sem("e0_gate_s"), st.sem("e0_gt_mm"), st.sem("e0_gt_s"),
                                              st.sem("e0_rep_mm"), st.sem("e0_rep_s"))
        l1_mm, l1_s, l2_mm, l2_s, gw_s, o_mm, o_s = (st.sem("e0_l1_mm"), st.sem("e0_l1_relu"), st.sem("e0_l2_mm"),
                                                     st.sem("e0_l2_relu"), st.sem("e0_gated"), st.sem("e0_out_mm"),
                                                     st.sem("e0_out_kept"))
        ln = LayerNorm(st, "ln1", R, G.tm, sq)
        tf = ToFeatures(st, "ln1_turn", G.tm, G.hT, ln.normed, True)
        G.middle_written = st.sem("slots_written_1")
        with nc.Block() as block:
            @block.gpsimd
            def _(pool):
                pool.memset(W2[:, :, :], 0.0).then_inc(zero_s, 1)
                scatter_last_batch(G, A, pool, G.middle_written, range(EARLY, MIDDLE))

            @block.sync
            def _(sp):
                sp.dma_start(W1[:, :, :].rearrange("d q (e h) -> d (q e) h", e=2),
                             A["L0_ffn_W1"].rearrange("e d h -> d e h")).then_inc(w_in, 16)
                sp.dma_start(Wo[:, :, :], A["L0_ffn_Wo"].rearrange("(q e) h d -> (e h) q d", e=2)).then_inc(w_in, 16)
                sp.dma_start(bo[:, :], A["L0_ffn_bo"]).then_inc(w_in, 16)
                sp.dma_start(Wr[:, :], A["L0_ffn_Wr"]).then_inc(w_in, 16)
                sp.dma_start(br[:, :], A["L0_ffn_br"].rearrange("(o e) -> o e", o=1)).then_inc(w_in, 16)
                sp.dma_start(pick[:, :, :], A["c_pick"]).then_inc(w_in, 16)
                sp.wait_ge(zero_s, 1)
                w2v = A["L0_ffn_W2"].rearrange("(q e) h k -> e h q k", e=2)
                for e in range(2):
                    sp.dma_start(W2[e * D:(e + 1) * D, :, e * D:(e + 1) * D], w2v[e]).then_inc(w2_in, 16)
                for n in ("b1", "g1", "be1", "m1", "v1", "b2", "g2", "be2", "m2", "v2"):
                    sp.dma_start(par[n][:, :], A["bn_" + n]).then_inc(bn_in, 16)

            @block.tensor
            def _(pe):
                pe.wait_ge(w_in, 96)
                pe.wait_ge(feat_s, 2)
                pe.matmul(G.bank[7][:, 0:EXP0], feat[:, :, :].rearrange("d r f -> d (r f)"), Wr[:, :], start=True,
                          stop=False)
                pe.matmul(G.bank[7][:, 0:EXP0], ones[:, :], br[:, :], start=False, stop=True).then_inc(log_mm, 1)
                pe.wait_ge(gate_s, 1)
                pe.transpose(G.bank[6][0:EXP0, 0:P], gate[:, :], G.ident[:, :]).then_inc(gT_mm, 1)
                pe.wait_ge(gT_s, 1)
                for q in range(NPAIR):
                    ins = pe.matmul(G.bank[7][:, 64 + q * T:64 + (q + 1) * T], pick[:, q, :], gT[:, 0:T], start=True,
                                    stop=True)
                ins.then_inc(rep_mm, 1)
                pe.wait_ge(w2_in, 32)

                def layer1(n):
                    k, q = n // NPAIR, n % NPAIR
                    if n >= 2:
                        pe.wait_ge(l1_s, n - 1)
                    pe.matmul(G.bank[n % 2][:, :], W1[:, q, :], G.hT[:, k * TILE:(k + 1) * TILE], start=True,
                              stop=True).then_inc(l1_mm, 1)

                def layer2(n):
                    pe.wait_ge(l1_s, n + 1)
                    if n >= 2:
                        pe.wait_ge(l2_s, n - 1)
                    pe.matmul(G.bank[2 + n % 2][:, :], W2[:, n % NPAIR, :], H1[:, n % 2, :], start=True,
                              stop=True).then_inc(l2_mm, 1)

                def out(k):
                    pe.wait_ge(gw_s, NPAIR * (k + 1))
                    if k >= 2:
                        pe.wait_ge(o_s, k - 1)
                    for i in range(CPT):
                        to = G.bank[4 + k % 2][:, i * D:(i + 1) * D]
                        for q in range(NPAIR):
                            pe.matmul(to, H2w[:, k % 2, q, i * P:(i + 1) * P], Wo[:, q, :], start=(q == 0), stop=False)
                        ins = pe.matmul(to, gT[:, :], bo[:, :], start=False, stop=True)
                    ins.then_inc(o_mm, 1)

                N = NT * NPAIR
                for n in range(N + 1):
                    if n < N:
                        layer1(n)
                    if n >= 1:
                        layer2(n - 1)
                    if n >= 3 and (n - 3) % NPAIR == 0 and n > 3:
                        out((n - 3) // NPAIR - 1)
                out(NT - 1)
                tf.tensor(pe, G)

            @block.scalar
            def _(act):
                for i in (1, 2):
                    act.wait_ge(bn_in, 160)
                    act.wait_ge(var_s, 1)
                    act.activation(par[f"t{i}"][:, :], par[f"v{i}"][:, :], ACT.Sqrt,
                                   bias=bn_eps[:, 0:1]).then_inc(std_s, 1)
                act.wait_ge(neg_s, 1)
                act.activation(gate[:, :], glog[:, :], ACT.Exp, bias=gm[:, 0:1], accum_out=gs[:, 0:1]
                               ).then_inc(exp_s, 1)
                act.wait_ge(ab_s, 2)
                N = NT * NPAIR
                for n in range(N + 1):
                    if n < N:
                        act.wait_ge(l1_mm, n + 1)
                        if n >= 2:
                            act.wait_ge(l2_mm, n - 1)
                        act.activation(H1[:, n % 2, :], G.bank[n % 2][:, :], ACT.Relu, bias=par["B1"][:, n % 4:n % 4 + 1],
                                       scale=par["A1"][:, n % 4:n % 4 + 1]).then_inc(l1_s, 1)
                    if n >= 1:
                        m = n - 1
                        act.wait_ge(l2_mm, m + 1)
                        if m >= 2:
                            act.wait_ge(gw_s, m - 1)
                        act.activation(H2[:, m % 2, :], G.bank[2 + m % 2][:, :], ACT.Relu,
                                       bias=par["B2"][:, m % 4:m % 4 + 1],
                                       scale=par["A2"][:, m % 4:m % 4 + 1]).then_inc(l2_s, 1)
                ln.scalar(act, G.ln_eps[:, 0:1])
                tf.scalar(act, G)

            def residual(dve, k):
                dve.wait_ge(o_mm, k + 1)
                c = slice(k * CPT, (k + 1) * CPT)
                dve.tensor_tensor(R[:, c, :], G.bank[4 + k % 2][:, 0:CPT * D].rearrange("p (c d) -> p c d", d=D),
                                  G.tm[:, c, :], ALU.add).then_inc(o_s, 1)

            @block.vector
            def _(dve):
                o = Steps(dve, own)
                dve.memset(bn_eps[:, :], BN_EPS).then_inc(var_s, 1)
                dve.memset(ones[:, :], 1.0).then_inc(feat_s, 1)
                o.then(dve.tensor_reduce(feat[:, 0, :], G.hT[:, :].rearrange("d (b f) -> d f b", f=T), AX_X, ALU.add))
                o.then(dve.tensor_scalar(feat[:, 0, :], feat[:, 0, :], 1.0 / B, None, ALU.mult))
                dve.tensor_copy(feat[:, 1, :], feat[:, 0, :]).then_inc(feat_s, 1)
                dve.wait_ge(std_s, 2)
                for i in "12":
                    A_, B_, t_ = par["A" + i], par["B" + i], par["t" + i]
                    o.then(dve.reciprocal(A_[:, :], t_[:, :]))
                    o.then(dve.tensor_tensor(A_[:, :], A_[:, :], par["g" + i][:, :], ALU.mult))
                    o.then(dve.tensor_tensor(B_[:, :], par["b" + i][:, :], par["m" + i][:, :], ALU.subtract))
                    o.then(dve.tensor_tensor(B_[:, :], B_[:, :], A_[:, :], ALU.mult))
                    dve.tensor_tensor(B_[:, :], B_[:, :], par["be" + i][:, :], ALU.add).then_inc(ab_s, 1)
                dve.wait_ge(log_mm, 1)
                o.then(dve.tensor_copy(glog[:, :], G.bank[7][:, 0:EXP0]))
                dve.tensor_reduce(gm[:, :], glog[:, :], AX_X, ALU.max, negate=True).then_inc(neg_s, 1)
                dve.wait_ge(exp_s, 1)
                o.then(dve.reciprocal(gi[:, :], gs[:, :]))
                dve.tensor_scalar(gate[:, :], gate[:, :], gi[:, 0:1], None, ALU.mult).then_inc(gate_s, 1)
                dve.wait_ge(gT_mm, 1)
                dve.tensor_copy(gT[:, :], G.bank[6][0:EXP0, 0:P]).then_inc(gT_s, 1)
                dve.wait_ge(rep_mm, 1)
                o.then(dve.tensor_copy(wrep[:, :, :], G.bank[7][:, 64:64 + NPAIR * T]))
                for n in range(NT * NPAIR):
                    k, q = n // NPAIR, n % NPAIR
                    dve.wait_ge(l2_s, n + 1)
                    if q == 0 and k >= 2:
                        dve.wait_ge(o_mm, k - 1)
                    dve.tensor_tensor(H2w[:, k % 2, q, :].rearrange("p (b f) -> p b f", f=T),
                                      H2[:, n % 2, :].rearrange("p (b f) -> p b f", f=T),
                                      wrep[:, q:q + 1, :].to_broadcast([P, TILE // T, T]), ALU.mult).then_inc(gw_s, 1)
                    if q == NPAIR - 1 and k >= 1:
                        residual(dve, k - 1)
                residual(dve, NT - 1)
                dve.wait_ge(o_s, NT)
                ln.vector(dve)
                tf.vector(dve, G)


def load_list(G, A, eng, k, list_in):
    eng.dma_start(G.raw[:, :], A["slots"].rearrange("(p s) o -> p (s o)", p=P)[:, bass.ds(k * PART, PART)]
                  ).then_inc(list_in, 16)


def sort_list(G, dve, o, rounds, seen=None):
    for j in rounds:
        top = G.sorted[:, 8 * j:8 * j + 8]
        o.then(dve.max(top, G.raw[:, :]))
        if seen is not None:
            dve.sem_inc(seen, 1)
        o.then(dve.match_replace(G.raw[:, :], top, G.raw[:, :], -1.0))
        if seen is not None:
            dve.sem_inc(seen, 1)


def read_list(G, dve, o):
    o.then(dve.tensor_copy(G.key_i[:, :], G.sorted[:, :]))
    o.mark(dve.tensor_scalar(G.place_i[:, :], G.key_i[:, :], 13, None, ALU.arith_shift_right))
    o.then(dve.tensor_scalar(G.src_i[:, :], G.key_i[:, :], NTOK - 1, None, ALU.bitwise_and))


def attention1(nc, G, A):
    with stage(nc, G) as st:
        DxT = st.sb("dx_t", [D, NSTATE])
        DyT = st.sb("dy_t", [D, NSTATE])
        Ew = st.sb("e_w", [P, NH2, D])
        decay = st.sb("decay", [P, P])
        pick = st.sb("pick_chunk", [P, 2 * NC - 1])
        X = st.sb("state_x", [P, NH2, NTOK])
        CH = [NC, P]
        u = st.sb("step_sums", CH)
        first = st.sb("step_is_first", CH)
        peak = st.sb("step_peak", CH)
        small = st.sb("step_small", CH)
        gain = st.sb("step_gain", CH)
        grown = st.sb("step_grown", CH)
        total = st.sb("step_total", CH)
        rates = st.sb("step_rates", [NC, 2, P])
        SM = st.sb("masked_scores", [P, NC, P])
        lnv = st.sb("lnv", [P, NC, D])
        xa = st.sb("xa", [P, NC, D])
        xb = st.sb("xb", [P, NC, D])
        par_in = st.sem("attn1_params_in")
        ones_s = st.sem("attn1_ones")
        u_mm, u_s, sum_mm = st.sem("u_mm"), st.sem("u_relu"), st.sem("sum_mm")
        own, x_s = st.sem("attn1_dve_steps"), st.sem("state_x_ready")
        Wg = st.sb("gat_w", [D, ROW])
        att = st.sb("gat_att", [D, 2, HEADS * EXP1])
        wa = st.sb("gat_w_att", [D, 2, HEADS * EXP1])
        w_in, wg_s, tab_mm, tab_s = (st.sem("gat_weights_in"), st.sem("gat_w_ready"), st.sem("table_mm"),
                                     st.sem("table_kept"))
        G.table_out = st.sem("table_out")
        gt_s = st.sem("gathered_zeroed")
        scat, all_out = st.sem("slots_written_2"), st.sem("all_slots_written")
        list_in, rate_s, spread_mm = (st.sem("first_list_in"), st.sem("rates_ready"),
                                               st.sem("rates_spread"))
        st_mm, sm_s, a_mm, a_s = st.sem("st_mm"), st.sem("sm_masked"), st.sem("a_mm"), st.sem("a_kept")
        y_mm, y_s, v_mm, v_s = st.sem("y_mm"), st.sem("y_s"), st.sem("v_mm"), st.sem("v_kept")
        lnv_n = LayerNorm(st, "lnv_n", G.tm, lnv, xb, xc=xa)
        lna = LayerNorm(st, "lna_n", xa, xb, lnv)
        lnw = LayerNorm(st, "lnw_n", xa, xb, lnv)
        lnh = LayerNorm(st, "lnh_n", xa, G.tm, lnv)
        ta = ToFeatures(st, "a_turn", xb, G.hT, lna.normed, True)
        th = ToFeatures(st, "ln3_turn", G.tm, G.hT, lnh.normed, True)
        with nc.Block() as block:
            @block.gpsimd
            def _(pool):
                scatter_last_batch(G, A, pool, scat, range(MIDDLE, RB))
                wait_for_scatter(G, pool, G.middle_written, range(EARLY, MIDDLE))
                wait_for_scatter(G, pool, scat, range(MIDDLE, RB))
                pool.sem_inc(all_out, 1)
                pool.memset(G.gathered[:, :, :], 0.0).then_inc(gt_s, 1)
                pool.wait_ge(gt_s, 1)

            @block.sync
            def _(sp):
                sp.dma_start(DxT[:, :], A["L1_attn_DxT"]).then_inc(par_in, 16)
                sp.dma_start(DyT[:, :], A["L1_attn_DyT"]).then_inc(par_in, 16)
                sp.dma_start(Ew[:, :, :], A["L1_attn_ET"].rearrange("(g p) d -> p g d", g=NH2)).then_inc(par_in, 16)
                sp.dma_start(decay[:, :], A["c_decay"]).then_inc(par_in, 16)
                sp.dma_start(Wg[:, 0:16], A["L1_ffn_W_gat"]).then_inc(w_in, 16)
                for i, n in enumerate((A["L1_ffn_att_src"], A["L1_ffn_att_dst"])):
                    sp.dma_start(att[:, i, :], n.rearrange("(o h) e -> o (h e)", o=1).to_broadcast([D, 16])
                                 ).then_inc(w_in, 16)
                sp.wait_ge(all_out, 1)
                load_list(G, A, sp, 0, list_in)
                sp.wait_ge(tab_s, 2)
                sp.dma_start(A["table"].rearrange("(c p) f -> p c f", p=P), G.tab[:, :, :]).then_inc(G.table_out, 16)
            @block.tensor
            def _(pe):
                pe.wait_ge(par_in, 64)
                pe.wait_ge(ones_s, 1)

                def sums(k):
                    pe.wait_ge(u_s, 2 * k + 2)
                    for c in range(k * CPT, (k + 1) * CPT):
                        for g in range(NH2):
                            ins = pe.matmul(G.bank[5][0:NC, 0:P], pick[:, NC - 1 - c:2 * NC - 1 - c],
                                            X[:, g, c * P:(c + 1) * P], start=(c == 0 and g == 0),
                                            stop=(c == NC - 1 and g == NH2 - 1))
                    return ins

                for k in range(NT):
                    for g in range(NH2):
                        n = 2 * k + g
                        if n >= 4:
                            pe.wait_ge(u_s, n - 3)
                        pe.matmul(G.bank[n % 4][:, :], DxT[:, g * P:(g + 1) * P], G.hT[:, k * TILE:(k + 1) * TILE],
                                  start=True, stop=True).then_inc(u_mm, 1)
                    if k:
                        sums(k - 1)
                sums(NT - 1).then_inc(sum_mm, 1)
                pe.wait_ge(rate_s, 1)

                def spread(k):
                    for i in range(CPT):
                        c = k * CPT + i
                        ins = pe.matmul(G.bank[2 * (k % 2) + i // 2][:, (i % 2) * 2 * P:(i % 2 + 1) * 2 * P],
                                        G.ident[0:NC, c:c + 1].to_broadcast([NC, P]),
                                        rates[:, :, :].rearrange("c r t -> c (r t)"), start=True, stop=True)
                    ins.then_inc(spread_mm, 1)

                spread(0)
                spread(1)
                for k in range(NT):
                    pe.wait_ge(x_s, k + 1)
                    if k >= 4:
                        pe.wait_ge(sm_s, k - 3)
                    for i in range(CPT):
                        c = slice((k * CPT + i) * P, (k * CPT + i + 1) * P)
                        for g in range(NH2):
                            ins = pe.matmul(G.bank[4 + k % 4][:, i * P:(i + 1) * P], X[:, g, c], X[:, g, c],
                                            start=(g == 0), stop=(g == NH2 - 1))
                    ins.then_inc(st_mm, 1)
                    if k + 2 < NT:
                        spread(k + 2)
                for k in range(4):
                    pe.wait_ge(sm_s, 2 * k + 2)
                    pe.wait_ge(lnv_n.normed, k + 1)
                    for i in range(8):
                        c = 8 * k + i
                        ins = pe.matmul(G.bank[k][:, i * D:(i + 1) * D], SM[:, c, :], lnv[:, c, :], start=True, stop=True)
                    ins.then_inc(a_mm, 1)
                ta.tensor(pe, G)
                for k in range(NT):
                    pe.wait_ge(ta.kept_dve if k % 2 else ta.kept_act, k // 2 + 1)
                    for g in range(NH2):
                        n = 2 * k + g
                        if n == 0:
                            ta.wait(pe)
                        if n >= 8:
                            pe.wait_ge(y_s, n - 7)
                        pe.matmul(G.bank[n % 8][:, :], DyT[:, g * P:(g + 1) * P], G.hT[:, k * TILE:(k + 1) * TILE],
                                  start=True, stop=True).then_inc(y_mm, 1)
                for k in range(4):
                    if k == 0:
                        pe.wait_ge(y_s, 16)
                    for i in range(8):
                        c = 8 * k + i
                        for g in range(NH2):
                            ins = pe.matmul(G.bank[k][:, i * D:(i + 1) * D], X[:, g, c * P:(c + 1) * P], Ew[:, g, :],
                                            start=(g == 0), stop=(g == NH2 - 1))
                    ins.then_inc(v_mm, 1)
                th.tensor(pe, G)
                pe.wait_ge(wg_s, 1)
                for h in range(2):
                    pe.wait_ge(th.kept_act, 2 * h + 2)
                    pe.wait_ge(th.kept_dve, 2 * h + 2)
                    for i in range(16):
                        c = 16 * h + i
                        ins = pe.matmul(G.bank[h][:, i * ROW:(i + 1) * ROW], G.hT[:, c * P:(c + 1) * P], Wg[:, :],
                                        start=True, stop=True)
                    ins.then_inc(tab_mm, 1)

            @block.scalar
            def _(act):
                for n in range(2 * NT):
                    if n == 4:
                        lnv_n.scalar(act, G.ln_eps[:, 0:1])
                    act.wait_ge(u_mm, n + 1)
                    act.activation(X[:, n % 2, (n // 2) * TILE:(n // 2 + 1) * TILE], G.bank[n % 4][:, :],
                                   ACT.Relu).then_inc(u_s, 1)
                lna.scalar(act, G.ln_eps[:, 0:1])
                ta.scalar(act, G)
                lnw.scalar(act, G.ln_eps[:, 0:1])
                lnh.scalar(act, G.ln_eps[:, 0:1])
                th.scalar(act, G)

            @block.vector
            def _(dve):
                o = Steps(dve, own)
                o.then(dve.memset(pick[:, :], 0.0))
                dve.memset(pick[:, NC - 1:NC], 1.0).then_inc(ones_s, 1)
                lnv_n.centre(dve)
                lnv_n.normalise(dve)
                dve.wait_ge(w_in, 48)
                o.then(dve.tensor_tensor(wa[:, :, :], att[:, :, :], Wg[:, 0:16].unsqueeze(1).to_broadcast([D, 2, 16]),
                                         ALU.mult))
                dve.tensor_reduce(Wg[:, 16:24], wa[:, :, :].rearrange("d s (h e) -> d (s h) e", e=EXP1), AX_X,
                                  ALU.add).then_inc(wg_s, 1)
                dve.wait_ge(list_in, 16)
                sort_list(G, dve, o, range(0, EARLY_SORT))
                o.mark(dve.memset(first[:, :], 1.0))
                o.wait()
                o.then(dve.memset(first[:, ::T], 0.0))
                def by_image(x, a, b):
                    return x[:, :].rearrange("c (b t) -> c b t", t=T)[:, :, a:b]

                dve.wait_ge(sum_mm, 1)
                o.then(dve.tensor_copy(u[:, :], G.bank[5][0:NC, 0:P]))
                o.then(dve.tensor_tensor_scan(peak[:, :], first[:, :], u[:, :], 0.0, ALU.mult, ALU.max))
                o.then(dve.tensor_scalar(small[:, :], peak[:, :], L1_EPS, DECAY / L1_EPS - 1.0, ALU.is_lt, ALU.mult))
                o.mark(dve.tensor_copy(by_image(gain, 1, 5), by_image(small, 0, 4)))
                o.mark(dve.scalar_tensor_tensor(out=by_image(gain, 5, T), in0=by_image(peak, 0, T - 5), scalar=0.0,
                                                in1=by_image(small, 4, T - 1), op0=ALU.is_equal, op1=ALU.mult))
                o.mark(dve.memset(gain[:, ::T], -1.0))
                o.wait()
                o.then(dve.tensor_scalar(gain[:, :], gain[:, :], 1.0, None, ALU.add))
                o.then(dve.tensor_tensor_scan(grown[:, :], gain[:, :], u[:, :], 0.0, ALU.mult, ALU.add))
                o.then(dve.tensor_scalar(grown[:, :], grown[:, :], L1_EPS, DECAY / L1_EPS, ALU.min, ALU.mult))
                o.mark(dve.tensor_copy(by_image(total, 0, 1), by_image(u, 0, 1)))
                o.mark(dve.tensor_tensor(by_image(total, 1, T), by_image(grown, 0, T - 1), by_image(u, 1, T),
                                         ALU.add))
                o.wait()
                o.then(dve.tensor_scalar(total[:, :], total[:, :], L1_EPS, None, ALU.max))
                o.then(dve.reciprocal(rates[:, 0, :], total[:, :]))
                o.then(dve.scalar_tensor_tensor(out=rates[:, 1, :], in0=rates[:, 0, :], scalar=DECAY, in1=first[:, :],
                                                op0=ALU.mult, op1=ALU.mult))
                dve.sem_inc(rate_s, 1)

                def mask(k):
                    dve.wait_ge(st_mm, k + 1)
                    dve.tensor_tensor(SM[:, k * CPT:(k + 1) * CPT, :],
                                      G.bank[4 + k % 4][:, :].rearrange("p (c t) -> p c t", t=P),
                                      decay[:, :].unsqueeze(1).to_broadcast([P, CPT, P]), ALU.mult).then_inc(sm_s, 1)

                for k in range(NT):
                    dve.wait_ge(spread_mm, k + 1)
                    for h in range(2):
                        bank = G.bank[2 * (k % 2) + h]
                        r3 = bank[:, :].rearrange("p (c r t) -> p c r t", c=2, r=2)
                        x3 = [X[:, g, k * TILE + h * 2 * P:k * TILE + (h + 1) * 2 * P].rearrange("p (c t) -> p c t", t=P)
                              for g in range(NH2)]
                        for g in range(NH2):
                            o.mark(dve.tensor_tensor(x3[g], x3[g], r3[:, :, 0, :], ALU.mult))
                        o.wait()
                        for g in range(NH2):
                            for c in range(2):
                                o.mark(dve.tensor_tensor_scan(x3[g][:, c, :], r3[:, c, 1, :], x3[g][:, c, :], 0.0,
                                                              ALU.mult, ALU.add))
                    o.wait()
                    dve.sem_inc(x_s, 1)
                    if k:
                        mask(k - 1)
                mask(NT - 1)
                for k in range(4):
                    dve.wait_ge(a_mm, k + 1)
                    dve.tensor_copy(xa[:, 8 * k:8 * k + 8, :], G.bank[k][:, :].rearrange("p (c d) -> p c d", d=D)
                                    ).then_inc(a_s, 1)
                dve.wait_ge(a_s, 4)
                lna.vector(dve)
                ta.vector(dve, G)
                for n in range(2 * NT):
                    x = X[:, n % 2, (n // 2) * TILE:(n // 2 + 1) * TILE]
                    dve.wait_ge(y_mm, n + 1)
                    dve.scalar_tensor_tensor(out=x, in0=G.bank[n % 8][:, :], scalar=0.0, in1=x, op0=ALU.max,
                                             op1=ALU.mult).then_inc(y_s, 1)
                late = np.array_split(np.arange(EARLY_SORT, PART // 8), 3)
                for k in range(4):
                    if k:
                        sort_list(G, dve, o, [int(j) for j in late[k - 1]])
                    dve.wait_ge(v_mm, k + 1)
                    dve.tensor_copy(xa[:, 8 * k:8 * k + 8, :], G.bank[k][:, :].rearrange("p (c d) -> p c d", d=D)
                                    ).then_inc(v_s, 1)
                dve.wait_ge(v_s, 4)
                lnw.centre(dve)
                read_list(G, dve, o)
                lnw.normalise(dve)
                dve.wait_ge(lnw.normed, LG)
                o.then(dve.tensor_tensor(xa[:, :, :], xb[:, :, :], G.tm[:, :, :], ALU.add))
                lnh.vector(dve)
                th.vector(dve, G)
                for h in range(2):
                    dve.wait_ge(tab_mm, h + 1)
                    dve.tensor_copy(G.tab[:, 16 * h:16 * h + 16, :], G.bank[h][:, 0:16 * ROW].rearrange(
                        "p (c f) -> p c f", f=ROW)).then_inc(tab_s, 1)


def graph_fill(nc, G, A):
    with stage(nc, G) as st:
        slot = st.sb("fill_slot", [P, 8])
        full = st.sb("fill_full", [P, 8])
        f_i = st.sb("fill_full_i", [P, 8], I32)
        s_i = st.sb("fill_slot_i", [P, 8], I32)
        bin_i = st.sb("fill_bin", [P, 8], I32)
        idx = st.sb("fill_index", [P, 8], I32)
        minus = st.sb("fill_value", [P, 8])
        own, idx_s, out_s, iota_s = (st.sem("fill_dve_steps"), st.sem("fill_index_ready"), st.sem("fill_written"),
                                     st.sem("fill_iota"))
        done, seen = st.sem("fill_done"), st.sem("fill_index_seen")
        per = PART // 8
        with nc.Block() as block:
            @block.gpsimd
            def _(pool):
                pool.iota(s_i[:, :], [[1, 8]], base=0, channel_multiplier=0).then_inc(iota_s, 1)
                pool.iota(bin_i[:, :], [[0, 8]], base=0, channel_multiplier=1).then_inc(iota_s, 1)
                n = pool.value_load(G.passes[0:1, 0:1], min_val=1, max_val=NEDGE // PART)
                with pool.If(n > 1):
                    with pool.Fori(0, (n - 1) * per) as i:
                        pool.wait_ge(idx_s, i + 1)
                        pool.sem_inc(seen, 1)
                        for t in range(8):
                            pool.indirect_dma_start(A["slots"], bass.IndirectOffsetOnAxis(ap=idx[:, t:t + 1], axis=0),
                                                    minus[:, t:t + 1], None, bounds_check=NSLOT - 1,
                                                    oob_is_err=False).then_inc(out_s, 16)
                        pool.wait_ge(out_s, i * 128 + 128)
                        pool.sem_inc(done, 1)

            @block.vector
            def _(dve):
                dve.wait_ge(iota_s, 2)
                o = Steps(dve, own)
                o.mark(dve.memset(minus[:, :], -1.0))
                o.mark(dve.tensor_scalar(bin_i[:, :], bin_i[:, :], BIN_BITS, None, ALU.logical_shift_left))
                o.then(dve.tensor_copy(slot[:, :], s_i[:, :]))
                o.then(dve.tensor_scalar(slot[:, :], slot[:, :], float(PART), None, ALU.add))
                start, PER = o.n, 16
                n = dve.value_load(G.passes[0:1, 0:1], min_val=1, max_val=NEDGE // PART)
                with dve.If(n > 1):
                    with dve.Fori(0, (n - 1) * per) as i:
                        r = Steps(dve, own, i * PER + start)
                        r.then(dve.tensor_scalar(full[:, :], slot[:, :], G.n_bin[:, 0:1], None, ALU.is_lt))
                        r.mark(dve.tensor_copy(f_i[:, :], full[:, :]))
                        r.then(dve.tensor_copy(s_i[:, :], slot[:, :]))
                        r.mark(dve.tensor_scalar(f_i[:, :], f_i[:, :], BIN_BITS + 8, None, ALU.logical_shift_left))
                        r.then(dve.tensor_tensor(s_i[:, :], s_i[:, :], bin_i[:, :], ALU.bitwise_or))
                        r.then(dve.tensor_tensor(idx[:, :], s_i[:, :], f_i[:, :], ALU.bitwise_or))
                        dve.sem_inc(idx_s, 1)
                        r.then(dve.tensor_scalar(slot[:, :], slot[:, :], 8.0, None, ALU.add))
                        dve.wait_ge(done, i + 1)
                        r.close(PER)


def graph_and_experts(nc, G, A):
    with stage(nc, G) as st:
        sb, sem = st.sb, st.sem
        W1 = sb("e1_w1", [D, EXP1, HID1])
        b1 = sb("e1_b1", [HID1, EXP1])
        W2 = sb("e1_w2", [HID1, EXP1, D])
        b2 = sb("e1_b2", [1, 2, EXP1 * D])
        ones = sb("e1_ones", [1, P])
        e_in, far_in, ones_s = sem("e1_weights_in"), sem("far_row_in"), sem("e1_ones_ready")
        l1_mm, gelu_s, l2_mm, x_s = sem("e1_l1_mm"), sem("e1_gelu"), sem("e1_l2_mm"), sem("e1_out_kept")
        thr_i = sb("node_thresholds_i", [P, NC], I32)
        thr = sb("node_thresholds", [P, NC])
        row_i = sb("list_row_i", [P, NC], I32)
        rowf = sb("list_row", [P, NC])
        loc = sb("list_node", [P, PART])
        cont = sb("same_as_before", [P, PART])
        contb = sb("same_as_after", [P, PART])
        mc = sb("before_penalty", [P, PART])
        mb = sb("after_penalty", [P, PART])
        endf = sb("segment_end", [P, NC])
        have = sb("node_has_edges", [P, NC])
        no = sb("no_edges_penalty", [P, NC])
        end_i = sb("segment_end_i", [P, NC], I32)
        Gt = G.gathered
        AS = sb("edge_src", [P, HEADS, PART])
        AD = sb("edge_dst", [P, HEADS, PART])
        MF = sb("edge_max", [P, HEADS, PART])
        MB = sb("edge_max_back", [P, HEADS, PART])
        Wt = sb("edge_weight", [P, HEADS, PART])
        MSG = sb("edge_msg", [P, 16, PART])
        ge = MSG[:, :, :].rearrange("p f n -> p (f n)").bitcast(BF16).rearrange("p (c n) -> p c n", c=NC)
        R = sb("segment_rows", [P, PART, ROW])
        HH = R[:, :, :].rearrange("p n f -> p (n f)")[:, 0:2 * EXP1 * TILE].rearrange("p (u e t) -> p u e t", u=2,
                                                                                      e=EXP1)
        N = sb("node_rows", [P, NC, ROW])
        m_run = sb("node_max", [P, NC, HEADS])
        m_new = sb("node_max_new", [P, NC, HEADS])
        den = sb("node_den", [P, NC, HEADS])
        agg = sb("node_agg", [P, NC, 16])
        lr = [sb(f"node_lrelu{i}", [P, NC, HEADS]) for i in range(3)]
        zz = sb("node_z", [P, 3, NC, HEADS])
        t16 = sb("node_t16", [P, NC, 16])
        gp = {n: sb("gat_" + n, [P, 16]) for n in ("bias", "gamma", "beta")}
        before = sb("expert_before", [P, 16])
        s1, s2, s3 = sb("gate_s1", [P, NC]), sb("gate_s2", [P, NC]), sb("gate_s3", [P, NC])
        sc, ex, rk = sb("gate_scores", [P, NC, EXP1]), sb("gate_exp", [P, NC, EXP1]), sb("gate_rank", [P, NC, EXP1])
        p1, p2 = sb("gate_pairs", [P, NC, EXP1, EXP1]), sb("gate_pairs2", [P, NC, EXP1, EXP1])
        list_ready = sem("list_ready")
        par_in, iota_s, own0, own = sem("gat_params_in"), sem("list_iotas"), sem("graph_dve_setup"), sem("graph_dve_steps")
        list_free, list_in, sort_s = sem("list_free"), sem("list_in"), sem("list_sorting")
        gat, seen, seen_dve = sem("rows_gathered"), sem("pool_seen"), sem("dve_seen")
        dif_s, w_s, rows_s, rows_out, ends_in = (sem("exponents_ready"), sem("weights_ready"), sem("segment_rows_ready"),
                                                 sem("segment_rows_out"), sem("node_rows_in"))
        nd_s, ne_s = sem("rescale_exponents"), sem("rescales_ready")
        sq_a, sq_b, std_a, std_b, ex_a, ex_b = (sem("gate_centred"), sem("gate_squared"), sem("gate_var"),
                                                sem("gate_std"), sem("gate_logits"), sem("gate_exps"))
        PER, RPP = 512, PART // 8 * 2 + 8
        fold = PART // 16

        def per_node(x, n):
            return x.unsqueeze(3).to_broadcast([P, NC, HEADS, n])

        def passes(eng):
            return eng.value_load(G.passes[0:1, 0:1], min_val=1, max_val=NEDGE // PART)

        with nc.Block() as block:
            @block.sync
            def _(sp):
                sp.wait_ge(G.table_out, 16)
                sp.dma_start(G.far[:, :], A["table"][FAR:FAR + 1, :].to_broadcast([P, ROW])).then_inc(far_in, 16)
                sp.dma_start(W1[:, :, :], A["L1_ffn_W1"].rearrange("e d h -> d e h")).then_inc(e_in, 16)
                sp.dma_start(b1[:, :], A["L1_ffn_b1T"]).then_inc(e_in, 16)
                sp.dma_start(W2[:, :, :], A["L1_ffn_W2"].rearrange("e h d -> h e d")).then_inc(e_in, 16)
                for i in range(2):
                    sp.dma_start(b2[:, i, :], A["L1_ffn_b2"].rearrange("(o e) d -> o (e d)", o=1)).then_inc(e_in, 16)
                for n, a in (("bias", A["L1_ffn_b_gat"]), ("gamma", A["L1_ffn_ln_gamma"]), ("beta", A["L1_ffn_ln_beta"])):
                    sp.dma_start(gp[n][:, :], a.rearrange("(o f) -> o f", o=1).to_broadcast([P, 16])).then_inc(par_in, 16)
                sp.dma_start(before[:, :], A["c_before"]).then_inc(par_in, 16)
                n = passes(sp)
                with sp.Fori(0, n) as k:
                    with sp.If(k > 0):
                        sp.wait_ge(list_free, k)
                        load_list(G, A, sp, k, list_in)
                    sp.wait_ge(rows_s, k + 1)
                    sp.dma_start(A["ends"].rearrange("(p s) f -> p s f", p=P), R[:, :, :]).then_inc(rows_out, 16)

            @block.gpsimd
            def _(pool):
                pool.iota(thr_i[:, :], [[2 * NTOK, NC]], base=0, channel_multiplier=0).then_inc(iota_s, 1)
                pool.iota(row_i[:, :], [[0, NC]], base=0, channel_multiplier=PART).then_inc(iota_s, 1)
                n = passes(pool)
                m = pool.value_load(G.groups[0:1, 0:1], min_val=1, max_val=fold)
                pool.wait_ge(G.table_out, 16)
                pool.sem_inc(seen, 1)
                with pool.Fori(0, n) as k:
                    pool.wait_ge(list_ready, k + 1)
                    pool.sem_inc(seen, 1)
                    for g in range(fold):
                        with pool.If(m + k * fold > g):
                            for j in range(16 * g, 16 * g + 16):
                                pool.indirect_dma_start(Gt[:, j, :], None, A["table"],
                                                        bass.IndirectOffsetOnAxis(ap=G.src_i[:, j:j + 1], axis=0)
                                                        ).then_inc(gat, 16)
                    pool.wait_ge(rows_out, 16 * k + 16)
                    pool.sem_inc(seen, 1)
                    for c in range(NC):
                        pool.indirect_dma_start(N[:, c, :], None, A["ends"],
                                                bass.IndirectOffsetOnAxis(ap=end_i[:, c:c + 1], axis=0)
                                                ).then_inc(ends_in, 16)

            @block.tensor
            def _(pe):
                pe.wait_ge(e_in, 80)
                pe.wait_ge(ones_s, 1)

                def layer2(k):
                    pe.wait_ge(gelu_s, EXP1 * (k + 1))
                    for h in range(2):
                        n = 2 * k + h
                        if n >= 2:
                            pe.wait_ge(x_s, n - 1)
                        pe.matmul(G.bank[6 + h][:, :], ones[:, :], b2[:, :, :].rearrange("o i f -> o (i f)"),
                                  start=True, stop=True)
                        for i in range(2):
                            for e in range(EXP1):
                                ins = pe.matmul(G.bank[6 + h][:, (i * EXP1 + e) * D:(i * EXP1 + e + 1) * D],
                                                HH[:, k % 2, e, (2 * h + i) * P:(2 * h + i + 1) * P], W2[:, e, :],
                                                start=False, stop=True, skip_group_check=True)
                        ins.then_inc(l2_mm, 1)

                for k in range(NT):
                    for e in range(EXP1):
                        n = k * EXP1 + e
                        if n >= EXP1:
                            pe.wait_ge(gelu_s, n - EXP1 + 1)
                        pe.matmul(G.bank[2 + n % 4][:, :], W1[:, e, :], G.hT[:, k * TILE:(k + 1) * TILE], start=True,
                                  stop=True).then_inc(l1_mm, 1)
                    if k:
                        layer2(k - 1)
                layer2(NT - 1)

            def keep_experts(act, k):
                for n in (2 * k, 2 * k + 1):
                    act.wait_ge(l2_mm, n + 1)
                    act.copy(G.xo[:, 2 * n:2 * n + 2, :], G.bank[6 + n % 2][:, :]).then_inc(x_s, 1)

            @block.scalar
            def _(act):
                act.wait_ge(nd_s, 1)
                act.activation(zz[:, 0:2, :, :], zz[:, 0:2, :, :], ACT.Exp).then_inc(ne_s, 1)
                act.wait_ge(e_in, 80)
                for n in range(NT * EXP1):
                    k, e = n // EXP1, n % EXP1
                    act.wait_ge(l1_mm, n + 1)
                    if k >= 2 and e == 0:
                        act.wait_ge(l2_mm, 2 * (k - 1))
                    act.activation(HH[:, k % 2, e, :], G.bank[2 + n % 4][:, :], ACT.Gelu, bias=b1[:, e:e + 1]
                                   ).then_inc(gelu_s, 1)
                    if k and e == EXP1 - 1:
                        keep_experts(act, k - 1)
                keep_experts(act, NT - 1)
                n = passes(act)
                with act.Fori(0, n) as k:
                    act.wait_ge(dif_s, k + 1)
                    act.activation(Wt[:, :, :], Wt[:, :, :], ACT.Exp).then_inc(w_s, 1)
                    act.wait_ge(nd_s, k + 2)
                    act.activation(zz[:, 0:2, :, :], zz[:, 0:2, :, :], ACT.Exp).then_inc(ne_s, 1)
                act.wait_ge(sq_a, 1)
                act.activation(t16[:, :, :], agg[:, :, :], ACT.Square).then_inc(sq_b, 1)
                act.wait_ge(std_a, 1)
                act.activation(s3[:, :], s2[:, :], ACT.Sqrt, bias=G.ln_eps[:, 0:1], scale=1.0 / 16).then_inc(std_b, 1)
                act.wait_ge(ex_a, 1)
                act.activation(ex[:, :, :], sc[:, :, :], ACT.Exp).then_inc(ex_b, 1)

            @block.vector
            def _(dve):
                o = Steps(dve, own0)
                dve.sem_inc(list_ready, 1)
                dve.sem_inc(sort_s, RPP)
                dve.memset(ones[:, :], 1.0).then_inc(ones_s, 1)
                dve.wait_ge(iota_s, 2)
                o.mark(dve.tensor_copy(thr[:, :], thr_i[:, :]))
                o.mark(dve.tensor_copy(rowf[:, :], row_i[:, :]))
                o.mark(dve.memset(cont[:, 0:1], 0.0))
                o.mark(dve.memset(contb[:, PART - 1:PART], 0.0))
                o.mark(dve.memset(N[:, :, 16:20], 1.0))
                o.mark(dve.tensor_copy(N[:, :, 0:16], G.tab[:, :, 0:16]))
                o.mark(dve.tensor_copy(N[:, :, 20:24], G.tab[:, :, 16:20]))
                o.mark(dve.tensor_copy(den[:, :, :], G.n_far[:, :].unsqueeze(2).to_broadcast([P, NC, HEADS])))
                dve.wait_ge(far_in, 16)
                o.mark(dve.tensor_tensor(agg[:, :, :], G.n_far[:, :].unsqueeze(2).to_broadcast([P, NC, 16]),
                                         G.far[:, 0:16].unsqueeze(1).to_broadcast([P, NC, 16]), ALU.mult))
                o.then(dve.tensor_scalar(s1[:, :], G.n_far[:, :], 0.0, -BIG, ALU.is_equal, ALU.mult))
                o.then(dve.tensor_tensor(m_run[:, :, :], s1[:, :].unsqueeze(2).to_broadcast([P, NC, HEADS]),
                                         G.far[:, 16:20].unsqueeze(1).to_broadcast([P, NC, HEADS]), ALU.add))

                def merge(f, step):
                    f.then(dve.tensor_tensor(m_new[:, :, :], m_run[:, :, :], N[:, :, 20:24], ALU.max))
                    for i, m in enumerate((m_run[:, :, :], N[:, :, 20:24], m_new[:, :, :])):
                        f.mark(dve.tensor_tensor(lr[i][:, :, :], m, G.tab[:, :, 20:24], ALU.add))
                    f.wait()
                    for i in range(3):
                        f.mark(dve.scalar_tensor_tensor(out=lr[i][:, :, :], in0=lr[i][:, :, :], scalar=0.2,
                                                        in1=lr[i][:, :, :], op0=ALU.mult, op1=ALU.max))
                    f.wait()
                    for i in range(2):
                        f.mark(dve.tensor_tensor(zz[:, i, :, :], lr[i][:, :, :], lr[2][:, :, :], ALU.subtract))
                    f.wait()
                    dve.sem_inc(nd_s, 1)
                    f.then(dve.tensor_copy(m_run[:, :, :], m_new[:, :, :]))
                    dve.wait_ge(ne_s, step + 1)
                    f.mark(dve.tensor_tensor(den[:, :, :], den[:, :, :], zz[:, 0, :, :], ALU.mult))
                    f.mark(dve.tensor_tensor(lr[0][:, :, :], N[:, :, 16:20], zz[:, 1, :, :], ALU.mult))
                    f.mark(dve.tensor_tensor(agg[:, :, :].rearrange("p c (h e) -> p c h e", e=4),
                                             agg[:, :, :].rearrange("p c (h e) -> p c h e", e=4),
                                             per_node(zz[:, 0, :, :], 4), ALU.mult))
                    f.then(dve.tensor_tensor(t16[:, :, :].rearrange("p c (h e) -> p c h e", e=4),
                                             N[:, :, 0:16].rearrange("p c (h e) -> p c h e", e=4),
                                             per_node(zz[:, 1, :, :], 4), ALU.mult))
                    f.mark(dve.tensor_tensor(den[:, :, :], den[:, :, :], lr[0][:, :, :], ALU.add))
                    f.then(dve.tensor_tensor(agg[:, :, :], agg[:, :, :], t16[:, :, :], ALU.add))

                merge(o, 0)
                n = passes(dve)
                m = dve.value_load(G.groups[0:1, 0:1], min_val=1, max_val=fold)
                with dve.Fori(0, n) as k:
                    f = Steps(dve, own, k * PER)
                    with dve.If(k > 0):
                        r = Steps(dve, sort_s, k * RPP)
                        dve.wait_ge(list_in, 16 * k)
                        dve.sem_inc(seen_dve, 1)
                        sort_list(G, dve, r, range(PART // 8), seen_dve)
                        read_list(G, dve, r)
                        r.close(RPP)
                        dve.sem_inc(list_ready, 1)
                    f.then(dve.tensor_copy(loc[:, :], G.place_i[:, :]))
                    f.mark(dve.tensor_tensor(cont[:, 1:PART], loc[:, 1:PART], loc[:, 0:PART - 1], ALU.is_equal))
                    f.then(dve.tensor_tensor(contb[:, 0:PART - 1], loc[:, 0:PART - 1], loc[:, 1:PART], ALU.is_equal))
                    f.mark(dve.tensor_scalar(mc[:, :], cont[:, :], 1.0, BIG, ALU.subtract, ALU.mult))
                    f.mark(dve.tensor_scalar(mb[:, :], contb[:, :], 1.0, BIG, ALU.subtract, ALU.mult))
                    f.then(dve.tensor_tensor(ge[:, :, :], G.sorted[:, :].unsqueeze(1).to_broadcast([P, NC, PART]),
                                             thr[:, :].unsqueeze(2).to_broadcast([P, NC, PART]), ALU.is_ge))
                    f.then(dve.tensor_reduce(endf[:, :], ge[:, :, :], AX_X, ALU.add))
                    f.mark(dve.tensor_tensor(have[:, 0:NC - 1], endf[:, 0:NC - 1], endf[:, 1:NC], ALU.is_gt))
                    f.then(dve.tensor_scalar(have[:, NC - 1:NC], endf[:, NC - 1:NC], 0.0, None, ALU.is_gt))
                    f.mark(dve.tensor_scalar(no[:, :], have[:, :], 1.0, BIG, ALU.subtract, ALU.mult))
                    f.then(dve.tensor_scalar(endf[:, :], endf[:, :], 1.0, 1.0, ALU.max, ALU.subtract))
                    f.then(dve.tensor_tensor(endf[:, :], endf[:, :], rowf[:, :], ALU.add))
                    f.then(dve.tensor_copy(end_i[:, :], endf[:, :]))
                    f.then(dve.memset(AD[:, :, :], 0.0))
                    for c in range(NC):
                        own_score = (Wt, MB)[c % 2]
                        for h in range(HEADS):
                            f.mark(dve.tensor_scalar(own_score[:, h, :], loc[:, :], float(c),
                                                     G.tab[:, c, 20 + h:21 + h], ALU.is_equal, ALU.mult))
                        f.wait()
                        f.mark(dve.tensor_tensor(AD[:, :, :], AD[:, :, :], own_score[:, :, :], ALU.add))
                    f.wait()
                    dve.wait_ge(gat, m * 256 + k * (16 * PART))
                    src_score = Gt[:, :, 16:20].rearrange("p n h -> p h n")
                    for h in range(HEADS):
                        f.mark(dve.tensor_tensor_scan(MF[:, h, :], mc[:, :], src_score[:, h, :], -BIG, ALU.add, ALU.max))
                        f.mark(dve.tensor_tensor_scan(MB[:, h, ::-1], mb[:, ::-1], src_score[:, h, ::-1], -BIG, ALU.add,
                                                      ALU.max))
                    f.wait()
                    f.then(dve.tensor_tensor(MF[:, :, :], MF[:, :, :], MB[:, :, :], ALU.max))
                    dve.wait_ge(x_s, 2 * NT)
                    f.mark(dve.tensor_copy(R[:, :, 20:24].rearrange("p n h -> p h n"), MF[:, :, :]))
                    f.mark(dve.tensor_tensor(AS[:, :, :], src_score, AD[:, :, :], ALU.add))
                    f.then(dve.tensor_tensor(MB[:, :, :], MF[:, :, :], AD[:, :, :], ALU.add))
                    f.mark(dve.scalar_tensor_tensor(out=AS[:, :, :], in0=AS[:, :, :], scalar=0.2, in1=AS[:, :, :],
                                                    op0=ALU.mult, op1=ALU.max))
                    f.then(dve.scalar_tensor_tensor(out=MB[:, :, :], in0=MB[:, :, :], scalar=0.2, in1=MB[:, :, :],
                                                    op0=ALU.mult, op1=ALU.max))
                    f.then(dve.tensor_tensor(Wt[:, :, :], AS[:, :, :], MB[:, :, :], ALU.subtract))
                    dve.sem_inc(dif_s, 1)
                    dve.wait_ge(w_s, k + 1)
                    for h in range(HEADS):
                        f.mark(dve.tensor_tensor(MSG[:, 4 * h:4 * h + 4, :],
                                                 Gt[:, :, 4 * h:4 * h + 4].rearrange("p n f -> p f n"),
                                                 Wt[:, h:h + 1, :].to_broadcast([P, 4, PART]), ALU.mult))
                    f.wait()
                    for q in range(16):
                        f.mark(dve.tensor_tensor_scan(R[:, :, q], cont[:, :], MSG[:, q, :], 0.0, ALU.mult, ALU.add))
                    for h in range(HEADS):
                        f.mark(dve.tensor_tensor_scan(R[:, :, 16 + h], cont[:, :], Wt[:, h, :], 0.0, ALU.mult,
                                                      ALU.add))
                    f.wait()
                    dve.sem_inc(rows_s, 1)
                    dve.wait_ge(ends_in, k * (16 * NC) + 16 * NC)
                    f.then(dve.tensor_tensor(N[:, :, :], N[:, :, :], have[:, :].unsqueeze(2).to_broadcast([P, NC, ROW]),
                                             ALU.mult))
                    f.then(dve.tensor_tensor(N[:, :, 20:24], N[:, :, 20:24],
                                             no[:, :].unsqueeze(2).to_broadcast([P, NC, HEADS]), ALU.add))
                    merge(f, k + 1)
                    dve.sem_inc(list_free, 1)
                    f.close(PER)
                dve.wait_ge(par_in, 64)
                b16 = [P, NC, 16]
                o.then(dve.tensor_scalar(den[:, :, :], den[:, :, :], 1e-16, None, ALU.add))
                o.then(dve.reciprocal(den[:, :, :], den[:, :, :]))
                o.then(dve.tensor_tensor(agg[:, :, :].rearrange("p c (h e) -> p c h e", e=4),
                                         agg[:, :, :].rearrange("p c (h e) -> p c h e", e=4),
                                         per_node(den[:, :, :], 4), ALU.mult))
                o.then(dve.tensor_tensor(agg[:, :, :], agg[:, :, :], gp["bias"][:, :].unsqueeze(1).to_broadcast(b16),
                                         ALU.add))
                o.then(dve.tensor_reduce(s1[:, :], agg[:, :, :], AX_X, ALU.add))
                o.then(dve.scalar_tensor_tensor(out=agg[:, :, :], in0=s1[:, :].unsqueeze(2).to_broadcast(b16),
                                                scalar=-1.0 / 16, in1=agg[:, :, :], op0=ALU.mult, op1=ALU.add))
                dve.sem_inc(sq_a, 1)
                dve.wait_ge(sq_b, 1)
                o.then(dve.tensor_reduce(s2[:, :], t16[:, :, :], AX_X, ALU.add))
                dve.sem_inc(std_a, 1)
                dve.wait_ge(std_b, 1)
                o.then(dve.reciprocal(s1[:, :], s3[:, :]))
                o.then(dve.tensor_tensor(agg[:, :, :], agg[:, :, :], s1[:, :].unsqueeze(2).to_broadcast(b16), ALU.mult))
                o.then(dve.tensor_tensor(agg[:, :, :], agg[:, :, :], gp["gamma"][:, :].unsqueeze(1).to_broadcast(b16),
                                         ALU.mult))
                o.then(dve.tensor_tensor(agg[:, :, :], agg[:, :, :], gp["beta"][:, :].unsqueeze(1).to_broadcast(b16),
                                         ALU.add))
                o.then(dve.tensor_reduce(sc[:, :, :], agg[:, :, :].rearrange("p c (h e) -> p c e h", e=4), AX_X,
                                         ALU.add))
                o.then(dve.tensor_scalar(sc[:, :, :], sc[:, :, :], 1.0 / HEADS, None, ALU.mult))
                other = sc[:, :, :].unsqueeze(2).to_broadcast([P, NC, EXP1, EXP1])
                mine = sc[:, :, :].unsqueeze(3).to_broadcast([P, NC, EXP1, EXP1])
                o.mark(dve.tensor_tensor(p1[:, :, :, :], other, mine, ALU.is_gt))
                o.mark(dve.tensor_tensor(p2[:, :, :, :], other, mine, ALU.is_equal))
                o.then(dve.tensor_reduce(s1[:, :], sc[:, :, :], AX_X, ALU.max))
                o.mark(dve.tensor_tensor(p2[:, :, :, :].rearrange("p c e f -> p c (e f)"),
                                         p2[:, :, :, :].rearrange("p c e f -> p c (e f)"),
                                         before[:, :].unsqueeze(1).to_broadcast(b16), ALU.mult))
                o.then(dve.tensor_tensor(sc[:, :, :], sc[:, :, :], s1[:, :].unsqueeze(2).to_broadcast([P, NC, EXP1]),
                                         ALU.subtract))
                dve.sem_inc(ex_a, 1)
                o.then(dve.tensor_tensor(p1[:, :, :, :], p1[:, :, :, :], p2[:, :, :, :], ALU.add))
                o.then(dve.tensor_reduce(rk[:, :, :], p1[:, :, :, :], AX_X, ALU.add))
                dve.wait_ge(ex_b, 1)
                o.then(dve.scalar_tensor_tensor(out=ex[:, :, :], in0=rk[:, :, :], scalar=2.0, in1=ex[:, :, :],
                                                op0=ALU.is_lt, op1=ALU.mult))
                o.then(dve.tensor_reduce(s2[:, :], ex[:, :, :], AX_X, ALU.add))
                o.then(dve.reciprocal(s2[:, :], s2[:, :]))
                o.then(dve.tensor_tensor(G.gates[:, :, :], ex[:, :, :],
                                         s2[:, :].unsqueeze(2).to_broadcast([P, NC, EXP1]), ALU.mult))


def combine(nc, G, A):
    with stage(nc, G) as st:
        R = st.sb("mix", [P, NC, D])
        Y = st.sb("mix_tmp", [P, NC, D])
        own, own_p, out_s, mixed = (st.sem("mix_dve_steps"), st.sem("mix_pool_steps"), st.sem("out_written"),
                                    st.sem("mixed_by_pool"))
        ln = LayerNorm(st, "ln4", R, G.tm, Y)

        def mix(eng, o, g):
            c = slice(g * LC, (g + 1) * LC)
            for e in range(EXP1):
                gate = G.gates[:, c, e:e + 1].to_broadcast([P, LC, D])
                o.then(eng.tensor_tensor(Y[:, c, :], G.xo[:, c, e * D:(e + 1) * D], gate, ALU.mult))
                o.then(eng.tensor_tensor(R[:, c, :], Y[:, c, :], G.tm[:, c, :] if e == 0 else R[:, c, :], ALU.add))

        with nc.Block() as block:
            @block.gpsimd
            def _(pool):
                mix(pool, Steps(pool, own_p), LG - 1)
                pool.sem_inc(mixed, 1)

            @block.vector
            def _(dve):
                o = Steps(dve, own)
                for g in range(LG - 1):
                    mix(dve, o, g)
                    ln.centre(dve, (g,))
                dve.wait_ge(mixed, 1)
                ln.centre(dve, (LG - 1,))
                ln.normalise(dve)

            @block.scalar
            def _(act):
                ln.scalar(act, G.ln_eps[:, 0:1])

            @block.sync
            def _(sp):
                for g in range(LG):
                    sp.wait_ge(ln.normed, g + 1)
                    sp.dma_start(A["out"].rearrange("b t d -> (b t) d").rearrange("(c p) d -> p c d", p=P)[
                        :, g * LC:(g + 1) * LC, :], G.tm[:, g * LC:(g + 1) * LC, :]).then_inc(out_s, 16)
                sp.wait_ge(out_s, 16 * LG)


def program(nc, A):
    A["slots"] = nc.dram_tensor("bin_slots", [NSLOT, 1], F32).ap()
    A["table"] = nc.dram_tensor("node_table", [NTOK, ROW], F32).ap()
    A["ends"] = nc.dram_tensor("segment_table", [P * PART, ROW], F32).ap()
    G = Shared()
    with stage(nc, G) as st:
        G.bank = [st.enter_context(nc.psum_tensor(f"bank{i}", [P, TILE], F32)) for i in range(8)]
        G.hT = st.sb("h_features", [D, NTOK])
        G.ident = st.sb("ident", [P, P])
        G.ln_eps = st.sb("ln_eps", [P, 1])
        G.rounds = st.sb("sort_rounds", [P, 1], I32)
        G.wide = st.sb("keys_are_left", [P, 1], I32)
        G.batches = st.sb("sort_batches", [P, 1], I32)
        G.slot_key = st.sb("slot_key", [P, SORTED])
        G.slot_idx = st.sb("slot_index", [P, SORTED], I32)
        G.passes = st.sb("graph_passes", [P, 1], I32)
        G.groups = st.sb("first_groups", [P, 1], I32)
        G.n_bin = st.sb("n_bin", [P, 1])
        G.n_far = st.sb("n_far", [P, NC])
        G.keys = st.sb("edge_keys_then_tokens", [P, CAND + EW])
        G.tm = G.keys[:, 0:NC * D].rearrange("p (c d) -> p c d", d=D)
        tokens_and_counts(nc, G, A)
        G.raw = st.sb("list_raw", [P, PART])
        G.sorted = st.sb("list_sorted", [P, PART])
        G.key_i = st.sb("list_key_i", [P, PART], I32)
        G.place_i = st.sb("list_place_i", [P, PART], I32)
        G.src_i = st.sb("list_src_i", [P, PART], I32)
        attention0_and_sort(nc, G, A)
        fresh_semaphores(nc, G)
        experts0(nc, G, A)
        G.gathered = st.sb("gathered", [P, PART, ROW])
        G.tab = st.sb("node_rows_own", [P, NC, ROW])
        attention1(nc, G, A)
        graph_fill(nc, G, A)
        G.far = st.sb("far_row", [P, ROW])
        G.gates = st.sb("gates", [P, NC, EXP1])
        G.xo = st.sb("expert_out", [P, NC, EXP1 * D])
        graph_and_experts(nc, G, A)
        combine(nc, G, A)


_INS = ["x", "L0_tok_W", "L0_tok_b", "L0_attn_Q", "L0_attn_K", "L0_attn_VT", "L0_ffn_Wr", "L0_ffn_br", "L0_ffn_W1",
        "L0_ffn_W2", "L0_ffn_Wo", "L0_ffn_bo", "L1_attn_DxT", "L1_attn_DyT", "L1_attn_ET", "L1_ffn_W_gat",
        "L1_ffn_att_src", "L1_ffn_att_dst", "L1_ffn_b_gat", "L1_ffn_ln_gamma", "L1_ffn_ln_beta", "L1_ffn_W1",
        "L1_ffn_b1T", "L1_ffn_W2", "L1_ffn_b2", "L1_ffn_edge_index"]
_BN = ["b1", "g1", "be1", "m1", "v1", "b2", "g2", "be2", "m2", "v2"]


def layouts(inputs):
    a = {k: np.asarray(v) for k, v in inputs.items()}
    for name in ("L0_attn_V", "L1_attn_Dx", "L1_attn_Dy", "L1_attn_E", "L1_ffn_b1"):
        a[name + "T"] = np.ascontiguousarray(a[name].T)
    for n in _BN:
        a["bn_" + n] = np.ascontiguousarray(a["L0_ffn_" + n].reshape(NPAIR, 2 * 64).T)
    return a


def kernel(**inputs):
    import concourse.bacc as bacc
    from concourse.bass_utils import run_bass_kernel_spmd

    nc = bacc.Bacc("TRN2", target_bir_lowering=False, num_devices=1)
    consts = shape_constants()
    data = layouts(inputs)
    arrays, A = {}, {}

    def declare(name, a):
        arrays[f"in_{name}"] = np.ascontiguousarray(a)
        return nc.dram_tensor(f"in_{name}", a.shape, mybir.dt.from_np(a.dtype), kind="ExternalInput").ap()

    for name in _INS:
        A[name] = declare(name, data[name])
    for name in _BN:
        A["bn_" + name] = declare("bn_" + name, data["bn_" + name])
    for name in consts:
        A[name] = declare(name, consts[name])
    A["out"] = nc.dram_tensor("out_dram", (B, T, D), F32, kind="ExternalOutput").ap()
    program(nc, A)
    r = run_bass_kernel_spmd(nc, [arrays], core_ids=[0])
    return r.results[0]["out_dram"]
```
